# Optimizing a Trainium2 kernel written in Bass

```python
import numpy as np
import jax
import jax.numpy as jnp

def _softmax(x, axis=-1):
    return jax.nn.softmax(x, axis=axis)

def _gelu(x):
    return jax.nn.gelu(x, approximate=True)

def _silu(x):
    return jax.nn.silu(x)

def _sigmoid(x):
    return jax.nn.sigmoid(x)

def _layernorm(x, axis=-1, eps=1e-05):
    m = jnp.mean(x, axis=axis, keepdims=True)
    v = jnp.var(x, axis=axis, keepdims=True)
    return (x - m) / jnp.sqrt(v + eps)

def _scatter_add(tgt, idx, src, axis=0):
    return tgt.at[idx].add(src)

def _segment_sum(src, seg, n):
    return jax.ops.segment_sum(src, seg, n)
kernel_name = 'mk_gnn_ffn_d4_gnn_r32_feeedd'

def setup_inputs(seed: int=0):
    np.random.seed(seed)
    _w = jnp.asarray

    def _rec_inputs():
        import jax
        import jax.numpy as jnp
        _gk = jax.random.key(seed)
        x = -8.776e-05 + 1 * jax.random.normal(jax.random.fold_in(_gk, 1), (625, 256), jnp.float32)
        src = jax.random.randint(jax.random.fold_in(_gk, 2), (20000,), 0, 625, jnp.int32)
        dst = jax.random.randint(jax.random.fold_in(_gk, 3), (20000,), 0, 625, jnp.int32)
        _o = jnp.argsort(dst, stable=True)
        src = src[_o]
        dst = dst[_o]
        return (x, src, dst)
    x, src, dst = _rec_inputs()

    def _L0_gnn_setup():
        import jax, jax.numpy as jnp
        import numpy as np
        N, E, IN, OUT = (625, 10000, 256, 256)
        H1, H2 = (IN // 64, OUT // 64)
        EPS = 1e-05
        ALPHA = 0.2

        def _bn(x, g, b, m, v):
            return (x - m) * jax.lax.rsqrt(v + EPS) * g + b

        def _mlp(x, W1, b1, g1, be1, m1, v1, W2, b2, g2, be2, m2, v2):
            h = jax.nn.leaky_relu(_bn(x @ W1 + b1, g1, be1, m1, v1), 0.01)
            return jax.nn.relu(_bn(h @ W2 + b2, g2, be2, m2, v2))
        key = jax.random.key(seed)
        ks = iter(jax.random.split(key, 40))
        nrm = lambda shape, s=0.1: jax.random.normal(next(ks), shape, jnp.float32) * s
        pos = lambda shape: jax.random.uniform(next(ks), shape, jnp.float32) + 0.5
        inp = {'n_feature': jax.random.normal(next(ks), (N, IN), jnp.float32), 'src': jax.random.randint(next(ks), (E,), 0, N, jnp.int32), 'dst': jax.random.randint(next(ks), (E,), 0, N, jnp.int32), 'attn_l': nrm((OUT,)), 'attn_r': nrm((OUT,)), 'fe_W1': nrm((2 * IN, H1)), 'fe_b1': nrm((H1,)), 'fe_g1': pos((H1,)), 'fe_be1': nrm((H1,)), 'fe_m1': nrm((H1,)), 'fe_v1': pos((H1,)), 'fe_W2': nrm((H1, OUT)), 'fe_b2': nrm((OUT,)), 'fe_g2': pos((OUT,)), 'fe_be2': nrm((OUT,)), 'fe_m2': nrm((OUT,)), 'fe_v2': pos((OUT,)), 'fn_W1': nrm((IN + OUT, H2)), 'fn_b1': nrm((H2,)), 'fn_g1': pos((H2,)), 'fn_be1': nrm((H2,)), 'fn_m1': nrm((H2,)), 'fn_v1': pos((H2,)), 'fn_W2': nrm((H2, OUT)), 'fn_b2': nrm((OUT,)), 'fn_g2': pos((OUT,)), 'fn_be2': nrm((OUT,)), 'fn_m2': nrm((OUT,)), 'fn_v2': pos((OUT,))}
        return inp
    _L0_gnn_all = _L0_gnn_setup()
    _L0_gnn_in = {k: v for k, v in _L0_gnn_all.items() if k in ('attn_l', 'attn_r', 'fe_W1', 'fe_b1', 'fe_g1', 'fe_be1', 'fe_m1', 'fe_v1', 'fe_W2', 'fe_b2', 'fe_g2', 'fe_be2', 'fe_m2', 'fe_v2', 'fn_W1', 'fn_b1', 'fn_g1', 'fn_be1', 'fn_m1', 'fn_v1', 'fn_W2', 'fn_b2', 'fn_g2', 'fn_be2', 'fn_m2', 'fn_v2')}
    del _L0_gnn_all

    def _L0_ffn_setup():
        import jax, jax.numpy as jnp
        import numpy as np
        B, K, D = (512, 16, 256)
        E = 32
        H = int(D * 0.25)
        key = jax.random.key(seed)
        ks = jax.random.split(key, 7)
        d_rs = D ** (-0.5)
        h_rs = H ** (-0.5)
        x = jax.random.normal(ks[0], (B, K, D), dtype=jnp.float32)
        router_w = jax.random.uniform(ks[1], (E, D), jnp.float32, -d_rs, d_rs)
        router_b = jax.random.uniform(ks[2], (E,), jnp.float32, -d_rs, d_rs)
        W1 = jax.random.uniform(ks[3], (E, D, H), jnp.float32, -h_rs, h_rs)
        b1 = jax.random.uniform(ks[4], (E, H), jnp.float32, -h_rs, h_rs)
        W2 = jax.random.uniform(ks[5], (E, H, D), jnp.float32, -d_rs, d_rs)
        b2 = jax.random.uniform(ks[6], (E, D), jnp.float32, -d_rs, d_rs)
        return {'x': x, 'router_w': router_w, 'router_b': router_b, 'W1': W1, 'b1': b1, 'W2': W2, 'b2': b2}
    _L0_ffn_all = _L0_ffn_setup()
    _L0_ffn_in = {k: v for k, v in _L0_ffn_all.items() if k in ('router_w', 'router_b', 'W1', 'b1', 'W2', 'b2')}
    del _L0_ffn_all

    def _L1_gnn_setup():
        import jax, jax.numpy as jnp
        import numpy as np
        N_NODES, N_EDGES, D_IN, D_HID, N_LAYERS = (50000, 25000, 256, 256, 3)
        key = jax.random.key(seed)
        k_x, k_e, k_w = jax.random.split(key, 3)
        x = jax.random.normal(k_x, (N_NODES, D_IN), dtype=jnp.float32)
        edge_index = jax.random.randint(k_e, (2, N_EDGES), 0, N_NODES, dtype=jnp.int32)
        W = jax.random.normal(k_w, (N_LAYERS, D_IN, D_HID), dtype=jnp.float32) * (1.0 / np.sqrt(D_IN))
        b = jnp.zeros((N_LAYERS, D_HID), dtype=jnp.float32)
        return {'x': x, 'edge_index': edge_index, 'W': W, 'b': b}
    _L1_gnn_all = _L1_gnn_setup()
    _L1_gnn_in = {k: v for k, v in _L1_gnn_all.items() if k in ('W', 'b')}
    del _L1_gnn_all

    def _L1_ffn_setup():
        import jax, jax.numpy as jnp
        import numpy as np
        B, N, D = (16, 128, 256)
        NUM_EXPERTS, TOP_K, HEADS = (4, 2, 4)
        N_EDGES = 32768
        LN_EPS = 1e-05

        def _layernorm(x, g, b):
            mu = x.mean(-1, keepdims=True)
            var = ((x - mu) ** 2).mean(-1, keepdims=True)
            return (x - mu) * jax.lax.rsqrt(var + LN_EPS) * g + b

        def _forward(x, edge_index, W_gat, att_src, att_dst, b_gat, ln_gamma, ln_beta, W1, b1, W2, b2):
            Bc, Nc, Dc = x.shape
            M = Bc * Nc
            x_flat = x.reshape(M, Dc)
            h = (x_flat @ W_gat).reshape(M, HEADS, NUM_EXPERTS)
            loops = jnp.arange(M, dtype=edge_index.dtype)
            src = jnp.concatenate([edge_index[0], loops])
            dst = jnp.concatenate([edge_index[1], loops])
            a_src = (h * att_src).sum(-1)
            a_dst = (h * att_dst).sum(-1)
            e = jax.nn.leaky_relu(a_src[src] + a_dst[dst], negative_slope=0.2)
            e_max = jax.ops.segment_max(e, dst, num_segments=M)
            ee = jnp.exp(e - e_max[dst])
            denom = jax.ops.segment_sum(ee, dst, num_segments=M)
            alpha = ee / (denom[dst] + 1e-16)
            msg = h[src] * alpha[:, :, None]
            agg = jax.ops.segment_sum(msg, dst, num_segments=M).reshape(M, HEADS * NUM_EXPERTS) + b_gat
            scores = _layernorm(agg, ln_gamma, ln_beta).reshape(M, HEADS, NUM_EXPERTS).mean(1)
            scores = scores.reshape(Bc, Nc, NUM_EXPERTS)
            topk_s, topk_i = jax.lax.top_k(scores, TOP_K)
            w = jax.nn.softmax(topk_s, axis=-1)
            out = jnp.zeros_like(x)
            for ei in range(NUM_EXPERTS):
                g = jnp.where(topk_i == ei, w, 0.0).sum(-1)
                hh = jax.nn.gelu(x @ W1[ei] + b1[ei], approximate=False)
                out = out + g[..., None] * (hh @ W2[ei] + b2[ei])
            return out
        key = jax.random.key(seed)
        ks = jax.random.split(key, 8)
        s = 0.05
        return {'x': jax.random.normal(ks[0], (B, N, D), jnp.float32), 'W_gat': jax.random.normal(ks[1], (D, HEADS * NUM_EXPERTS), jnp.float32) * s, 'att_src': jax.random.normal(ks[2], (HEADS, NUM_EXPERTS), jnp.float32) * s, 'att_dst': jax.random.normal(ks[3], (HEADS, NUM_EXPERTS), jnp.float32) * s, 'b_gat': jnp.zeros((HEADS * NUM_EXPERTS,), jnp.float32), 'ln_gamma': jnp.ones((HEADS * NUM_EXPERTS,), jnp.float32), 'ln_beta': jnp.zeros((HEADS * NUM_EXPERTS,), jnp.float32), 'W1': jax.random.normal(ks[4], (NUM_EXPERTS, D, 2 * D), jnp.float32) * s, 'b1': jnp.zeros((NUM_EXPERTS, 2 * D), jnp.float32), 'W2': jax.random.normal(ks[5], (NUM_EXPERTS, 2 * D, D), jnp.float32) * s, 'b2': jnp.zeros((NUM_EXPERTS, D), jnp.float32), 'edge_index': jax.random.randint(ks[6], (2, N_EDGES), 0, B * N, jnp.int32)}
    _L1_ffn_all = _L1_ffn_setup()
    _L1_ffn_in = {k: v for k, v in _L1_ffn_all.items() if k in ('W_gat', 'att_src', 'att_dst', 'b_gat', 'ln_gamma', 'ln_beta', 'W1', 'b1', 'W2', 'b2', 'edge_index')}
    del _L1_ffn_all

    def _L2_gnn_setup():
        import jax, jax.numpy as jnp
        import numpy as np
        ALPHA = 0.2
        LN_EPS = 1e-05

        def _gat_layer(x, src, dst, W, b, a, g, beta, N, concat):
            h = x @ W.T + b
            d = W.shape[0]
            s_src = h @ a[:d]
            s_dst = h @ a[d:]
            score = s_src[src] + s_dst[dst]
            e = jnp.exp(-jax.nn.leaky_relu(score, ALPHA))
            h_prime = jax.ops.segment_sum(e[:, None] * h[dst], src, num_segments=N)
            mu = jnp.mean(h_prime, axis=-1, keepdims=True)
            var = jnp.var(h_prime, axis=-1, keepdims=True)
            h_prime = (h_prime - mu) * jax.lax.rsqrt(var + LN_EPS) * g + beta
            return jax.nn.elu(h_prime) if concat else h_prime
        key = jax.random.key(seed)
        ks = jax.random.split(key, 13)
        N, E, F, D, H = (50000, 25000, 256, 64, 8)
        S = 0.02
        inp = {'embeds': jax.random.normal(ks[0], (N, F), dtype=jnp.float32), 'W_heads': jax.random.normal(ks[1], (H, D, F), dtype=jnp.float32) * S, 'b_heads': jax.random.normal(ks[2], (H, D), dtype=jnp.float32) * S, 'a_heads': jax.random.normal(ks[3], (H, 2 * D), dtype=jnp.float32) * S, 'g_heads': jnp.ones((H, D), dtype=jnp.float32), 'beta_heads': jnp.zeros((H, D), dtype=jnp.float32), 'W_out': jax.random.normal(ks[4], (F, D * H), dtype=jnp.float32) * S, 'b_out': jax.random.normal(ks[5], (F,), dtype=jnp.float32) * S, 'a_out': jax.random.normal(ks[6], (2 * F,), dtype=jnp.float32) * S, 'g_out': jnp.ones((F,), dtype=jnp.float32), 'beta_out': jnp.zeros((F,), dtype=jnp.float32), 'edge_index': jax.random.randint(ks[7], (2, E), 0, N, dtype=jnp.int32)}
        return inp
    _L2_gnn_all = _L2_gnn_setup()
    _L2_gnn_in = {k: v for k, v in _L2_gnn_all.items() if k in ('W_heads', 'b_heads', 'a_heads', 'g_heads', 'beta_heads', 'W_out', 'b_out', 'a_out', 'g_out', 'beta_out')}
    del _L2_gnn_all

    def _L2_ffn_setup():
        import jax, jax.numpy as jnp
        import numpy as np
        D_MODEL = 256
        EXPERT_DIM = 512
        NUM_EXPERTS = 8
        TOP_K = 2
        SEQ_LEN = 64
        BATCH = 2
        key = jax.random.key(seed)
        ks = jax.random.split(key, 8)
        s = 0.02
        x = jax.random.normal(ks[0], (SEQ_LEN, BATCH, D_MODEL), dtype=jnp.float32)
        Wg = jax.random.normal(ks[1], (D_MODEL, NUM_EXPERTS), dtype=jnp.float32) * s
        bg = jax.random.normal(ks[2], (NUM_EXPERTS,), dtype=jnp.float32) * s
        bias = jnp.zeros((NUM_EXPERTS,), dtype=jnp.float32)
        W1 = jax.random.normal(ks[3], (NUM_EXPERTS, D_MODEL, EXPERT_DIM), dtype=jnp.float32) * s
        b1 = jax.random.normal(ks[4], (NUM_EXPERTS, EXPERT_DIM), dtype=jnp.float32) * s
        W2 = jax.random.normal(ks[5], (NUM_EXPERTS, EXPERT_DIM, D_MODEL), dtype=jnp.float32) * s
        b2 = jax.random.normal(ks[6], (NUM_EXPERTS, D_MODEL), dtype=jnp.float32) * s
        return {'x': x, 'Wg': Wg, 'bg': bg, 'bias': bias, 'W1': W1, 'b1': b1, 'W2': W2, 'b2': b2}
    _L2_ffn_all = _L2_ffn_setup()
    _L2_ffn_in = {k: v for k, v in _L2_ffn_all.items() if k in ('Wg', 'bg', 'bias', 'W1', 'b1', 'W2', 'b2')}
    del _L2_ffn_all

    def _L3_gnn_setup():
        import jax, jax.numpy as jnp
        import numpy as np
        N_NODES = 50000

        def _gcn_conv(x, edge_index, W, b):
            n = x.shape[0]
            loop = jnp.arange(n, dtype=edge_index.dtype)
            src = jnp.concatenate([edge_index[0], loop])
            dst = jnp.concatenate([edge_index[1], loop])
            h = x @ W
            deg = jax.ops.segment_sum(jnp.ones_like(dst, dtype=h.dtype), dst, num_segments=n)
            dinv = jnp.where(deg > 0, jax.lax.rsqrt(deg), 0.0)
            norm = dinv[src] * dinv[dst]
            msg = h[src] * norm[:, None]
            out = jax.ops.segment_sum(msg, dst, num_segments=n)
            return out + b
        key = jax.random.key(seed)
        k1, k2, k3, k4 = jax.random.split(key, 4)
        in_c, hid = (256, 128)
        x = jax.random.normal(k1, (N_NODES, in_c), dtype=jnp.float32)
        edge_index = jax.random.randint(k2, (2, 25000), 0, N_NODES, dtype=jnp.int32)
        W_conv = jax.random.normal(k3, (in_c, hid), dtype=jnp.float32) * (1.0 / np.sqrt(in_c))
        b_conv = jnp.zeros((hid,), dtype=jnp.float32)
        limit = np.sqrt(6.0 / (hid + in_c))
        W_lin = jax.random.uniform(k4, (hid, in_c), dtype=jnp.float32, minval=-limit, maxval=limit)
        b_lin = jnp.zeros((in_c,), dtype=jnp.float32)
        return {'x': x, 'edge_index': edge_index, 'W_conv': W_conv, 'b_conv': b_conv, 'W_lin': W_lin, 'b_lin': b_lin}
    _L3_gnn_all = _L3_gnn_setup()
    _L3_gnn_in = {k: v for k, v in _L3_gnn_all.items() if k in ('W_conv', 'b_conv', 'W_lin', 'b_lin')}
    del _L3_gnn_all

    def _L3_ffn_setup():
        import jax, jax.numpy as jnp
        import numpy as np
        B, S, D = (8, 128, 256)
        H = 4 * D
        CAPACITY = 0.5
        key = jax.random.key(seed)
        ks = jax.random.split(key, 6)
        x = jax.random.normal(ks[0], (B, S, D), dtype=jnp.float32)
        attention_mask = jnp.zeros((B, 1, 1, S), dtype=jnp.float32)
        wr = jax.random.normal(ks[1], (D, 1), dtype=jnp.float32) * 0.02
        br = jnp.zeros((1,), dtype=jnp.float32)
        w1 = jax.random.normal(ks[2], (D, H), dtype=jnp.float32) * 0.02
        b1 = jnp.zeros((H,), dtype=jnp.float32)
        w2 = jax.random.normal(ks[3], (H, D), dtype=jnp.float32) * 0.02
        b2 = jnp.zeros((D,), dtype=jnp.float32)
        return {'x': x, 'attention_mask': attention_mask, 'wr': wr, 'br': br, 'w1': w1, 'b1': b1, 'w2': w2, 'b2': b2}
    _L3_ffn_all = _L3_ffn_setup()
    _L3_ffn_in = {k: v for k, v in _L3_ffn_all.items() if k in ('attention_mask', 'wr', 'br', 'w1', 'b1', 'w2', 'b2')}
    del _L3_ffn_all
    return {'x': x, 'src': src, 'dst': dst, 'L0_gnn_attn_l': _L0_gnn_in['attn_l'], 'L0_gnn_attn_r': _L0_gnn_in['attn_r'], 'L0_gnn_fe_W1': _L0_gnn_in['fe_W1'], 'L0_gnn_fe_b1': _L0_gnn_in['fe_b1'], 'L0_gnn_fe_g1': _L0_gnn_in['fe_g1'], 'L0_gnn_fe_be1': _L0_gnn_in['fe_be1'], 'L0_gnn_fe_m1': _L0_gnn_in['fe_m1'], 'L0_gnn_fe_v1': _L0_gnn_in['fe_v1'], 'L0_gnn_fe_W2': _L0_gnn_in['fe_W2'], 'L0_gnn_fe_b2': _L0_gnn_in['fe_b2'], 'L0_gnn_fe_g2': _L0_gnn_in['fe_g2'], 'L0_gnn_fe_be2': _L0_gnn_in['fe_be2'], 'L0_gnn_fe_m2': _L0_gnn_in['fe_m2'], 'L0_gnn_fe_v2': _L0_gnn_in['fe_v2'], 'L0_gnn_fn_W1': _L0_gnn_in['fn_W1'], 'L0_gnn_fn_b1': _L0_gnn_in['fn_b1'], 'L0_gnn_fn_g1': _L0_gnn_in['fn_g1'], 'L0_gnn_fn_be1': _L0_gnn_in['fn_be1'], 'L0_gnn_fn_m1': _L0_gnn_in['fn_m1'], 'L0_gnn_fn_v1': _L0_gnn_in['fn_v1'], 'L0_gnn_fn_W2': _L0_gnn_in['fn_W2'], 'L0_gnn_fn_b2': _L0_gnn_in['fn_b2'], 'L0_gnn_fn_g2': _L0_gnn_in['fn_g2'], 'L0_gnn_fn_be2': _L0_gnn_in['fn_be2'], 'L0_gnn_fn_m2': _L0_gnn_in['fn_m2'], 'L0_gnn_fn_v2': _L0_gnn_in['fn_v2'], 'L0_ffn_router_w': _L0_ffn_in['router_w'], 'L0_ffn_router_b': _L0_ffn_in['router_b'], 'L0_ffn_W1': _L0_ffn_in['W1'], 'L0_ffn_b1': _L0_ffn_in['b1'], 'L0_ffn_W2': _L0_ffn_in['W2'], 'L0_ffn_b2': _L0_ffn_in['b2'], 'L1_gnn_W': _L1_gnn_in['W'], 'L1_gnn_b': _L1_gnn_in['b'], 'L1_ffn_W_gat': _L1_ffn_in['W_gat'], 'L1_ffn_att_src': _L1_ffn_in['att_src'], 'L1_ffn_att_dst': _L1_ffn_in['att_dst'], 'L1_ffn_b_gat': _L1_ffn_in['b_gat'], 'L1_ffn_ln_gamma': _L1_ffn_in['ln_gamma'], 'L1_ffn_ln_beta': _L1_ffn_in['ln_beta'], 'L1_ffn_W1': _L1_ffn_in['W1'], 'L1_ffn_b1': _L1_ffn_in['b1'], 'L1_ffn_W2': _L1_ffn_in['W2'], 'L1_ffn_b2': _L1_ffn_in['b2'], 'L1_ffn_edge_index': _L1_ffn_in['edge_index'], 'L2_gnn_W_heads': _L2_gnn_in['W_heads'], 'L2_gnn_b_heads': _L2_gnn_in['b_heads'], 'L2_gnn_a_heads': _L2_gnn_in['a_heads'], 'L2_gnn_g_heads': _L2_gnn_in['g_heads'], 'L2_gnn_beta_heads': _L2_gnn_in['beta_heads'], 'L2_gnn_W_out': _L2_gnn_in['W_out'], 'L2_gnn_b_out': _L2_gnn_in['b_out'], 'L2_gnn_a_out': _L2_gnn_in['a_out'], 'L2_gnn_g_out': _L2_gnn_in['g_out'], 'L2_gnn_beta_out': _L2_gnn_in['beta_out'], 'L2_ffn_Wg': _L2_ffn_in['Wg'], 'L2_ffn_bg': _L2_ffn_in['bg'], 'L2_ffn_bias': _L2_ffn_in['bias'], 'L2_ffn_W1': _L2_ffn_in['W1'], 'L2_ffn_b1': _L2_ffn_in['b1'], 'L2_ffn_W2': _L2_ffn_in['W2'], 'L2_ffn_b2': _L2_ffn_in['b2'], 'L3_gnn_W_conv': _L3_gnn_in['W_conv'], 'L3_gnn_b_conv': _L3_gnn_in['b_conv'], 'L3_gnn_W_lin': _L3_gnn_in['W_lin'], 'L3_gnn_b_lin': _L3_gnn_in['b_lin'], 'L3_ffn_attention_mask': _L3_ffn_in['attention_mask'], 'L3_ffn_wr': _L3_ffn_in['wr'], 'L3_ffn_br': _L3_ffn_in['br'], 'L3_ffn_w1': _L3_ffn_in['w1'], 'L3_ffn_b1': _L3_ffn_in['b1'], 'L3_ffn_w2': _L3_ffn_in['w2'], 'L3_ffn_b2': _L3_ffn_in['b2']}

def reference(x, src, dst, L0_gnn_attn_l, L0_gnn_attn_r, L0_gnn_fe_W1, L0_gnn_fe_b1, L0_gnn_fe_g1, L0_gnn_fe_be1, L0_gnn_fe_m1, L0_gnn_fe_v1, L0_gnn_fe_W2, L0_gnn_fe_b2, L0_gnn_fe_g2, L0_gnn_fe_be2, L0_gnn_fe_m2, L0_gnn_fe_v2, L0_gnn_fn_W1, L0_gnn_fn_b1, L0_gnn_fn_g1, L0_gnn_fn_be1, L0_gnn_fn_m1, L0_gnn_fn_v1, L0_gnn_fn_W2, L0_gnn_fn_b2, L0_gnn_fn_g2, L0_gnn_fn_be2, L0_gnn_fn_m2, L0_gnn_fn_v2, L0_ffn_router_w, L0_ffn_router_b, L0_ffn_W1, L0_ffn_b1, L0_ffn_W2, L0_ffn_b2, L1_gnn_W, L1_gnn_b, L1_ffn_W_gat, L1_ffn_att_src, L1_ffn_att_dst, L1_ffn_b_gat, L1_ffn_ln_gamma, L1_ffn_ln_beta, L1_ffn_W1, L1_ffn_b1, L1_ffn_W2, L1_ffn_b2, L1_ffn_edge_index, L2_gnn_W_heads, L2_gnn_b_heads, L2_gnn_a_heads, L2_gnn_g_heads, L2_gnn_beta_heads, L2_gnn_W_out, L2_gnn_b_out, L2_gnn_a_out, L2_gnn_g_out, L2_gnn_beta_out, L2_ffn_Wg, L2_ffn_bg, L2_ffn_bias, L2_ffn_W1, L2_ffn_b1, L2_ffn_W2, L2_ffn_b2, L3_gnn_W_conv, L3_gnn_b_conv, L3_gnn_W_lin, L3_gnn_b_lin, L3_ffn_attention_mask, L3_ffn_wr, L3_ffn_br, L3_ffn_w1, L3_ffn_b1, L3_ffn_w2, L3_ffn_b2):
    import jax
    import jax.numpy as jnp

    def _L0_gnn_ref(n_feature, src, dst, attn_l, attn_r, fe_W1, fe_b1, fe_g1, fe_be1, fe_m1, fe_v1, fe_W2, fe_b2, fe_g2, fe_be2, fe_m2, fe_v2, fn_W1, fn_b1, fn_g1, fn_be1, fn_m1, fn_v1, fn_W2, fn_b2, fn_g2, fn_be2, fn_m2, fn_v2):
        import jax, jax.numpy as jnp
        import numpy as np
        N, E, IN, OUT = (625, 10000, 256, 256)
        H1, H2 = (IN // 64, OUT // 64)
        EPS = 1e-05
        ALPHA = 0.2

        def _bn(x, g, b, m, v):
            return (x - m) * jax.lax.rsqrt(v + EPS) * g + b

        def _mlp(x, W1, b1, g1, be1, m1, v1, W2, b2, g2, be2, m2, v2):
            h = jax.nn.leaky_relu(_bn(x @ W1 + b1, g1, be1, m1, v1), 0.01)
            return jax.nn.relu(_bn(h @ W2 + b2, g2, be2, m2, v2))
        a1 = n_feature @ attn_l
        a2 = n_feature @ attn_r
        a = jax.nn.leaky_relu(a1[src] + a2[dst], ALPHA)
        amax = jax.ops.segment_max(a, dst, num_segments=N)
        ex = jnp.exp(a - amax[dst])
        den = jax.ops.segment_sum(ex, dst, num_segments=N)
        att = ex / den[dst]
        hs = n_feature[src]
        hd = n_feature[dst]
        edge_feat = _mlp(jnp.concatenate([hs, hd], axis=1), fe_W1, fe_b1, fe_g1, fe_be1, fe_m1, fe_v1, fe_W2, fe_b2, fe_g2, fe_be2, fe_m2, fe_v2)
        msg = _mlp(jnp.concatenate([hs, edge_feat], axis=1), fn_W1, fn_b1, fn_g1, fn_be1, fn_m1, fn_v1, fn_W2, fn_b2, fn_g2, fn_be2, fn_m2, fn_v2)
        m = msg * att[:, None]
        return jax.ops.segment_sum(m, dst, num_segments=N) + n_feature

    def _L0_ffn_ref(x, router_w, router_b, W1, b1, W2, b2):
        import jax, jax.numpy as jnp
        import numpy as np
        B, K, D = (512, 16, 256)
        E = 32
        H = int(D * 0.25)
        xf = x.reshape(-1, D)
        logits = xf @ router_w.T + router_b
        idx = jnp.argmax(logits, axis=-1)
        w1t = jnp.take(W1, idx, axis=0)
        h = jnp.einsum('nd,ndh->nh', xf, w1t) + jnp.take(b1, idx, axis=0)
        h = jax.nn.relu(h)
        w2t = jnp.take(W2, idx, axis=0)
        out = jnp.einsum('nh,nhd->nd', h, w2t) + jnp.take(b2, idx, axis=0)
        out = jax.nn.relu(out)
        return out.reshape(x.shape)

    def _L1_gnn_ref(x, edge_index, W, b):
        import jax, jax.numpy as jnp
        import numpy as np
        N_NODES, N_EDGES, D_IN, D_HID, N_LAYERS = (50000, 25000, 256, 256, 3)
        'Stacked GCNConv (PyG semantics: self-loops + symmetric norm) with ReLU.\n            Dropout is identity (eval mode) for a deterministic baseline.'
        N = x.shape[0]
        loops = jnp.arange(N, dtype=edge_index.dtype)
        src = jnp.concatenate([edge_index[0], loops])
        dst = jnp.concatenate([edge_index[1], loops])
        deg = jax.ops.segment_sum(jnp.ones(dst.shape, jnp.float32), dst, num_segments=N)
        dinv = jnp.where(deg > 0, jax.lax.rsqrt(deg), 0.0)
        norm = (dinv[src] * dinv[dst])[:, None]
        h = x
        for l in range(W.shape[0]):
            t = h @ W[l]
            msg = t[src] * norm
            agg = jax.ops.segment_sum(msg, dst, num_segments=N)
            h = jax.nn.relu(agg + b[l])
        return h

    def _L1_ffn_ref(x, W_gat, att_src, att_dst, b_gat, ln_gamma, ln_beta, W1, b1, W2, b2, edge_index):
        import jax, jax.numpy as jnp
        import numpy as np
        B, N, D = (16, 128, 256)
        NUM_EXPERTS, TOP_K, HEADS = (4, 2, 4)
        N_EDGES = 32768
        LN_EPS = 1e-05

        def _layernorm(x, g, b):
            mu = x.mean(-1, keepdims=True)
            var = ((x - mu) ** 2).mean(-1, keepdims=True)
            return (x - mu) * jax.lax.rsqrt(var + LN_EPS) * g + b

        def _forward(x, edge_index, W_gat, att_src, att_dst, b_gat, ln_gamma, ln_beta, W1, b1, W2, b2):
            Bc, Nc, Dc = x.shape
            M = Bc * Nc
            x_flat = x.reshape(M, Dc)
            h = (x_flat @ W_gat).reshape(M, HEADS, NUM_EXPERTS)
            loops = jnp.arange(M, dtype=edge_index.dtype)
            src = jnp.concatenate([edge_index[0], loops])
            dst = jnp.concatenate([edge_index[1], loops])
            a_src = (h * att_src).sum(-1)
            a_dst = (h * att_dst).sum(-1)
            e = jax.nn.leaky_relu(a_src[src] + a_dst[dst], negative_slope=0.2)
            e_max = jax.ops.segment_max(e, dst, num_segments=M)
            ee = jnp.exp(e - e_max[dst])
            denom = jax.ops.segment_sum(ee, dst, num_segments=M)
            alpha = ee / (denom[dst] + 1e-16)
            msg = h[src] * alpha[:, :, None]
            agg = jax.ops.segment_sum(msg, dst, num_segments=M).reshape(M, HEADS * NUM_EXPERTS) + b_gat
            scores = _layernorm(agg, ln_gamma, ln_beta).reshape(M, HEADS, NUM_EXPERTS).mean(1)
            scores = scores.reshape(Bc, Nc, NUM_EXPERTS)
            topk_s, topk_i = jax.lax.top_k(scores, TOP_K)
            w = jax.nn.softmax(topk_s, axis=-1)
            out = jnp.zeros_like(x)
            for ei in range(NUM_EXPERTS):
                g = jnp.where(topk_i == ei, w, 0.0).sum(-1)
                hh = jax.nn.gelu(x @ W1[ei] + b1[ei], approximate=False)
                out = out + g[..., None] * (hh @ W2[ei] + b2[ei])
            return out
        return _forward(x, edge_index, W_gat, att_src, att_dst, b_gat, ln_gamma, ln_beta, W1, b1, W2, b2)

    def _L2_gnn_ref(embeds, W_heads, b_heads, a_heads, g_heads, beta_heads, W_out, b_out, a_out, g_out, beta_out, edge_index):
        import jax, jax.numpy as jnp
        import numpy as np
        ALPHA = 0.2
        LN_EPS = 1e-05

        def _gat_layer(x, src, dst, W, b, a, g, beta, N, concat):
            h = x @ W.T + b
            d = W.shape[0]
            s_src = h @ a[:d]
            s_dst = h @ a[d:]
            score = s_src[src] + s_dst[dst]
            e = jnp.exp(-jax.nn.leaky_relu(score, ALPHA))
            h_prime = jax.ops.segment_sum(e[:, None] * h[dst], src, num_segments=N)
            mu = jnp.mean(h_prime, axis=-1, keepdims=True)
            var = jnp.var(h_prime, axis=-1, keepdims=True)
            h_prime = (h_prime - mu) * jax.lax.rsqrt(var + LN_EPS) * g + beta
            return jax.nn.elu(h_prime) if concat else h_prime
        N = embeds.shape[0]
        src, dst = (edge_index[0], edge_index[1])
        H = W_heads.shape[0]
        heads = [_gat_layer(embeds, src, dst, W_heads[i], b_heads[i], a_heads[i], g_heads[i], beta_heads[i], N, concat=True) for i in range(H)]
        x = jnp.concatenate(heads, axis=1)
        out = _gat_layer(x, src, dst, W_out, b_out, a_out, g_out, beta_out, N, concat=False)
        return jax.nn.elu(out)

    def _L2_ffn_ref(x, Wg, bg, bias, W1, b1, W2, b2):
        import jax, jax.numpy as jnp
        import numpy as np
        D_MODEL = 256
        EXPERT_DIM = 512
        NUM_EXPERTS = 8
        TOP_K = 2
        SEQ_LEN = 64
        BATCH = 2
        x_flat = x.reshape(-1, D_MODEL)
        gate_logits = x_flat @ Wg + bg + bias
        topk_vals, topk_idx = jax.lax.top_k(gate_logits, TOP_K)
        topk_w = jax.nn.softmax(topk_vals, axis=-1)
        combine = (jax.nn.one_hot(topk_idx, NUM_EXPERTS, dtype=x.dtype) * topk_w[..., None]).sum(axis=1)
        h = jax.nn.relu(jnp.einsum('td,edh->teh', x_flat, W1) + b1)
        y = jnp.einsum('teh,ehd->ted', h, W2) + b2
        out = jnp.einsum('ted,te->td', y, combine)
        return out.reshape(x.shape)

    def _L3_gnn_ref(x, edge_index, W_conv, b_conv, W_lin, b_lin):
        import jax, jax.numpy as jnp
        import numpy as np
        N_NODES = 50000

        def _gcn_conv(x, edge_index, W, b):
            n = x.shape[0]
            loop = jnp.arange(n, dtype=edge_index.dtype)
            src = jnp.concatenate([edge_index[0], loop])
            dst = jnp.concatenate([edge_index[1], loop])
            h = x @ W
            deg = jax.ops.segment_sum(jnp.ones_like(dst, dtype=h.dtype), dst, num_segments=n)
            dinv = jnp.where(deg > 0, jax.lax.rsqrt(deg), 0.0)
            norm = dinv[src] * dinv[dst]
            msg = h[src] * norm[:, None]
            out = jax.ops.segment_sum(msg, dst, num_segments=n)
            return out + b
        h = _gcn_conv(x, edge_index, W_conv, b_conv)
        return h @ W_lin + b_lin

    def _L3_ffn_ref(x, attention_mask, wr, br, w1, b1, w2, b2):
        import jax, jax.numpy as jnp
        import numpy as np
        B, S, D = (8, 128, 256)
        H = 4 * D
        CAPACITY = 0.5
        b, s, d = x.shape
        weights = (jnp.einsum('bsd,do->bso', x, wr) + br)[..., 0]
        k = max(1, int(CAPACITY * s))
        kk = k - 1 if k > 1 else 1
        _, idx = jax.lax.top_k(weights, k)
        sel_idx = idx[:, :kk]
        sel = jnp.take_along_axis(x, sel_idx[:, :, None], axis=1)
        h = jax.nn.gelu(jnp.einsum('bkd,dh->bkh', sel, w1) + b1)
        y = jnp.einsum('bkh,hd->bkd', h, w2) + b2
        w_sel = jnp.take_along_axis(weights, sel_idx, axis=1)
        y = y * w_sel[..., None]
        batch_idx = jnp.arange(b)[:, None]
        processed = jnp.zeros_like(x).at[batch_idx, sel_idx].set(y)
        return processed + x
    edge_index = jnp.stack([src, dst])
    x = x + _L0_gnn_ref(_layernorm(x, axis=-1), src, dst, L0_gnn_attn_l, L0_gnn_attn_r, L0_gnn_fe_W1, L0_gnn_fe_b1, L0_gnn_fe_g1, L0_gnn_fe_be1, L0_gnn_fe_m1, L0_gnn_fe_v1, L0_gnn_fe_W2, L0_gnn_fe_b2, L0_gnn_fe_g2, L0_gnn_fe_be2, L0_gnn_fe_m2, L0_gnn_fe_v2, L0_gnn_fn_W1, L0_gnn_fn_b1, L0_gnn_fn_g1, L0_gnn_fn_be1, L0_gnn_fn_m1, L0_gnn_fn_v1, L0_gnn_fn_W2, L0_gnn_fn_b2, L0_gnn_fn_g2, L0_gnn_fn_be2, L0_gnn_fn_m2, L0_gnn_fn_v2)
    x = x + _L0_ffn_ref(_layernorm(x, axis=-1)[None], L0_ffn_router_w, L0_ffn_router_b, L0_ffn_W1, L0_ffn_b1, L0_ffn_W2, L0_ffn_b2)[0]
    x = x + _L1_gnn_ref(_layernorm(x, axis=-1), edge_index, L1_gnn_W, L1_gnn_b)
    x = x + _L1_ffn_ref(_layernorm(x, axis=-1)[None], L1_ffn_W_gat, L1_ffn_att_src, L1_ffn_att_dst, L1_ffn_b_gat, L1_ffn_ln_gamma, L1_ffn_ln_beta, L1_ffn_W1, L1_ffn_b1, L1_ffn_W2, L1_ffn_b2, L1_ffn_edge_index)[0]
    x = x + _L2_gnn_ref(_layernorm(x, axis=-1), L2_gnn_W_heads, L2_gnn_b_heads, L2_gnn_a_heads, L2_gnn_g_heads, L2_gnn_beta_heads, L2_gnn_W_out, L2_gnn_b_out, L2_gnn_a_out, L2_gnn_g_out, L2_gnn_beta_out, edge_index)
    x = x + _L2_ffn_ref(_layernorm(x, axis=-1)[None], L2_ffn_Wg, L2_ffn_bg, L2_ffn_bias, L2_ffn_W1, L2_ffn_b1, L2_ffn_W2, L2_ffn_b2)[0]
    x = x + _L3_gnn_ref(_layernorm(x, axis=-1), edge_index, L3_gnn_W_conv, L3_gnn_b_conv, L3_gnn_W_lin, L3_gnn_b_lin)
    x = x + _L3_ffn_ref(_layernorm(x, axis=-1)[None], L3_ffn_attention_mask, L3_ffn_wr, L3_ffn_br, L3_ffn_w1, L3_ffn_b1, L3_ffn_w2, L3_ffn_b2)[0]
    return x

_drawn_inputs = setup_inputs


def setup_inputs(seed=0):
    import zlib

    import numpy as np

    out = dict(_drawn_inputs(seed))
    spreads = {'L1_gnn_b': (0.0, 0.1),
     'L1_ffn_b_gat': (0.0, 0.1),
     'L1_ffn_ln_gamma': (1.0, 0.6),
     'L1_ffn_ln_beta': (0.0, 0.8),
     'L1_ffn_b1': (0.0, 0.1),
     'L1_ffn_b2': (0.0, 0.1),
     'L2_gnn_g_heads': (1.0, 0.2),
     'L2_gnn_beta_heads': (0.0, 0.1),
     'L2_gnn_g_out': (1.0, 0.2),
     'L2_gnn_beta_out': (0.0, 0.1),
     'L2_ffn_bias': (0.0, 0.482),
     'L3_gnn_b_conv': (0.0, 0.1),
     'L3_gnn_b_lin': (0.0, 0.1),
     'L3_ffn_b1': (0.0, 0.8),
     'L3_ffn_b2': (0.0, 0.768)}
    factors = {'L0_gnn_attn_r': 6.976,
     'L0_gnn_fe_W1': 5.352,
     'L0_gnn_fe_b1': 8.0,
     'L0_gnn_fe_g1': 7.172,
     'L0_gnn_fe_be1': 8.0,
     'L0_gnn_fe_m1': 8.0,
     'L0_gnn_fe_v1': 8.0,
     'L0_gnn_fe_b2': 6.477,
     'L0_gnn_fe_g2': 6.87,
     'L0_gnn_fe_be2': 6.627,
     'L0_gnn_fe_m2': 3.54,
     'L0_gnn_fe_v2': 6.852,
     'L0_gnn_fn_b1': 3.651,
     'L0_gnn_fn_be1': 8.0,
     'L0_gnn_fn_m1': 8.0,
     'L0_ffn_b1': 8.0,
     'L0_ffn_b2': 4.19,
     'L1_ffn_att_src': 8.0,
     'L1_ffn_att_dst': 8.0,
     'L2_gnn_a_heads': 3.611,
     'L2_gnn_a_out': 64.0,
     'L2_ffn_bg': 7.642,
     'L2_ffn_b1': 8.0,
     'L2_ffn_b2': 8.0,
     'L3_ffn_wr': 5.228,
     'L3_ffn_w1': 5.261,
     'L3_ffn_w2': 5.046}
    for name, (base, spread) in spreads.items():
        noise = np.random.default_rng([zlib.crc32(name.encode()), seed]).standard_normal(out[name].shape)
        drawn = base * np.exp(spread * noise) if base else spread * noise
        out[name] = jnp.asarray(drawn.astype(out[name].dtype))
    for name, factor in factors.items():
        out[name] = (out[name] * factor).astype(out[name].dtype)
    return out
```

```python
import numpy as np

N, P, J, D = 625, 125, 5, 256
E1, E2 = 20000, 32768
NT1, NT2 = E1 // 125, E2 // 128
FFN_TILES = [16, 16, 32, 8]
FFN_BASE = [0, 16, 32, 64]
FFN_EXPERTS = [32, 4, 8, 1]
ROW_SIZES = [("b", 520), ("g", 520), ("be", 520), ("m", 520), ("v", 520),
             ("router_b", 32), ("gcn_b2", 256),
             ("att_src", 16), ("att_dst", 16), ("b_gat", 16), ("ln_gamma", 16), ("ln_beta", 16),
             ("b_heads", 512), ("a_src", 512), ("a_dst", 512), ("g_heads", 512), ("beta_heads", 512),
             ("b_out", 256), ("a_out_src", 256), ("a_out_dst", 256), ("g_out", 256), ("beta_out", 256),
             ("bg", 8), ("bias", 8), ("b_lin", 256), ("br", 1)]
ROW_AT, _at = {}, 0
for _n, _s in ROW_SIZES:
    ROW_AT[_n] = (_at, _s)
    _at += _s
ROWS, ROWS_L0 = _at, 2600
W_SIZES = [("table", 14), ("fn_W1b", 4), ("router", 32), ("W_gat", 16), ("Wg", 8), ("wr", 1), ("W_conv", 128),
           ("W_heads", 512), ("gcn_W", 768)]
W_AT, _at = {}, 0
for _n, _s in W_SIZES:
    W_AT[_n] = (_at, _s)
    _at += _s
WCOLS = _at
COL_FFN = [0, 16, 32, 64]
COL_GCN, COL_CONV, COLS = 72, 76, 77


SEAM = 4
TILES_PER_NODE_TILE = NT1 // J


def usual_node_tiles(t):
    m, at = divmod(t, TILES_PER_NODE_TILE)
    return [k for k, near in ((m - 1, at < SEAM), (m, True), (m + 1, at >= TILES_PER_NODE_TILE - SEAM))
            if near and 0 <= k < J]


def gnn_ffn_program(nc, a, out):
    import concourse.bass as bass
    from concourse import mybir
    from concourse.alu_op_type import AluOpType as ALU
    from contextlib import ExitStack

    F32, BF16, F16, I32 = mybir.dt.float32, mybir.dt.bfloat16, mybir.dt.float16, mybir.dt.int32
    ACT = mybir.ActivationFunctionType
    AX = mybir.AxisListType.X
    EPS = 1e-5
    ABSENT = -1e30
    ds = bass.ds

    ctx = ExitStack()
    with ctx:
        def sb(name, shape, dt=F32):
            return ctx.enter_context(nc.sbuf_tensor(name, shape, dt))

        ident = sb("ident", [128, 128])
        ident16 = sb("ident16", [128, 128], BF16)
        node_iota = sb("node_iota", [128, N], F16)
        node_id = sb("node_id", [128, J])
        before8 = sb("before8", [P, 8, 8])
        before4 = sb("before4", [P, 4, 4])
        rev32 = sb("rev32", [P, 32])
        ones_row = sb("ones_row", [1, N])
        ones_col = sb("ones_col", [P, 1])
        rows = sb("rows", [128, ROWS])
        cols = sb("cols", [128, COLS])
        wmat = sb("wmat", [128, 2, WCOLS])
        wout = sb("wout", [128, 4, D])
        usual = sb("usual", [P, 1])
        is_usual = sb("is_usual", [1, 1], I32)
        wlin = sb("wlin", [128, D])
        w2rows = sb("w2rows", [32, 2, D])
        part = sb("part", [32, 4])
        b2 = sb("b2", [32, 4, D])
        id1 = sb("id1", [P, 2, NT1])
        id2 = sb("id2", [128, 2, NT2])
        X = sb("X", [P, J, D])
        XN = sb("XN", [P, J, D])
        XT = sb("XT", [128, 2, N])
        TT = sb("TT", [P, J, D])
        stats = sb("stats", [P, J, 6])
        mv = sb("mv", [P, J, 2])
        veps = sb("veps", [P, J])
        std = sb("std", [P, J])
        rstd = sb("rstd", [P, J])
        C1 = sb("C1", [P, J, N])
        AH = sb("AH", [P, J, N])
        C2 = sb("C2", [P, J, N])
        C2T = sb("C2T", [P, J, N])
        big = sb("big", [128, 4, J * N])
        bounds = big[0:P, 2, 400:720].rearrange("p (a b) -> p a b", a=2)
        inside = big[0:P, 2, 720:880]
        inside2 = big[0:P, 2, 2000:2160]
        hid_all = sb("hid_all", [128, 4, 632])
        onehot = hid_all[:, :, :].rearrange("p b n -> p (b n)").bitcast(BF16).rearrange(
            "p (b s n) -> p b s n", b=4, s=2)
        HA = C2[:, :, :].rearrange("p j n -> p (j n)")[:, 0:J * 512].rearrange("p (j n) -> p j n", j=J)
        HB_ = C2T[:, :, :].rearrange("p j n -> p (j n)")[:, 0:J * 512].rearrange("p (j n) -> p j n", j=J)
        TAB = sb("TAB", [P, J, 14])
        tabf = sb("tabf", [P, 2, J, 10])
        tabr = sb("tabr", [P, 2, J, 10])
        tab16 = sb("tab16", [P, 2, J, 10, 3], BF16)
        idxrow = big[0:P, 1, 0:2000].bitcast(I32).rearrange("p (b c) -> p b c", b=2)
        idxrow16 = big[0:P, 1, 2000:3000].bitcast(F16).rearrange("p (b c) -> p b c", b=2)
        onehotT = big[0:P, 2:4, :].rearrange("p a c -> p (a c)")[:, 0:5000].bitcast(BF16).rearrange(
            "p (b s j c) -> p b s j c", b=2, s=2, j=J)
        in_AH = AH[:, :, :].rearrange("p j n -> p (j n)")
        in_C2T = C2T[:, :, :].rearrange("p j n -> p (j n)")
        GS = in_AH[:, 0:10 * NT1].rearrange("p (t c) -> p t c", c=10)
        h1 = in_AH[:, 1600:2240].rearrange("p (t c) -> p t c", c=4)
        h2 = in_AH[:, 2240:2880].rearrange("p (t c) -> p t c", c=4)
        FR = h1
        hs16 = in_C2T[:, 0:16 * NT1].bitcast(BF16).rearrange("p (t c) -> p t c", c=32)
        EX = in_C2T[:, 2560:2560 + NT1]
        in_TT = TT[:, :, :].rearrange("p j n -> p (j n)")
        foldS, foldT = in_TT[:, 0:520], in_TT[:, 520:1040]
        idx1 = big[0:P, 2, 0:2 * NT1].bitcast(I32).rearrange("p (a b) -> p a b", a=2)
        idx2 = big[:, 2, 1000:1000 + 2 * NT2].bitcast(I32).rearrange("p (a b) -> p a b", a=2)
        w2v = big[0:32, 3, 0:514].rearrange("p (a b) -> p a b", a=2)
        w2r = big[0:32, 3, 514:1028].rearrange("p (a b) -> p a b", a=2)
        w2h = big[0:32, 3, 1028:1285].bitcast(BF16).rearrange("p (a b) -> p a b", a=2)
        w2m = big[0:32, 3, 1285:1542].bitcast(BF16).rearrange("p (a b) -> p a b", a=2)
        w2s = sb("w2s", [32, 2, 257], BF16)
        hT = sb("hT", [32, 2, 500], BF16)
        EF = big[:, 2:4, :].rearrange("p a c -> p (a c)")[:, 0:2000].rearrange("p (b h c) -> p b h c", b=2, h=2)
        msg = big[0:P, 0, 0:4 * 257].rearrange("p (b c) -> p b c", b=4)
        msgr = big[0:P, 0, 1100:1100 + 4 * 257].rearrange("p (b c) -> p b c", b=4)
        msg16 = big[0:P, 1, 0:1548].bitcast(BF16).rearrange("p (b s c) -> p b s c", b=4, s=3)[:, :, :, 0:257]
        wtile = sb("wtile", [128, 4, 512])
        hid, hidg = hid_all[:, 0:2, 0:N], hid_all[:, 2:4, 0:N]
        gate = sb("gate", [P, J, 32])
        gateT = sb("gateT", [32, N])
        grow16 = big[:, 0:2, :].rearrange("p a c -> p (a c)")[:, 0:5000].bitcast(BF16).rearrange(
            "p (e n) -> p e n", e=16)
        grow = big[:, 0:2, :].rearrange("p a c -> p (a c)")[:, 0:5000].rearrange("p (e n) -> p e n", e=8)
        gateT16 = big[0:32, 2, 0:313].bitcast(BF16)[:, 0:N]
        pair16 = big[0:32, 2, 320:1344].bitcast(BF16).rearrange("p (e c) -> p e c", e=16)
        s32a = sb("s32a", [P, J, 32])
        s32b = sb("s32b", [P, J, 32])
        s5a = sb("s5a", [P, J])
        s5b = sb("s5b", [P, J])
        s40a = sb("s40a", [P, 40])
        s40b = sb("s40b", [P, 40])
        s320a = in_TT[:, 0:320].rearrange("p (j c) -> p j c", j=J)
        s320b = in_TT[:, 320:640].rearrange("p (j c) -> p j c", j=J)
        mx = sb("mx", [P, J, 4])
        bmax = sb("bmax", [P, J, 4])
        asrc = sb("asrc", [P, J, 8])
        adst = sb("adst", [P, J, 8])
        esrc = sb("esrc", [P, J, 8])
        nb02 = sb("nb02", [P, J, 8])
        pa02 = sb("pa02", [P, J, 4])
        hx = sb("hx", [P, J, 4, 5])
        dinv = sb("dinv", [P, J])
        wrow = big[0:P, 3, 0:N]

        PS = ctx.enter_context(nc.psum_tensor("PS", [128, 8, 512], F32))

        def wide(b, p=128):
            return PS[0:p, b:b + 2, :].rearrange("p b c -> p (b c)")[:, 0:640].rearrange(
                "p (j c) -> p j c", c=128)[:, :, 0:125]

        def yv(j):
            return PS[0:P, 4 + j // 2, (j % 2) * 256:(j % 2) * 256 + 256]

        def blocks(ap):
            return ap.rearrange("p (b c) -> p b c", c=125)

        def row(name, p=P):
            o, s = ROW_AT[name]
            return rows[0:p, o:o + s]

        def wm(name, h):
            o, s = W_AT[name]
            return wmat[:, h, o:o + s]

        def mid_b(ap, n):
            return ap.unsqueeze(1).to_broadcast([ap.shape[0], n, ap.shape[1]])

        def last_b(ap, n):
            return ap.unsqueeze(2).to_broadcast([ap.shape[0], ap.shape[1], n])

        names = """consts usual_ready usual_psum usual_known x_in idx_in l0_in rest_in out_done
            vector_step pool_step
            var_ready std_ready ln_rows xt_psum xt_sb
            table_ready tables_split onehot_ready onehot_used counts_out
            fold_var fold_std
            a1_row edge_max_ready rows_cast ids_onehot gathered gather_read
            logit_in edge_exp h1_ready
            hT_psum hT_sb fe_psum ef_act ef_dve fn1_psum fn1_read h2_ready
            hT2_psum hT2_sb fn2_psum msg_ready msg_hi msg_rest msg_mid msg_lo msg_used edges_done
            deg_ready deg_std b_ready bt_psum bt_act bt_dve
            t_ready t_act t_dve agg_psum h_act h_dve last_psum
            gat_h gat_a row_psum row_read rows2_psum gat_sum gat_sub gat_exp gat_mul gat_mm
            gat_var gat_std sm_in sm_out gates_ready gr_psum gr_act gr_dve gt_psum gt_sb
            h_psum h_sb h_gated y_used y_ready logits_ready
            hh_psum s_ready head_row esrc_ready relu_act relu_dve head_exp head_mul head_psum head_out head_read
            hln_var hln_std elu_in elu_exp x2_ready x2_psum x2_act x2_dve
            ho_psum so_ready o_row o_exp o_mul o_psum oelu_in oelu_exp
            w_col w_row_psum w_row_sb w_bcast x_final tri_ready""".split()
        S = {n: ctx.enter_context(nc.semaphore(n)) for n in names}
        idx_row_in = [ctx.enter_context(nc.semaphore(f"idx_row_in{u}")) for u in range(2)]
        w_in = [ctx.enter_context(nc.semaphore(f"w_in{u}")) for u in range(4)]

        block = ctx.enter_context(nc.Block())
        NCONST = 16

        @block.sync
        def _(sp):
            sp.dma_start(X[:], a["x"].rearrange("(j p) d -> p j d", p=P)).then_inc(S["x_in"], 16)
            sp.dma_start(idx2, a["idx2"]).then_inc(S["idx_in"], 16)
            sp.dma_start(idx1, a["idx1"]).then_inc(S["idx_in"], 16)
            sp.dma_start(bounds, a["bounds"].rearrange("a b -> (a b)").unsqueeze(0).to_broadcast([P, 2 * NT1])
                         .rearrange("p (a b) -> p a b", a=2)).then_inc(S["idx_in"], 16)
            sp.dma_start(wmat[:], a["wmat"]).then_inc(S["l0_in"], 16)
            sp.dma_start(w2rows[:], a["w2rows"]).then_inc(S["l0_in"], 16)
            sp.dma_start(part[:], a["part"]).then_inc(S["l0_in"], 16)
            sp.dma_start(rows[:], a["rows"].to_broadcast([128, ROWS])).then_inc(S["l0_in"], 16)
            sp.dma_start(cols[:], a["cols"]).then_inc(S["rest_in"], 16)
            sp.dma_start(wout[:], a["wout"].rearrange("(k p) n -> p k n", p=128)).then_inc(S["rest_in"], 16)
            sp.dma_start(wlin[:], a["wlin"]).then_inc(S["rest_in"], 16)
            sp.dma_start(b2[:], a["b2"]).then_inc(S["rest_in"], 16)
            for u in range(4):
                sp.dma_start(wtile[:, u, :], a["wffn"][u]).then_inc(w_in[u], 16)

            def id_rows(i, first):
                for u in range(2):
                    if not first:
                        sp.wait_ge(S["rows_cast"], 2 * i + u - 1)
                    sp.dma_start(idxrow[:, u, :], a["idxrow"][ds(2 * i + u, 1), :].to_broadcast([P, 1000])
                                 ).then_inc(idx_row_in[u], 16)
            sp.wait_ge(S["edge_max_ready"], 1)
            id_rows(0, True)
            with sp.Fori(1, 20) as i:
                id_rows(i, False)

            with sp.Fori(1, sum(FFN_TILES) // 4) as i:
                for u in range(4):
                    sp.wait_ge(S["y_used"], 4 * i + u - 3)
                    sp.dma_start(wtile[:, u, :], a["wffn"][ds(4 * i + u, 1), :, :].rearrange("a p c -> p (a c)")
                                 ).then_inc(w_in[u], 16)

            sp.wait_ge(S["x_final"], 1)
            sp.dma_start(out.rearrange("(j p) d -> p j d", p=P), X[:]).then_inc(S["out_done"], 16)
            sp.wait_ge(S["out_done"], 16)

        @block.gpsimd
        def _(pool):
            g = nc.gpsimd
            step = [0]

            def link(ins):
                step[0] += 1
                ins.then_inc(S["pool_step"], 1)
                pool.wait_ge(S["pool_step"], step[0])

            link(g.memset(ident[:], 0.0))
            link(g.memset(before8[:], 1.0))
            link(g.memset(before4[:], 1.0))
            c = S["consts"]
            g.affine_select(out=ident[:], in_=ident[:], compare_op=ALU.not_equal, fill=1.0, base=0,
                            pattern=[[-1, 128]], channel_multiplier=1).then_inc(c, 1)
            pool.wait_ge(c, 1)
            g.tensor_copy(ident16[:], ident[:]).then_inc(c, 1)
            g.iota(node_iota[:], pattern=[[1, N]], base=0, channel_multiplier=0,
                   allow_small_or_imprecise_dtypes=True).then_inc(c, 1)
            g.iota(node_id[:], pattern=[[P, J]], base=0, channel_multiplier=1,
                   allow_small_or_imprecise_dtypes=True).then_inc(c, 1)
            g.affine_select(out=before8[:], in_=before8[:], compare_op=ALU.is_gt, fill=0.0, base=0,
                            pattern=[[1, 8], [-1, 8]], channel_multiplier=0).then_inc(c, 1)
            g.affine_select(out=before4[:], in_=before4[:], compare_op=ALU.is_gt, fill=0.0, base=0,
                            pattern=[[1, 4], [-1, 4]], channel_multiplier=0).then_inc(c, 1)
            g.iota(rev32[:], pattern=[[-1, 32]], base=32, channel_multiplier=0,
                   allow_small_or_imprecise_dtypes=True).then_inc(c, 1)
            g.memset(ones_row[:], 1.0).then_inc(c, 1)
            g.memset(hs16, 0.0).then_inc(c, 1)
            pool.wait_ge(c, 9)
            g.memset(hs16[:, :, 24:27], 1.0).then_inc(c, 1)
            g.memset(hx[:, :, :, 4:5], 1.0).then_inc(c, 1)
            g.memset(tabf[:, 0, :, 9:10], 0.0).then_inc(c, 1)
            g.memset(tabf[:, 1, :, 5:9], 0.0).then_inc(c, 1)
            g.memset(ones_col[:], 1.0).then_inc(c, 1)
            g.memset(s5b[:], 0.0).then_inc(c, 1)
            g.memset(std[:], 0.0).then_inc(c, 1)

            def rest(t, b):
                pool.wait_ge(S["msg_hi"], t + 1)
                g.tensor_tensor(msgr[:, b, :], msg[:, b, :], msg16[:, b, 0, :], ALU.subtract
                                ).then_inc(S["msg_rest"], 1)

            def rests(i, last):
                for q in range(8):
                    t = 8 * i + q
                    b = q % 4
                    if not (last and q == 7):
                        rest(t + 1, (q + 1) % 4)
                    pool.wait_ge(S["msg_mid"], t + 1)
                    g.tensor_tensor(msg16[:, b, 2, :], msgr[:, b, :], msg16[:, b, 1, :], ALU.subtract
                                    ).then_inc(S["msg_lo"], 1)
            rest(0, 0)
            with pool.Fori(0, 19) as i:
                rests(i, False)
            rests(19, True)

            tri = big[0:P, 0, :]
            pool.wait_ge(S["y_ready"], 3)
            g.memset(tri, 1.0).then_inc(S["tri_ready"], 1)
            pool.wait_ge(S["tri_ready"], 1)
            triv = tri.rearrange("p (j n) -> p j n", j=J)
            g.affine_select(out=triv, in_=triv, compare_op=ALU.is_gt, fill=0.0, base=0,
                            pattern=[[P, J], [-1, N]], channel_multiplier=1).then_inc(S["tri_ready"], 1)
            pool.wait_ge(S["w_row_sb"], 1)
            g.partition_broadcast(wrow, gateT[0:1, :], channels=P).then_inc(S["w_bcast"], 1)

        @block.scalar
        def _(act):
            s = nc.scalar

            def layernorm(k):
                act.wait_ge(S["var_ready"], k + 1)
                s.activation(std[:], veps[:], ACT.Sqrt).then_inc(S["std_ready"], 1)
                act.wait_ge(S["xt_psum"], 2 * k + 1)
                s.copy(blocks(XT[:, 0, :]), wide(0)).then_inc(S["xt_sb"], 1)

            def evacuate_counts(C):
                s.copy(C[:, :, 0:500], PS[0:P, 0:5, 0:500])
                s.copy(C[:, 0:4, 500:625], PS[0:P, 5, 0:500].rearrange("p (m c) -> p m c", m=4))
                s.copy(C[:, 4, 500:625], PS[0:P, 6, 0:125]).then_inc(S["counts_out"], 1)

            act.wait_ge(S["consts"], NCONST)
            layernorm(0)
            act.wait_ge(S["fold_var"], 1)
            s.activation(foldS, foldS, ACT.Sqrt).then_inc(S["fold_std"], 1)
            act.wait_ge(S["onehot_used"], NT2)
            evacuate_counts(C2)
            act.wait_ge(S["onehot_used"], NT2 + NT1)
            evacuate_counts(C1)

            def cast_ids(i, first):
                for u in range(2):
                    t = 2 * i + u
                    act.wait_ge(idx_row_in[u], 16 * i + 16)
                    if not first:
                        act.wait_ge(S["ids_onehot"], t - 1)
                    s.copy(idxrow16[:, u, :], idxrow[:, u, :]).then_inc(S["rows_cast"], 1)
            cast_ids(0, True)
            with act.Fori(1, 20) as i:
                cast_ids(i, False)

            act.wait_ge(S["logit_in"], 1)
            s.activation(EX, EX, ACT.Exp).then_inc(S["edge_exp"], 1)

            hTp = [blocks(PS[0:32, b, 0:500]) for b in range(8)]

            def edge_hT(t, u):
                act.wait_ge(S["hT_psum"], t + 1)
                s.copy(blocks(hT[:, u, :]), hTp[u]).then_inc(S["hT_sb"], 1)

            def edge_relu(t, u):
                act.wait_ge(S["fe_psum"], t + 1)
                s.activation(EF[:, u, 0, :], PS[:, 2 + 2 * u, 0:500], ACT.Relu).then_inc(S["ef_act"], 1)

            edge_hT(0, 0)

            def loop_a(i, last):
                for u in range(2):
                    if not (last and u == 1):
                        edge_hT(2 * i + u + 1, 1 - u)
                    edge_relu(2 * i + u, u)
            loop_a(0, False)
            with act.Fori(1, 19) as i:
                loop_a(i, False)
            loop_a(19, True)

            def msg_high(t, b):
                act.wait_ge(S["msg_ready"], t + 1)
                s.copy(msg16[:, b, 0, :], msg[:, b, :]).then_inc(S["msg_hi"], 1)

            def loop_b(i, last):
                for q in range(8):
                    t = 8 * i + q
                    b = q % 4
                    if q % 4 == 0 and not (last and q == 4):
                        gnext = 2 * i + q // 4 + 1
                        act.wait_ge(S["hT2_psum"], gnext + 1)
                        s.copy(blocks(hT[:, 1 - q // 4, :]), hTp[5]).then_inc(S["hT2_sb"], 1)
                    if not (last and q == 7):
                        msg_high(t + 1, (q + 1) % 4)
                    act.wait_ge(S["msg_rest"], t + 1)
                    s.copy(msg16[:, b, 1, :], msgr[:, b, :]).then_inc(S["msg_mid"], 1)
            act.wait_ge(S["hT2_psum"], 1)
            s.copy(blocks(hT[:, 0, :]), hTp[5]).then_inc(S["hT2_sb"], 1)
            msg_high(0, 0)
            loop_b(0, False)
            with act.Fori(1, 19) as i:
                loop_b(i, False)
            loop_b(19, True)

            def gate_rows(n, done):
                tiles = 16 if n == 0 else FFN_EXPERTS[n]
                dst = grow16 if n == 0 else grow
                for e in range(0, tiles, 2):
                    act.wait_ge(S["gr_psum"], done + e + 1)
                    s.copy(blocks(dst[:, e, :]), wide(0)).then_inc(S["gr_act"], 1)

            def hidden(n, func):
                base, T = FFN_BASE[n], FFN_TILES[n]

                def body(i, first):
                    for u in range(4):
                        t = base + 4 * i + u
                        act.wait_ge(S["h_psum"], t + 1)
                        if not (first and u < 2):
                            act.wait_ge(S["h_gated"] if n < 3 else S["y_used"], t - 1)
                        s.activation(blocks(hid[:, u % 2, :]), wide(2 * (u % 2)), func,
                                     bias=cols[:, ds(COL_FFN[n] + 4 * i + u, 1)]).then_inc(S["h_sb"], 1)
                body(0, True)
                with act.Fori(1, T // 4) as i:
                    body(i, False)

            act.wait_ge(S["rest_in"], 64)
            layernorm(1)
            gate_rows(0, 0)
            hidden(0, ACT.Relu)

            act.wait_ge(S["deg_ready"], 1)
            s.activation(dinv[:], dinv[:], ACT.Sqrt).then_inc(S["deg_std"], 1)
            for i in range(0, 10, 2):
                act.wait_ge(S["bt_psum"], i + 1)
                if i < 5:
                    s.activation(blocks(AH[:, i, :]), wide(0, P), ACT.Copy, scale=dinv[:, i:i + 1]).then_inc(S["bt_act"], 1)
                else:
                    s.copy(blocks(C2T[:, i - 5, :]), wide(0, P)).then_inc(S["bt_act"], 1)
            layernorm(2)
            tps = PS[0:P, 4:7, :].rearrange("p b c -> p (b c)")
            for l in range(3):
                act.wait_ge(S["t_ready"], l + 1)
                s.copy(TT[:, 0:2, :], tps[:, 0:512].rearrange("p (j c) -> p j c", c=D)).then_inc(S["t_act"], 1)
                if l < 2:
                    act.wait_ge(S["agg_psum"], 2 * l + 1)
                    s.activation(blocks(XT[:, 0, :]), wide(0), ACT.Relu,
                                 bias=cols[:, COL_GCN + 2 * l:COL_GCN + 2 * l + 1]).then_inc(S["h_act"], 1)

            layernorm(3)

            def z(b):
                return big[0:P, b, :].rearrange("p (j n) -> p j n", j=J)

            def scores(h):
                act.wait_ge(S["rows2_psum"], 2 * h + 1)
                for j in range(J):
                    ins = s.activation(blocks(z(h)[:, j, :]), wide(0, P), ACT.Relu,
                                       bias=asrc[:, j, h:h + 1])
                ins.then_inc(S["gat_sum"], 1)

            def exps(h):
                act.wait_ge(S["gat_sub"], h + 1)
                for j in range(J):
                    ins = s.activation(z(h)[:, j, :], z(h)[:, j, :], ACT.Exp, bias=pa02[:, j, h:h + 1])
                ins.then_inc(S["gat_exp"], 1)
            scores(0)
            for h in range(4):
                if h < 3:
                    scores(h + 1)
                exps(h)
            act.wait_ge(S["gat_var"], 1)
            s.activation(s5a[:], s5a[:], ACT.Sqrt).then_inc(S["gat_std"], 1)
            act.wait_ge(S["sm_in"], 1)
            s.activation(s32a[:, :, 0:4], s32a[:, :, 0:4], ACT.Exp).then_inc(S["sm_out"], 1)
            gate_rows(1, 16)
            hidden(1, ACT.Gelu)

            layernorm(4)
            act.wait_ge(S["s_ready"], 1)
            s.activation(esrc[:], asrc[:], ACT.Exp, scale=-0.2).then_inc(S["esrc_ready"], 1)

            def head_relu(h):
                act.wait_ge(S["head_row"], h + 1)
                if h >= 4:
                    act.wait_ge(S["head_psum"], h - 3)
                for j in range(J):
                    ins = s.activation(blocks(z(h % 4)[:, j, :]), wide(2 * (h % 2), P), ACT.Relu,
                                       bias=adst[:, j, h:h + 1])
                ins.then_inc(S["relu_act"], 1)

            def head_exp(h):
                act.wait_ge(S["relu_dve" if h % 2 else "relu_act"], h // 2 + 1)
                for j in range(J):
                    ins = s.activation(z(h % 4)[:, j, :], z(h % 4)[:, j, :], ACT.Exp, scale=-0.8,
                                       bias=nb02[:, j, h:h + 1])
                ins.then_inc(S["head_exp"], 1)
            head_relu(0)
            for h in range(8):
                if h % 2 and h < 7:
                    head_relu(h + 1)
                head_exp(h)
            act.wait_ge(S["hln_var"], 1)
            s.activation(s40a[:], s40a[:], ACT.Sqrt).then_inc(S["hln_std"], 1)
            act.wait_ge(S["elu_in"], 1)
            s.activation(HA, HA, ACT.Exp).then_inc(S["elu_exp"], 1)
            x2t = big[:, 3, 0:2500].rearrange("p (k n) -> p k n", k=4)
            for k in range(0, 4, 2):
                act.wait_ge(S["x2_psum"], k + 1)
                s.copy(blocks(x2t[:, k, :]), wide(0)).then_inc(S["x2_act"], 1)
            act.wait_ge(S["so_ready"], 1)
            s.activation(esrc[:, :, 0], asrc[:, :, 0], ACT.Exp, scale=-0.2).then_inc(S["esrc_ready"], 1)
            act.wait_ge(S["o_row"], 1)
            for j in range(J):
                ins = s.activation(blocks(z(0)[:, j, :]), wide(0, P), ACT.Relu, bias=adst[:, j, 0:1])
            ins.then_inc(S["relu_act"], 1)
            act.wait_ge(S["relu_act"], 5)
            for j in range(J):
                ins = s.activation(z(0)[:, j, :], z(0)[:, j, :], ACT.Exp, scale=-0.8, bias=nb02[:, j, 0:1])
            ins.then_inc(S["o_exp"], 1)
            act.wait_ge(S["hln_var"], 2)
            s.activation(std[:], veps[:], ACT.Sqrt).then_inc(S["hln_std"], 1)
            act.wait_ge(S["oelu_in"], 1)
            s.activation(XN[:], XN[:], ACT.Exp).then_inc(S["oelu_exp"], 1)

            layernorm(5)
            act.wait_ge(S["sm_in"], 2)
            s.activation(s32a[:, :, 0:8], s32a[:, :, 0:8], ACT.Exp).then_inc(S["sm_out"], 1)
            gate_rows(2, 20)
            hidden(2, ACT.Relu)

            layernorm(6)
            act.wait_ge(S["t_ready"], 4)
            s.copy(TT[:, :, 0:128], PS[0:P, 4:6, :].rearrange("p b c -> p (b c)")[:, 0:640].rearrange(
                "p (j c) -> p j c", c=128)).then_inc(S["t_act"], 1)
            act.wait_ge(S["agg_psum"], 5)
            s.activation(blocks(XT[:, 0, :]), wide(0), ACT.Identity, bias=cols[:, COL_CONV:COL_CONV + 1]
                         ).then_inc(S["h_act"], 1)

            layernorm(7)
            act.wait_ge(S["w_row_psum"], 1)
            s.copy(blocks(gateT[0:1, :]), wide(0, 1)).then_inc(S["w_row_sb"], 1)
            hidden(3, ACT.Gelu_apprx_tanh)

        @block.tensor
        def _(pe):
            mm = nc.tensor.matmul
            idn = ident[0:P, 0:P]

            def layernorm(k):
                pe.wait_ge(S["ln_rows"], J * (k + 1))
                for h in range(2):
                    for j in range(J):
                        ins = nc.tensor.transpose(wide(2 * h)[:, j, :], XN[:, j, h * 128:h * 128 + 128], idn)
                    ins.then_inc(S["xt_psum"], 1)
                pe.wait_ge(S["xt_sb"], 2 * (k + 1))

            def project(name, outs, done):
                for j in range(J):
                    for h in range(2):
                        ins = mm(outs[j], XT[:, h, j * P:j * P + P], wm(name, h), start=(h == 0), stop=(h == 1))
                ins.then_inc(done, 1)

            def spread(b, col, p, done):
                for j in range(J):
                    ins = mm(wide(b, p)[:, j, :], col(j), idn, start=True, stop=True)
                ins.then_inc(done, 1)

            pe.wait_ge(S["consts"], NCONST)
            pe.wait_ge(S["l0_in"], 64)
            layernorm(0)
            project("table", [PS[0:P, 4, 16 * j:16 * j + 14] for j in range(J)], S["table_ready"])

            def count(t, u, rows_, nodes, fresh):
                pe.wait_ge(S["onehot_ready"], t + 1)
                for m in nodes:
                    w = onehot[0:rows_, u, 1, m * P:m * P + P]
                    mm(PS[0:P, m, 0:500], w, onehot[0:rows_, u, 0, 0:500], start=m in fresh, stop=False,
                       skip_group_check=True)
                    b, c = (5, m * P) if m < 4 else (6, 0)
                    ins = mm(PS[0:P, b, c:c + P], w, onehot[0:rows_, u, 0, 500:625],
                             start=m in fresh and m in (0, 4), stop=False, skip_group_check=True)
                ins.then_inc(S["onehot_used"], 1)

            def count_all(base, tiles, rows_):
                for u in range(4):
                    count(base + u, u, rows_, range(J), range(J) if u == 0 else ())
                with pe.Fori(1, tiles // 4) as i:
                    for u in range(4):
                        count(4 * i + u + base, u, rows_, range(J), ())

            def fresh_at(t):
                return [m for m in usual_node_tiles(t) if t == 0 or m not in usual_node_tiles(t - 1) and
                        m > max(usual_node_tiles(t - 1))]

            pe.wait_ge(S["usual_ready"], 1)
            mm(PS[0:1, 7, 0:1], usual[:], ones_col[0:P, :], start=True, stop=True).then_inc(S["usual_psum"], 1)
            count_all(0, NT2, 128)
            pe.wait_ge(S["usual_known"], 1)
            flag = pe.value_load(is_usual[:], min_val=0, max_val=1)
            pe.wait_ge(S["counts_out"], 1)
            with pe.If(flag > 0):
                for m in range(J):
                    t0 = m * TILES_PER_NODE_TILE
                    for u in range(4):
                        count(NT2 + t0 + u, u, P, usual_node_tiles(t0 + u), fresh_at(t0 + u))
                    with pe.Fori(t0 // 4 + 1, t0 // 4 + TILES_PER_NODE_TILE // 4 - 1) as i:
                        for u in range(4):
                            count(4 * i + u + NT2, u, P, [m], ())
                    for u in range(4):
                        t = t0 + TILES_PER_NODE_TILE - 4 + u
                        count(NT2 + t, u, P, usual_node_tiles(t), fresh_at(t))
            with pe.Else():
                count_all(NT2, NT1, P)

            pe.wait_ge(S["counts_out"], 2)
            spread(0, lambda j: TAB[:, j, 4:5].to_broadcast([P, P]), P, S["a1_row"])
            pe.wait_ge(S["tables_split"], 1)

            def gather(i, first):
                for u in range(2):
                    t = 2 * i + u
                    pe.wait_ge(S["ids_onehot"], t + 1)
                    if not first:
                        pe.wait_ge(S["gather_read"], t - 1)
                    for q in range(4):
                        for sd in range(2):
                            for j in range(J):
                                ins = mm(PS[0:P, u, 30 * q:30 * q + 30], onehotT[:, u, sd, j, q * P:q * P + P],
                                         tab16[:, sd, j, :, :].rearrange("p a b -> p (a b)"),
                                         start=(sd == 0 and j == 0), stop=(sd == 1 and j == J - 1))
                    ins.then_inc(S["gathered"], 1)
            gather(0, True)
            with pe.Fori(1, 20) as i:
                gather(i, False)

            hTp = [blocks(PS[0:32, b, 0:500]) for b in range(8)]

            def edge_transpose(t, u, first):
                if not first:
                    pe.wait_ge(S["hT_sb"], t - 1)
                for q in range(4):
                    ins = mm(hTp[u][:, q, :], hs16[:, ds(4 * t + q, 1), :].rearrange("p a c -> p (a c)"),
                             ident16[0:P, 0:P], start=True, stop=True)
                ins.then_inc(S["hT_psum"], 1)

            def edge_up(t, u, first):
                pe.wait_ge(S["hT_sb"], t + 1)
                if not first:
                    pe.wait_ge(S["ef_act"], t - 1)
                    pe.wait_ge(S["ef_dve"], t - 1)
                for h in range(2):
                    ins = mm(PS[:, 2 + 2 * u + h, 0:500], w2s[:, 0, h * 128:h * 128 + 128], hT[:, u, :],
                             start=True, stop=True)
                ins.then_inc(S["fe_psum"], 1)

            def edge_down(t, u, first):
                pe.wait_ge(S["ef_act"], t + 1)
                pe.wait_ge(S["ef_dve"], t + 1)
                if not first:
                    pe.wait_ge(S["fn1_read"], t - 1)
                for q in range(4):
                    for h in range(2):
                        ins = mm(PS[0:P, 6 + u, 4 * q:4 * q + 4], EF[:, u, h, q * P:q * P + P], wm("fn_W1b", h),
                                 start=(h == 0), stop=(h == 1))
                ins.then_inc(S["fn1_psum"], 1)

            pe.wait_ge(S["h1_ready"], 1)
            edge_transpose(0, 0, True)

            def loop_a(i, first, last):
                for u in range(2):
                    t = 2 * i + u
                    if not (last and u == 1):
                        edge_transpose(t + 1, 1 - u, first and u == 0)
                    edge_up(t, u, first)
                    if not (first and u == 0):
                        edge_down(t - 1, 1 - u, first)
            loop_a(0, True, False)
            with pe.Fori(1, 2) as i:
                for u in range(2):
                    t = 2 * i + u
                    edge_transpose(t + 1, 1 - u, False)
                    edge_up(t, u, False)
                    edge_down(t - 1, 1 - u, u == 0)
            with pe.Fori(2, 19) as i:
                loop_a(i, False, False)
            loop_a(19, False, True)
            edge_down(39, 1, False)

            pe.wait_ge(S["h2_ready"], 1)

            def msg_transpose(g, first):
                if not first:
                    pe.wait_ge(S["hT2_sb"], g)
                for q in range(4):
                    ins = mm(hTp[5][:, q, :], hs16[:, ds(4 * g + q, 1), :].rearrange("p a c -> p (a c)"),
                             ident16[0:P, 0:P], start=True, stop=True)
                ins.then_inc(S["hT2_psum"], 1)

            def msg_up(q):
                mm(PS[0:P, 6 + q % 2, 0:257], hT[:, q // 4, (q % 4) * P:(q % 4) * P + P], w2s[:, 1, :],
                   start=True, stop=True).then_inc(S["fn2_psum"], 1)

            def msg_sum(t, q, nodes, fresh):
                pe.wait_ge(S["onehot_ready"], NT2 + NT1 + 1 + t)
                pe.wait_ge(S["msg_lo"], t + 1)
                for m in nodes:
                    for c in range(3):
                        ins = mm(PS[0:P, m, 0:257], onehot[0:P, q % 4, 1, m * P:m * P + P], msg16[:, q % 4, c, :],
                                 start=m in fresh and c == 0, stop=False, skip_group_check=True)
                ins.then_inc(S["msg_used"], 1)

            def eight(i, nodes, fresh, last):
                for q in range(8):
                    t = 8 * i + q
                    if q % 4 == 0 and not (last and q == 4):
                        msg_transpose(2 * i + q // 4 + 1, False)
                    if not (last and q >= 6):
                        if q % 4 == 2:
                            pe.wait_ge(S["hT2_sb"], 2 * i + (2 if q == 2 else 3))
                        pe.wait_ge(S["msg_ready"], t + 1)
                        msg_up((q + 2) % 8)
                    msg_sum(t, q, nodes(q), fresh(q))

            msg_transpose(0, True)
            pe.wait_ge(S["hT2_sb"], 1)
            msg_up(0)
            msg_up(1)
            with pe.If(flag > 0):
                per = TILES_PER_NODE_TILE // 8
                for m in range(J):
                    eight(per * m, lambda q: usual_node_tiles(8 * per * m + q), lambda q: fresh_at(8 * per * m + q), False)
                    with pe.Fori(per * m + 1, per * m + per - 1) as i:
                        eight(i, lambda q: [m], lambda q: (), False)
                    end = per * m + per - 1
                    eight(end, lambda q: usual_node_tiles(8 * end + q), lambda q: fresh_at(8 * end + q), m == J - 1)
            with pe.Else():
                eight(0, lambda q: range(J), lambda q: range(J) if q == 0 else (), False)
                with pe.Fori(1, 19) as i:
                    eight(i, lambda q: range(J), lambda q: (), False)
                eight(19, lambda q: range(J), lambda q: (), True)

            def gate_rows(n, done):
                pe.wait_ge(S["gates_ready"], n + 1)
                E = FFN_EXPERTS[n]
                for j in range(J):
                    ins = nc.tensor.transpose(wide(4, E)[:, j, :], gate[:, j, 0:E], idn)
                ins.then_inc(S["gt_psum"], 1)
                if n == 0:
                    pe.wait_ge(S["gt_sb"], 1)
                for e in range(16 if n == 0 else E):
                    if e >= 2:
                        pe.wait_ge(S["gr_dve" if e % 2 else "gr_act"], done // 2 + e // 2)
                    if n == 0:
                        for c0, c1 in ((0, 4), (4, 5)):
                            ins = mm(wide(2 * (e % 2))[:, c0:c1, :], pair16[:, e, :], gateT16[:, c0 * P:c1 * P],
                                     start=True, stop=True)
                        ins.then_inc(S["gr_psum"], 1)
                    else:
                        spread(2 * (e % 2), lambda j: gate[:, j, e:e + 1].to_broadcast([P, 128]), 128, S["gr_psum"])
                k = (16 if n == 0 else E) + done
                pe.wait_ge(S["gr_dve"], k // 2)
                pe.wait_ge(S["gr_act"], k // 2)
                pe.wait_ge(S["gt_sb"], n + 1)

            def ffn(n):
                base, T, E = FFN_BASE[n], FFN_TILES[n], FFN_EXPERTS[n]

                def up(i, u, first):
                    t = base + 4 * i + u
                    pe.wait_ge(w_in[u], 16 * (base // 4 + i) + 16)
                    if not first:
                        pe.wait_ge(S["h_sb"], t - 1)
                    for c0, c1 in ((0, 4), (4, 5)):
                        for h in range(2):
                            ins = mm(wide(2 * (u % 2))[:, c0:c1, :], wtile[:, u, h * 128:h * 128 + 128],
                                     XT[:, h, c0 * P:c1 * P], start=(h == 0), stop=(h == 1))
                    ins.then_inc(S["h_psum"], 1)

                src, ready = (hidg, S["h_gated"]) if n < 3 else (hid, S["h_sb"])

                def down(i, u, first):
                    t = base + 4 * i + u
                    pe.wait_ge(ready, t + 1)
                    for j in range(J):
                        ins = mm(yv(j), src[:, u % 2, j * P:j * P + P], wtile[:, u, 256:512],
                                 start=first and j % 2 == 0, stop=False, skip_group_check=True)
                    ins.then_inc(S["y_used"], 1)

                def body(i, first, last):
                    for u in range(4):
                        if u < 3:
                            up(i, u + 1, first and u == 0)
                        elif not last:
                            up(i + 1, 0, False)
                        down(i, u, first and u == 0)
                up(0, 0, True)
                body(0, True, False)
                if T > 8:
                    with pe.Fori(1, T // 4 - 1) as i:
                        body(i, False, False)
                body(T // 4 - 1, False, True)
                lhs = gateT if n < 3 else ones_row
                for j in range(J):
                    ins = mm(yv(j), lhs[0:E, j * P:j * P + P], b2[0:E, n, :], start=False, stop=True,
                             skip_group_check=True)
                ins.then_inc(S["y_ready"], 1)

            pe.wait_ge(S["rest_in"], 64)
            small = [PS[0:P, 7, 32 * j:32 * j + 32] for j in range(J)]
            layernorm(1)
            project("router", small, S["logits_ready"])
            gate_rows(0, 0)
            ffn(0)

            pe.wait_ge(S["b_ready"], 1)
            b1 = big[0:P, 2, :].rearrange("p (j n) -> p j n", j=J)
            for i in range(10):
                src = b1 if i < 5 else C2
                if i >= 2:
                    pe.wait_ge(S["bt_dve" if i % 2 else "bt_act"], i // 2)
                for j in range(J):
                    ins = nc.tensor.transpose(wide(2 * (i % 2), P)[:, j, :], src[:, j, (i % 5) * P:(i % 5) * P + P], idn)
                ins.then_inc(S["bt_psum"], 1)
            pe.wait_ge(S["bt_dve"], 5)
            pe.wait_ge(S["bt_act"], 5)
            layernorm(2)

            def aggregate(h, width, done):
                for c0, c1 in ((0, 4), (4, 5)):
                    for i in range(J):
                        ins = mm(wide(2 * h)[:, c0:c1, :], TT[:, i, h * 128:h * 128 + 128], AH[:, i, c0 * P:c1 * P],
                                 start=(i == 0), stop=(i == J - 1))
                ins.then_inc(done, 1)

            for l in range(3):
                if l > 0:
                    pe.wait_ge(S["h_act"], l)
                    pe.wait_ge(S["h_dve"], l)
                for j in range(J):
                    for h in range(2):
                        o = W_AT["gcn_W"][0] + l * D
                        ins = mm(yv(j), XT[:, h, j * P:j * P + P], wmat[:, h, o:o + D], start=(h == 0), stop=(h == 1))
                ins.then_inc(S["t_ready"], 1)
                pe.wait_ge(S["t_act"], l + 1)
                pe.wait_ge(S["t_dve"], l + 1)
                if l < 2:
                    for h in range(2):
                        aggregate(h, 256, S["agg_psum"])
                else:
                    for j in range(J):
                        for i in range(J):
                            ins = mm(yv(j), AH[:, i, j * P:j * P + P], TT[:, i, :], start=(i == 0), stop=(i == J - 1))
                    ins.then_inc(S["last_psum"], 1)

            def z(b):
                return big[0:P, b, :].rearrange("p (j n) -> p j n", j=J)

            layernorm(3)
            project("W_gat", [v[:, 0:16] for v in small], S["gat_h"])
            pe.wait_ge(S["gat_a"], 1)
            for h in range(4):
                if h >= 2:
                    pe.wait_ge(S["row_read"], h - 1)
                spread(2 * (h % 2), lambda j: asrc[:, j, h:h + 1].to_broadcast([P, P]), P, S["row_psum"])
            pe.wait_ge(S["gat_a"], 2)

            def two_rows(h):
                if h:
                    pe.wait_ge(S["gat_sum"], h)
                spread(0, lambda j: adst[:, j, h:h + 1].to_broadcast([P, P]), P, S["rows2_psum"])
                if h:
                    pe.wait_ge(S["gat_sub"], h)
                spread(2, lambda j: bmax[:, j, h:h + 1].to_broadcast([P, P]), P, S["rows2_psum"])
            two_rows(0)
            for h in range(4):
                if h < 3:
                    two_rows(h + 1)
                pe.wait_ge(S["gat_mul"], h + 1)
                for i in range(J):
                    for j in range(J):
                        ins = mm(PS[0:P, 7, (i * 4 + h) * 5:(i * 4 + h) * 5 + 5], z(h)[:, j, i * P:i * P + P],
                                 hx[:, j, h, :], start=(j == 0), stop=(j == J - 1))
                ins.then_inc(S["gat_mm"], 1)
            gate_rows(1, 16)
            ffn(1)

            layernorm(4)
            project("W_heads", [PS[0:P, 3 + j, :] for j in range(J)], S["hh_psum"])
            pe.wait_ge(S["s_ready"], 1)

            def head_row(h):
                if h >= 2:
                    pe.wait_ge(S["relu_dve" if h % 2 else "relu_act"], h // 2)
                spread(2 * (h % 2), lambda j: asrc[:, j, h:h + 1].to_broadcast([P, P]), P, S["head_row"])
            head_row(0)
            head_row(1)
            for h in range(8):
                if h < 6:
                    head_row(h + 2)
                pe.wait_ge(S["head_mul"], h + 1)
                if h >= 2:
                    pe.wait_ge(S["head_out"], h - 1)
                for i in range(J):
                    for j in range(J):
                        ins = mm(PS[0:P, 4 + h % 2, i * 64:i * 64 + 64], z(h % 4)[:, j, i * P:i * P + P],
                                 HA[:, j, h * 64:h * 64 + 64], start=(j == 0), stop=(j == J - 1))
                ins.then_inc(S["head_psum"], 1)
            pe.wait_ge(S["x2_ready"], 1)
            x2t = big[:, 3, 0:2500].rearrange("p (k n) -> p k n", k=4)
            for k in range(4):
                if k >= 2:
                    pe.wait_ge(S["x2_dve" if k % 2 else "x2_act"], k // 2)
                for j in range(J):
                    ins = nc.tensor.transpose(wide(2 * (k % 2))[:, j, :], HB_[:, j, k * 128:k * 128 + 128], idn)
                ins.then_inc(S["x2_psum"], 1)
            pe.wait_ge(S["x2_act"], 2)
            pe.wait_ge(S["x2_dve"], 2)
            for j in range(J):
                for k in range(4):
                    ins = mm(yv(j), x2t[:, k, j * P:j * P + P], wout[:, k, :], start=(k == 0), stop=(k == 3))
            ins.then_inc(S["ho_psum"], 1)
            pe.wait_ge(S["so_ready"], 1)
            spread(0, lambda j: asrc[:, j, 0:1].to_broadcast([P, P]), P, S["o_row"])
            pe.wait_ge(S["o_mul"], 1)
            for i in range(J):
                for j in range(J):
                    ins = mm(yv(i), z(0)[:, j, i * P:i * P + P], TT[:, j, :], start=(j == 0), stop=(j == J - 1))
            ins.then_inc(S["o_psum"], 1)

            layernorm(5)
            project("Wg", [v[:, 0:8] for v in small], S["logits_ready"])
            gate_rows(2, 20)
            ffn(2)

            layernorm(6)
            tps = PS[0:P, 4:6, :].rearrange("p b c -> p (b c)")
            project("W_conv", [tps[:, 128 * j:128 * j + 128] for j in range(J)], S["t_ready"])
            pe.wait_ge(S["t_act"], 4)
            aggregate(0, 128, S["agg_psum"])
            pe.wait_ge(S["h_act"], 3)
            for j in range(J):
                ins = mm(yv(j), XT[:, 0, j * P:j * P + P], wlin[:], start=True, stop=True)
            ins.then_inc(S["last_psum"], 1)

            layernorm(7)
            project("wr", [PS[0:P, 7, j:j + 1] for j in range(J)], S["logits_ready"])
            pe.wait_ge(S["w_col"], 1)
            for j in range(J):
                ins = nc.tensor.transpose(wide(0, 1)[:, j, :], s5a[:, j:j + 1], idn)
            ins.then_inc(S["w_row_psum"], 1)
            pe.wait_ge(S["w_row_sb"], 1)
            ffn(3)

        @block.vector
        def _(dve):
            v = nc.vector
            step = [0]

            def link(ins):
                step[0] += 1
                ins.then_inc(S["vector_step"], 1)
                dve.wait_ge(S["vector_step"], step[0])

            def split(parts, x, rest):
                link(v.tensor_copy(parts[0], x))
                link(v.tensor_tensor(rest, x, parts[0], ALU.subtract))
                link(v.tensor_copy(parts[1], rest))
                link(v.tensor_tensor(parts[2], rest, parts[1], ALU.subtract))

            def moments(src):
                for j in range(J):
                    ins = v.bn_stats(stats[:, j, :], src(j))
                link(ins)
                for j in range(J):
                    ins = v.bn_aggr(mv[:, j, :], stats[:, j, :])
                link(ins)

            def layernorm(k):
                moments(lambda j: X[:, j, :])
                v.tensor_scalar_add(veps[:], mv[:, :, 1], EPS).then_inc(S["var_ready"], 1)
                dve.wait_ge(S["std_ready"], k + 1)
                link(v.reciprocal(rstd[:], std[:]))
                for j in range(J):
                    ins = v.tensor_scalar(XN[:, j, :], X[:, j, :], mv[:, j, 0:1], rstd[:, j:j + 1], ALU.subtract,
                                          ALU.mult)
                    ins.then_inc(S["ln_rows"], 1)
                dve.wait_ge(S["xt_psum"], 2 * k + 2)
                v.tensor_copy(blocks(XT[:, 1, :]), wide(2)).then_inc(S["xt_sb"], 1)

            dve.wait_ge(S["consts"], NCONST)
            dve.wait_ge(S["x_in"], 16)
            layernorm(0)

            dve.wait_ge(S["l0_in"], 64)
            v.tensor_scalar_add(foldS, row("v"), EPS).then_inc(S["fold_var"], 1)
            dve.wait_ge(S["fold_std"], 1)
            link(v.reciprocal(foldS, foldS))
            link(v.tensor_tensor(foldS, foldS, row("g"), ALU.mult))
            link(v.tensor_tensor(foldT, row("b"), row("m"), ALU.subtract))
            link(v.tensor_tensor(foldT, foldT, foldS, ALU.mult))
            link(v.tensor_tensor(foldT, foldT, row("be"), ALU.add))
            for n, o in ((0, 4), (1, 264)):
                link(v.tensor_tensor(w2v[:, n, 0:D], w2rows[:, n, :], foldS[0:32, o:o + D], ALU.mult))
                link(v.scalar_tensor_tensor(out=w2v[:, n, 0:D], in0=foldT[0:32, o:o + D], scalar=part[:, 3:4],
                                            in1=w2v[:, n, 0:D], op0=ALU.mult, op1=ALU.add))
                link(v.tensor_copy(w2v[:, n, D:D + 1], part[:, 3:4]))
            link(v.tensor_copy(w2h, w2v))
            link(v.tensor_tensor(w2r, w2v, w2h, ALU.subtract))
            link(v.tensor_copy(w2m, w2r))
            link(v.tensor_tensor(w2r, w2r, w2m, ALU.subtract))
            link(v.tensor_scalar(w2r, w2r, part[:, 2:3], None, ALU.mult))
            link(v.scalar_tensor_tensor(out=w2r, in0=w2m, scalar=part[:, 1:2], in1=w2r, op0=ALU.mult,
                                        op1=ALU.add))
            link(v.scalar_tensor_tensor(out=w2s[:], in0=w2h, scalar=part[:, 0:1], in1=w2r, op0=ALU.mult,
                                        op1=ALU.add))
            dve.wait_ge(S["table_ready"], 1)
            link(v.tensor_copy(TAB[:], PS[0:P, 4, 0:80].rearrange("p (j c) -> p j c", c=16)[:, :, 0:14]))

            dve.wait_ge(S["idx_in"], 48)
            link(v.tensor_copy(id1[:], idx1))
            link(v.tensor_tensor(inside, id1[:, 1, :], bounds[:, 0, :], ALU.is_ge))
            link(v.tensor_tensor(inside2, id1[:, 1, :], bounds[:, 1, :], ALU.is_lt))
            link(v.tensor_tensor(inside, inside, inside2, ALU.mult))
            v.tensor_reduce(usual[:], inside, AX, ALU.min).then_inc(S["usual_ready"], 1)
            dve.wait_ge(S["usual_psum"], 1)
            v.tensor_scalar(is_usual[:], PS[0:1, 7, 0:1], P - 0.5, None, ALU.is_gt).then_inc(S["usual_known"], 1)
            link(v.tensor_copy(id2[:, 1, :], idx2[:, 1, :]))
            link(v.tensor_scalar(id2[:, 0, :], idx2[:, 0, :], float(N - 1), None, ALU.min))

            def onehots(ids, t, u, rows_, sides, wait):
                if wait is not None:
                    dve.wait_ge(S["onehot_used"], wait)
                for sd in sides:
                    ins = v.tensor_scalar(onehot[0:rows_, u, sd, 0:N], node_iota[0:rows_, :], ids[0:rows_, sd, ds(t, 1)],
                                          None, ALU.is_equal)
                ins.then_inc(S["onehot_ready"], 1)
            for u in range(4):
                onehots(id2, u, u, 128, (0, 1), None)
            with dve.Fori(1, NT2 // 4) as i:
                for u in range(4):
                    onehots(id2, 4 * i + u, u, 128, (0, 1), 4 * i + u - 3)
            with dve.Fori(0, NT1 // 4) as i:
                for u in range(4):
                    onehots(id1, 4 * i + u, u, P, (0, 1), 4 * i + u + NT2 - 3)

            def z(b):
                return big[0:P, b, :].rearrange("p (j n) -> p j n", j=J)

            dve.wait_ge(S["counts_out"], 2)
            link(v.tensor_scalar(z(0), C1[:], 0.0, ABSENT, ALU.is_equal, ALU.mult))
            dve.wait_ge(S["a1_row"], 1)

            def masked_max(dst, mask, scratch, scores):
                for j in range(J):
                    ins = v.tensor_tensor_reduce(out=blocks(scratch[:, j, :]), in0=blocks(mask[:, j, :]), in1=scores,
                                                 scale=1.0, scalar=-3e38, op0=ALU.add, op1=ALU.max, accum_out=dst[j])
                return ins
            link(masked_max([s5a[:, j:j + 1] for j in range(J)], z(0), z(1), wide(0, P)))
            link(v.tensor_tensor(s5a[:], s5a[:], TAB[:, :, 13], ALU.add))
            link(v.scalar_tensor_tensor(out=tabf[:, 1, :, 9], in0=s5a[:], scalar=0.2, in1=s5a[:], op0=ALU.mult,
                                        op1=ALU.max))
            link(v.tensor_copy(tabf[:, 0, :, 0:9], TAB[:, :, 0:9]))
            link(v.tensor_copy(tabf[:, 1, :, 0:5], TAB[:, :, 9:14]))
            split([tab16[:, :, :, :, c] for c in range(3)], tabf[:], tabr[:])
            v.tensor_copy(s5b[:], s5a[:]).then_inc(S["tables_split"], 1)
            dve.wait_ge(S["tables_split"], 1)
            v.tensor_copy(s5b[:], s5a[:]).then_inc(S["edge_max_ready"], 1)

            def ids_onehot(t, u, first):
                dve.wait_ge(S["rows_cast"], t + 1)
                if not first:
                    dve.wait_ge(S["gathered"], t - 1)
                for sd in range(2):
                    for j in range(J):
                        ins = v.tensor_scalar(onehotT[:, u, sd, j, :], idxrow16[:, u, 500 * sd:500 * sd + 500],
                                              node_id[0:P, j:j + 1], None, ALU.is_equal)
                ins.then_inc(S["ids_onehot"], 1)

            def add_parts(t, u):
                dve.wait_ge(S["gathered"], t + 1)
                v.tensor_reduce(GS[:, ds(4 * t, 4), :], PS[0:P, u, 0:120].rearrange("p (q a b) -> p q a b", q=4, b=3),
                                AX, ALU.add).then_inc(S["gather_read"], 1)

            def gathers(i, first):
                for u in range(2):
                    ids_onehot(2 * i + u, u, first)
                    if not (first and u == 0):
                        add_parts(2 * i + u - 1, 1 - u)
            gathers(0, True)
            with dve.Fori(1, 20) as i:
                gathers(i, False)
            add_parts(39, 1)
            dve.wait_ge(S["gather_read"], 40)

            link(v.scalar_tensor_tensor(out=EX, in0=GS[:, :, 4], scalar=0.2, in1=GS[:, :, 4], op0=ALU.mult,
                                        op1=ALU.max))
            link(v.tensor_tensor(EX, EX, GS[:, :, 9], ALU.subtract))
            v.tensor_copy(s5b[:], s5a[:]).then_inc(S["logit_in"], 1)

            def stack(h, pre, o):
                link(v.tensor_tensor(h, pre, mid_b(foldS[0:P, o:o + 4], NT1), ALU.mult))
                link(v.tensor_tensor(h, h, mid_b(foldT[0:P, o:o + 4], NT1), ALU.add))
                link(v.scalar_tensor_tensor(out=h, in0=h, scalar=0.01, in1=h, op0=ALU.mult, op1=ALU.max))
                for c in range(3):
                    ins = v.tensor_copy(hs16[:, :, 4 * c:4 * c + 4], h)
                link(ins)
                link(v.tensor_tensor(h, h, hs16[:, :, 0:4], ALU.subtract))
                for c in range(3, 5):
                    ins = v.tensor_copy(hs16[:, :, 4 * c:4 * c + 4], h)
                link(ins)
                return v.tensor_tensor(hs16[:, :, 20:24], h, hs16[:, :, 12:16], ALU.subtract)
            stack(h1, GS[:, :, 0:4], 0).then_inc(S["h1_ready"], 1)

            def edge_relu(t, u):
                dve.wait_ge(S["fe_psum"], t + 1)
                v.tensor_scalar(EF[:, u, 1, :], PS[:, 3 + 2 * u, 0:500], 0.0, None, ALU.max).then_inc(S["ef_dve"], 1)

            def edge_add(t, u):
                dve.wait_ge(S["fn1_psum"], t + 1)
                v.tensor_tensor(FR[:, ds(4 * t, 4), :], PS[0:P, 6 + u, 0:16].rearrange("p (q c) -> p q c", q=4),
                                GS[:, ds(4 * t, 4), 5:9], ALU.add).then_inc(S["fn1_read"], 1)

            def loop_a(i, first):
                for u in range(2):
                    edge_relu(2 * i + u, u)
                    if not (first and u == 0):
                        edge_add(2 * i + u - 1, 1 - u)
            loop_a(0, True)
            with dve.Fori(1, 20) as i:
                loop_a(i, False)
            edge_add(39, 1)
            dve.wait_ge(S["fn1_read"], 40)
            stack(h2, FR, 260).then_inc(S["h2_ready"], 1)
            dve.wait_ge(S["edge_exp"], 1)

            def message(i, q, first):
                t = 8 * i + q
                onehots(id1, t, q % 4, P, (1,), None if first and q < 4 else NT2 + NT1)
                dve.wait_ge(S["fn2_psum"], t + 1)
                v.tensor_scalar(msg[:, q % 4, :], PS[0:P, 6 + q % 2, 0:257], 0.0, EX[:, ds(t, 1)], ALU.max,
                                ALU.mult).then_inc(S["msg_ready"], 1)

            def loop_m(i, first):
                for q in range(8):
                    if not (first and q < 4):
                        dve.wait_ge(S["msg_used"], 8 * i + q - 3)
                    else:
                        dve.wait_ge(S["onehot_used"], NT2 + NT1)
                    message(i, q, first)
            loop_m(0, True)
            with dve.Fori(1, 20) as i:
                loop_m(i, False)
            dve.wait_ge(S["msg_used"], NT1)
            for j in range(J):
                link(v.tensor_scalar(s5a[:, j:j + 1], PS[0:P, j, 256:257], 0.5, None, ALU.max))
            link(v.reciprocal(s5a[:], s5a[:]))
            for j in range(J):
                ins = v.scalar_tensor_tensor(out=XN[:, j, :], in0=PS[0:P, j, 0:D], scalar=s5a[:, j:j + 1],
                                             in1=XN[:, j, :], op0=ALU.mult, op1=ALU.add)
            link(ins)
            link(v.tensor_tensor(X[:], X[:], XN[:], ALU.add))

            def gate_rows(n, done):
                v.tensor_copy(s5b[:], s5a[:]).then_inc(S["gates_ready"], 1)
                E = FFN_EXPERTS[n]
                tiles = 16 if n == 0 else E
                dst = grow16 if n == 0 else grow
                dve.wait_ge(S["gt_psum"], n + 1)
                if n == 0:
                    v.tensor_copy(blocks(gateT16), wide(4, E))
                    v.tensor_copy(pair16.rearrange("p e (a b) -> p (e a) b", a=2), last_b(ident[0:32, 0:32], 64))
                v.tensor_copy(blocks(gateT[0:E, :]), wide(4, E)).then_inc(S["gt_sb"], 1)
                for e in range(1, tiles, 2):
                    dve.wait_ge(S["gr_psum"], done + e + 1)
                    v.tensor_copy(blocks(dst[:, e, :]), wide(2)).then_inc(S["gr_dve"], 1)
                dve.wait_ge(S["gr_dve"], (done + tiles) // 2)
                dve.wait_ge(S["gr_act"], (done + tiles) // 2)

            def gating(n):
                base, T = FFN_BASE[n], FFN_TILES[n]

                def body(i, first):
                    for u in range(4):
                        t = base + 4 * i + u
                        dve.wait_ge(S["h_sb"], t + 1)
                        if not (first and u < 2):
                            dve.wait_ge(S["y_used"], t - 1)
                        g = grow16[:, ds(4 * i + u, 1), :] if n == 0 else grow[:, ds(i, 1), :]
                        v.tensor_tensor(hidg[:, u % 2, :], hid[:, u % 2, :], g.rearrange("p a n -> p (a n)"), ALU.mult
                                        ).then_inc(S["h_gated"], 1)
                body(0, True)
                with dve.Fori(1, T // 4) as i:
                    body(i, False)
                dve.wait_ge(S["y_ready"], n + 1)

            def add_y():
                for j in range(J):
                    ins = v.tensor_tensor(X[:, j, :], X[:, j, :], yv(j), ALU.add)
                link(ins)

            def top_two(E, before, k):
                sc = s32a[:, :, 0:E]
                s3 = s320a[:, :, 0:E * E].rearrange("p j (e f) -> p j e f", e=E)
                s4 = s320b[:, :, 0:E * E].rearrange("p j (e f) -> p j e f", e=E)
                other = sc.unsqueeze(2).to_broadcast([P, J, E, E])
                own = sc.unsqueeze(3).to_broadcast([P, J, E, E])
                link(v.tensor_tensor(s3, other, own, ALU.is_equal))
                link(v.tensor_tensor(s3, s3, before[:].unsqueeze(1).to_broadcast([P, J, E, E]), ALU.mult))
                link(v.tensor_tensor(s4, other, own, ALU.is_gt))
                link(v.tensor_tensor(s3, s3, s4, ALU.add))
                rank = s32b[:, :, 0:E]
                link(v.tensor_reduce(rank, s3, AX, ALU.add))
                link(v.tensor_reduce(s5a[:], sc, AX, ALU.max))
                link(v.tensor_scalar(rank, rank, 1.5, None, ALU.is_lt))
                link(v.tensor_tensor(sc, sc, last_b(s5a[:], E), ALU.subtract))
                v.tensor_copy(s5b[:], s5a[:]).then_inc(S["sm_in"], 1)
                dve.wait_ge(S["sm_out"], k)
                link(v.tensor_tensor(sc, sc, rank, ALU.mult))
                link(v.tensor_reduce(s5a[:], sc, AX, ALU.add))
                link(v.reciprocal(s5a[:], s5a[:]))
                link(v.tensor_tensor(gate[:, :, 0:E], sc, last_b(s5a[:], E), ALU.mult))

            layernorm(1)
            small = PS[0:P, 7, 0:160].rearrange("p (j c) -> p j c", c=32)
            dve.wait_ge(S["logits_ready"], 1)
            link(v.tensor_tensor(s32a[:], small, mid_b(row("router_b"), J), ALU.add))
            link(v.tensor_reduce(s5a[:], s32a[:], AX, ALU.max))
            link(v.tensor_tensor(s32b[:], s32a[:], last_b(s5a[:], 32), ALU.is_equal))
            link(v.tensor_tensor(s32b[:], s32b[:], mid_b(rev32[:], J), ALU.mult))
            link(v.tensor_reduce(s5a[:], s32b[:], AX, ALU.max))
            link(v.tensor_tensor(gate[:], s32b[:], last_b(s5a[:], 32), ALU.is_equal))
            gate_rows(0, 0)
            gating(0)
            for j in range(J):
                ins = v.scalar_tensor_tensor(out=X[:, j, :], in0=yv(j), scalar=0.0, in1=X[:, j, :], op0=ALU.max,
                                             op1=ALU.add)
            link(ins)

            link(v.tensor_reduce(dinv[:], C1[:], AX, ALU.add))
            v.tensor_scalar_add(dinv[:], dinv[:], 1.0).then_inc(S["deg_ready"], 1)
            dve.wait_ge(S["deg_std"], 1)
            link(v.reciprocal(dinv[:], dinv[:]))
            for j in range(J):
                ins = v.tensor_scalar(z(2)[:, j, :], C1[:, j, :], dinv[:, j:j + 1], None, ALU.mult)
            link(ins)
            for j in range(J):
                dg = slice(j * P, j * P + P)
                v.scalar_tensor_tensor(out=z(2)[:, j, dg], in0=ident[0:P, 0:P], scalar=dinv[:, j:j + 1],
                                       in1=z(2)[:, j, dg], op0=ALU.mult, op1=ALU.add)
                ins = v.tensor_tensor(C2[:, j, dg], C2[:, j, dg], ident[0:P, 0:P], ALU.add)
            ins.then_inc(S["b_ready"], 1)
            for i in range(1, 10, 2):
                dve.wait_ge(S["bt_psum"], i + 1)
                if i < 5:
                    v.tensor_scalar(blocks(AH[:, i, :]), wide(2, P), dinv[:, i:i + 1], None, ALU.mult
                                    ).then_inc(S["bt_dve"], 1)
                else:
                    v.tensor_copy(blocks(C2T[:, i - 5, :]), wide(2, P)).then_inc(S["bt_dve"], 1)
            layernorm(2)
            tps = PS[0:P, 4:7, :].rearrange("p b c -> p (b c)")
            for l in range(3):
                dve.wait_ge(S["t_ready"], l + 1)
                v.tensor_copy(TT[:, 2:5, :], tps[:, 512:1280].rearrange("p (j c) -> p j c", c=D)
                              ).then_inc(S["t_dve"], 1)
                if l < 2:
                    dve.wait_ge(S["agg_psum"], 2 * l + 2)
                    v.tensor_scalar(blocks(XT[:, 1, :]), wide(2), cols[:, COL_GCN + 2 * l + 1:COL_GCN + 2 * l + 2],
                                    0.0, ALU.add, ALU.max).then_inc(S["h_dve"], 1)
            dve.wait_ge(S["last_psum"], 1)
            for j in range(J):
                ins = v.tensor_tensor(XN[:, j, :], yv(j), row("gcn_b2"), ALU.add)
            link(ins)
            link(v.scalar_tensor_tensor(out=X[:], in0=XN[:], scalar=0.0, in1=X[:], op0=ALU.max, op1=ALU.add))

            layernorm(3)
            dve.wait_ge(S["gat_h"], 1)
            link(v.tensor_copy(hx[:, :, :, 0:4], small[:, :, 0:16].rearrange("p j (h e) -> p j h e", h=4)))
            for name, dst in (("att_src", asrc), ("att_dst", adst)):
                link(v.tensor_tensor(s32a[:, :, 0:16], small[:, :, 0:16], mid_b(row(name), J), ALU.mult))
                link(v.tensor_reduce(dst[:, :, 0:4], s32a[:, :, 0:16].rearrange("p j (h e) -> p j h e", h=4), AX,
                                     ALU.add))
            v.tensor_copy(s5b[:], s5a[:]).then_inc(S["gat_a"], 1)
            link(v.tensor_scalar(z(2), C2[:], 0.0, ABSENT, ALU.is_equal, ALU.mult))
            for h in range(4):
                dve.wait_ge(S["row_psum"], h + 1)
                masked_max([mx[:, j, h:h + 1] for j in range(J)], z(2), z(3), wide(2 * (h % 2), P)
                           ).then_inc(S["row_read"], 1)
                dve.wait_ge(S["row_read"], h + 1)
            link(v.tensor_tensor(mx[:], mx[:], adst[:, :, 0:4], ALU.add))
            link(v.scalar_tensor_tensor(out=mx[:], in0=mx[:], scalar=0.2, in1=mx[:], op0=ALU.mult, op1=ALU.max))
            link(v.tensor_scalar(pa02[:], asrc[:, :, 0:4], 0.2, None, ALU.mult))
            v.scalar_tensor_tensor(out=bmax[:], in0=adst[:, :, 0:4], scalar=0.2, in1=mx[:], op0=ALU.mult,
                                   op1=ALU.subtract).then_inc(S["gat_a"], 1)

            def sub_max(h):
                dve.wait_ge(S["rows2_psum"], 2 * h + 2)
                dve.wait_ge(S["gat_sum"], h + 1)
                for j in range(J):
                    zj = blocks(z(h)[:, j, :])
                    ins = v.scalar_tensor_tensor(out=zj, in0=zj, scalar=0.8, in1=wide(2, P), op0=ALU.mult,
                                                 op1=ALU.add)
                ins.then_inc(S["gat_sub"], 1)

            sub_max(0)
            for h in range(4):
                if h < 3:
                    sub_max(h + 1)
                dve.wait_ge(S["gat_exp"], h + 1)
                v.tensor_tensor(z(h), z(h), C2T[:], ALU.mult).then_inc(S["gat_mul"], 1)
            dve.wait_ge(S["gat_mm"], 4)
            agg = PS[0:P, 7, 0:100].rearrange("p (i c) -> p i c", c=5)
            den = s40a[:, 0:20]
            g16 = s320a[:, :, 0:16]
            g20 = g16.rearrange("p j (h e) -> p j h e", h=4)
            link(v.tensor_scalar(den, agg[:, :, 4], 1e-16, None, ALU.add))
            link(v.reciprocal(den, den))
            link(v.tensor_tensor(g20, PS[0:P, 7, 0:100].rearrange("p (j h c) -> p j h c", j=J, c=5)[:, :, :, 0:4],
                                 den.rearrange("p (j h) -> p j h", j=J).unsqueeze(3).to_broadcast([P, J, 4, 4]),
                                 ALU.mult))
            link(v.tensor_tensor(g16, g16, mid_b(row("b_gat"), J), ALU.add))
            moments(lambda j: s320a[:, j, 0:16])
            v.tensor_scalar_add(s5a[:], mv[:, :, 1], EPS).then_inc(S["gat_var"], 1)
            dve.wait_ge(S["gat_std"], 1)
            link(v.reciprocal(s5a[:], s5a[:]))
            for j in range(J):
                ins = v.tensor_scalar(s320a[:, j, 0:16], s320a[:, j, 0:16], mv[:, j, 0:1], s5a[:, j:j + 1],
                                      ALU.subtract, ALU.mult)
            link(ins)
            link(v.tensor_tensor(g16, g16, mid_b(row("ln_gamma"), J), ALU.mult))
            link(v.tensor_tensor(g16, g16, mid_b(row("ln_beta"), J), ALU.add))
            link(v.tensor_reduce(s32a[:, :, 0:4], g16.rearrange("p j (h e) -> p j e h", h=4), AX, ALU.add))
            link(v.tensor_scalar(s32a[:, :, 0:4], s32a[:, :, 0:4], 0.25, None, ALU.mult))
            top_two(4, before4, 1)
            gate_rows(1, 16)
            gating(1)
            add_y()

            layernorm(4)
            dve.wait_ge(S["hh_psum"], 1)
            for j in range(J):
                ins = v.tensor_tensor(HA[:, j, :], PS[0:P, 3 + j, :], row("b_heads"), ALU.add)
            link(ins)
            tmp = z(2).rearrange("p j n -> p (j n)")[:, 0:J * 512].rearrange("p (j n) -> p j n", j=J)
            for name, dst in (("a_src", asrc), ("a_dst", adst)):
                link(v.tensor_tensor(tmp, HA, mid_b(row(name), J), ALU.mult))
                link(v.tensor_reduce(dst[:], tmp.rearrange("p j (h e) -> p j h e", h=8), AX, ALU.add))
            v.tensor_scalar(nb02[:], adst[:], -0.2, None, ALU.mult).then_inc(S["s_ready"], 1)

            dve.wait_ge(S["esrc_ready"], 1)

            def head_out(h):
                dve.wait_ge(S["head_psum"], h + 1)
                v.tensor_tensor(HB_[:, :, h * 64:h * 64 + 64], PS[0:P, 4 + h % 2, 0:320].rearrange(
                    "p (i c) -> p i c", c=64), last_b(esrc[:, :, h], 64), ALU.mult).then_inc(S["head_out"], 1)

            def head_relu(h):
                dve.wait_ge(S["head_row"], h + 1)
                if h >= 4:
                    dve.wait_ge(S["head_psum"], h - 3)
                for j in range(J):
                    ins = v.tensor_scalar(blocks(z(h % 4)[:, j, :]), wide(2, P), adst[:, j, h:h + 1], 0.0, ALU.add,
                                          ALU.max)
                ins.then_inc(S["relu_dve"], 1)
            for h in range(8):
                if h % 2 == 0:
                    head_relu(h + 1)
                dve.wait_ge(S["head_exp"], h + 1)
                v.tensor_tensor(z(h % 4), z(h % 4), C1[:], ALU.mult).then_inc(S["head_mul"], 1)
                if h >= 1:
                    head_out(h - 1)
            head_out(7)
            dve.wait_ge(S["head_out"], 8)
            hp = HB_.rearrange("p j (h e) -> p (j h) e", h=8)
            hq = HA.rearrange("p j (h e) -> p (j h) e", h=8)
            link(v.tensor_reduce(s40a[:], hp, AX, ALU.add))
            link(v.tensor_scalar(s40a[:], s40a[:], 1.0 / 64, None, ALU.mult))
            link(v.tensor_tensor(hp, hp, last_b(s40a[:], 64), ALU.subtract))
            link(v.tensor_tensor(hq, hp, hp, ALU.mult))
            link(v.tensor_reduce(s40a[:], hq, AX, ALU.add))
            v.tensor_scalar(s40a[:], s40a[:], 1.0 / 64, EPS, ALU.mult, ALU.add).then_inc(S["hln_var"], 1)
            dve.wait_ge(S["hln_std"], 1)
            link(v.reciprocal(s40a[:], s40a[:]))
            link(v.tensor_tensor(hp, hp, last_b(s40a[:], 64), ALU.mult))
            link(v.tensor_tensor(HB_, HB_, mid_b(row("g_heads"), J), ALU.mult))
            link(v.tensor_tensor(HB_, HB_, mid_b(row("beta_heads"), J), ALU.add))
            v.tensor_scalar(HA, HB_, 0.0, None, ALU.min).then_inc(S["elu_in"], 1)
            dve.wait_ge(S["elu_in"], 1)
            dve.wait_ge(S["elu_exp"], 1)
            link(v.tensor_scalar(HA, HA, -1.0, None, ALU.add))
            v.scalar_tensor_tensor(out=HB_, in0=HB_, scalar=0.0, in1=HA, op0=ALU.max, op1=ALU.add
                                   ).then_inc(S["x2_ready"], 1)
            x2t = big[:, 3, 0:2500].rearrange("p (k n) -> p k n", k=4)
            for k in range(1, 4, 2):
                dve.wait_ge(S["x2_psum"], k + 1)
                v.tensor_copy(blocks(x2t[:, k, :]), wide(2)).then_inc(S["x2_dve"], 1)
            dve.wait_ge(S["ho_psum"], 1)
            for j in range(J):
                ins = v.tensor_tensor(TT[:, j, :], yv(j), row("b_out"), ALU.add)
            link(ins)
            for name, dst in (("a_out_src", asrc), ("a_out_dst", adst)):
                link(v.tensor_tensor(XN[:], TT[:], mid_b(row(name), J), ALU.mult))
                link(v.tensor_reduce(dst[:, :, 0], XN[:], AX, ALU.add))
            v.tensor_scalar(nb02[:, :, 0], adst[:, :, 0], -0.2, None, ALU.mult).then_inc(S["so_ready"], 1)
            dve.wait_ge(S["o_exp"], 1)
            v.tensor_tensor(z(0), z(0), C1[:], ALU.mult).then_inc(S["o_mul"], 1)
            dve.wait_ge(S["o_psum"], 1)
            dve.wait_ge(S["esrc_ready"], 2)
            for j in range(J):
                ins = v.tensor_scalar(TT[:, j, :], yv(j), esrc[:, j, 0:1], None, ALU.mult)
            link(ins)
            moments(lambda j: TT[:, j, :])
            v.tensor_scalar_add(veps[:], mv[:, :, 1], EPS).then_inc(S["hln_var"], 1)
            dve.wait_ge(S["hln_std"], 2)
            link(v.reciprocal(rstd[:], std[:]))
            for j in range(J):
                ins = v.tensor_scalar(TT[:, j, :], TT[:, j, :], mv[:, j, 0:1], rstd[:, j:j + 1], ALU.subtract, ALU.mult)
            link(ins)
            link(v.tensor_tensor(TT[:], TT[:], mid_b(row("g_out"), J), ALU.mult))
            link(v.tensor_tensor(TT[:], TT[:], mid_b(row("beta_out"), J), ALU.add))
            v.tensor_scalar(XN[:], TT[:], 0.0, None, ALU.min).then_inc(S["oelu_in"], 1)
            dve.wait_ge(S["oelu_exp"], 1)
            link(v.tensor_scalar(XN[:], XN[:], -1.0, None, ALU.add))
            link(v.scalar_tensor_tensor(out=XN[:], in0=TT[:], scalar=0.0, in1=XN[:], op0=ALU.max, op1=ALU.add))
            link(v.tensor_tensor(X[:], X[:], XN[:], ALU.add))

            layernorm(5)
            dve.wait_ge(S["logits_ready"], 2)
            link(v.tensor_tensor(s32a[:, :, 0:8], small[:, :, 0:8], mid_b(row("bg"), J), ALU.add))
            link(v.tensor_tensor(s32a[:, :, 0:8], s32a[:, :, 0:8], mid_b(row("bias"), J), ALU.add))
            top_two(8, before8, 2)
            gate_rows(2, 20)
            gating(2)
            add_y()

            layernorm(6)
            dve.wait_ge(S["last_psum"], 2)
            add_y()
            link(v.tensor_tensor(X[:], X[:], mid_b(row("b_lin"), J), ALU.add))

            layernorm(7)
            dve.wait_ge(S["logits_ready"], 3)
            v.tensor_scalar(s5a[:], PS[0:P, 7, 0:5], row("br"), None, ALU.add).then_inc(S["w_col"], 1)
            dve.wait_ge(S["w_col"], 1)
            dve.wait_ge(S["w_bcast"], 1)
            dve.wait_ge(S["tri_ready"], 2)
            for j in range(J):
                link(v.tensor_scalar(z(1)[:, j, :], wrow, s5a[:, j:j + 1], None, ALU.is_gt))
                link(v.scalar_tensor_tensor(out=z(2)[:, j, :], in0=wrow, scalar=s5a[:, j:j + 1], in1=z(0)[:, j, :],
                                            op0=ALU.is_equal, op1=ALU.mult))
            link(v.tensor_tensor(z(1), z(1), z(2), ALU.add))
            link(v.tensor_reduce(s5b[:], z(1), AX, ALU.add))
            link(v.tensor_scalar(s5b[:], s5b[:], int(0.5 * N) - 1 - 0.5, None, ALU.is_lt))
            link(v.tensor_tensor(s5b[:], s5b[:], s5a[:], ALU.mult))
            link(v.tensor_tensor(X[:], X[:], XN[:], ALU.add))
            dve.wait_ge(S["y_ready"], 4)
            for j in range(J):
                ins = v.scalar_tensor_tensor(out=X[:, j, :], in0=yv(j), scalar=s5b[:, j:j + 1], in1=X[:, j, :],
                                             op0=ALU.mult, op1=ALU.add)
            ins.then_inc(S["x_final"], 1)


def kernel(**inputs):
    import concourse.bacc as _bacc
    from concourse import mybir as _mybir
    from concourse.bass_utils import run_bass_kernel_spmd as _run

    i = {k: np.asarray(v) for k, v in inputs.items()}
    w1 = np.concatenate([i["L0_ffn_W1"].transpose(1, 0, 2).reshape(D, -1), i["L1_ffn_W1"].transpose(1, 0, 2).reshape(D, -1),
                         i["L2_ffn_W1"].transpose(1, 0, 2).reshape(D, -1), i["L3_ffn_w1"]], axis=1)
    w2 = np.concatenate([i["L0_ffn_W2"].reshape(-1, D), i["L1_ffn_W2"].reshape(-1, D), i["L2_ffn_W2"].reshape(-1, D),
                         i["L3_ffn_w2"]], axis=0)
    T = sum(FFN_TILES)
    w1 = w1.reshape(2, 128, T, 128).transpose(2, 1, 0, 3).reshape(T, 128, 256)
    wffn = np.concatenate([w1, w2.reshape(T, 128, 256)], axis=2)
    fe1, fn1 = i["L0_gnn_fe_W1"], i["L0_gnn_fn_W1"]
    table = np.concatenate([fe1[:D], i["L0_gnn_attn_l"][:, None], fn1[:D], fe1[D:], i["L0_gnn_attn_r"][:, None]], axis=1)
    wmat = np.concatenate([table, fn1[D:], i["L0_ffn_router_w"].T, i["L1_ffn_W_gat"], i["L2_ffn_Wg"], i["L3_ffn_wr"],
                           i["L3_gnn_W_conv"], i["L2_gnn_W_heads"].reshape(512, D).T,
                           i["L1_gnn_W"].transpose(1, 0, 2).reshape(D, 768)], axis=1)
    wmat = wmat.reshape(2, 128, WCOLS).transpose(1, 0, 2)
    f = {}
    for k, n in (("b", "b"), ("g", "g"), ("be", "be"), ("m", "m"), ("v", "v")):
        f[k] = np.concatenate([i[f"L0_gnn_fe_{n}1"], i[f"L0_gnn_fe_{n}2"], i[f"L0_gnn_fn_{n}1"], i[f"L0_gnn_fn_{n}2"]])
    f["router_b"] = i["L0_ffn_router_b"]
    f["gcn_b2"] = i["L1_gnn_b"][2]
    for n in ("att_src", "att_dst", "b_gat", "ln_gamma", "ln_beta"):
        f[n] = i["L1_ffn_" + n].reshape(-1)
    for n in ("b_heads", "g_heads", "beta_heads", "b_out", "g_out", "beta_out"):
        f[n] = i["L2_gnn_" + n].reshape(-1)
    f["a_src"], f["a_dst"] = i["L2_gnn_a_heads"][:, :64].reshape(-1), i["L2_gnn_a_heads"][:, 64:].reshape(-1)
    f["a_out_src"], f["a_out_dst"] = i["L2_gnn_a_out"][:D], i["L2_gnn_a_out"][D:]
    f["bg"], f["bias"], f["b_lin"], f["br"] = i["L2_ffn_bg"], i["L2_ffn_bias"], i["L3_gnn_b_lin"], i["L3_ffn_br"]
    rows = np.concatenate([f[n] for n, _ in ROW_SIZES])[None]
    cols = np.concatenate([i["L0_ffn_b1"].reshape(-1), i["L1_ffn_b1"].reshape(-1), i["L2_ffn_b1"].reshape(-1),
                           i["L3_ffn_b1"], i["L1_gnn_b"][:2].reshape(-1), i["L3_gnn_b_conv"]]).reshape(COLS, 128).T
    w2rows = np.zeros((32, 2, D), np.float32)
    w2rows[:24, 0] = np.tile(i["L0_gnn_fe_W2"], (6, 1))
    w2rows[:24, 1] = np.tile(i["L0_gnn_fn_W2"], (6, 1))
    part = np.zeros((32, 4), np.float32)
    part[[0, 1, 2, 3, 12, 13, 14, 15, 20, 21, 22, 23, 24], 0] = 1
    part[[4, 5, 6, 7, 16, 17, 18, 19, 25], 1] = 1
    part[[8, 9, 10, 11, 26], 2] = 1
    part[24:27, 3] = 1
    b2 = np.zeros((32, 4, D), np.float32)
    for n, k in enumerate(("L0_ffn_b2", "L1_ffn_b2", "L2_ffn_b2", "L3_ffn_b2")):
        v = i[k].reshape(-1, D)
        b2[:v.shape[0], n] = v
    sd = np.stack([i["src"], i["dst"]])
    idx1 = sd.reshape(2, NT1, P).transpose(2, 0, 1)
    idx2 = i["L1_ffn_edge_index"].reshape(2, 128, NT2).transpose(1, 0, 2)
    idxrow = sd.reshape(2, 40, 500).transpose(1, 0, 2).reshape(40, 1000)
    bounds = np.array([[P * min(usual_node_tiles(t)) for t in range(NT1)],
                       [P * (max(usual_node_tiles(t)) + 1) for t in range(NT1)]], np.float32)
    arrays = {"x": i["x"], "bounds": bounds, "idx1": idx1, "idx2": idx2, "idxrow": idxrow, "wmat": wmat, "w2rows": w2rows, "part": part,
              "rows": rows, "cols": cols, "wout": i["L2_gnn_W_out"].T, "wlin": i["L3_gnn_W_lin"], "b2": b2, "wffn": wffn}

    nc = _bacc.Bacc("TRN2", target_bir_lowering=False, num_devices=1)
    feed, args = {}, {}
    for n, v in arrays.items():
        v = np.ascontiguousarray(v)
        feed[f"in_{n}"] = v
        args[n] = nc.dram_tensor(f"in_{n}", v.shape, _mybir.dt.from_np(v.dtype), kind="ExternalInput").ap()
    out = nc.dram_tensor("out_x", (N, D), _mybir.dt.float32, kind="ExternalOutput").ap()
    gnn_ffn_program(nc, args, out)
    r = _run(nc, [feed], core_ids=[0])
    return r.results[0]["out_x"]
```

```python
import numpy as np

N, P, J, D = 625, 125, 5, 256
E1, E2 = 20000, 32768
NT1, NT2 = E1 // 125, E2 // 128
FFN_TILES = [16, 16, 32, 8]
FFN_BASE = [0, 16, 32, 64]
FFN_EXPERTS = [32, 4, 8, 1]
ROW_SIZES = [("b", 520), ("g", 520), ("be", 520), ("m", 520), ("v", 520),
             ("router_b", 32), ("gcn_b2", 256),
             ("att_src", 16), ("att_dst", 16), ("b_gat", 16), ("ln_gamma", 16), ("ln_beta", 16),
             ("b_heads", 512), ("a_src", 512), ("a_dst", 512), ("g_heads", 512), ("beta_heads", 512),
             ("b_out", 256), ("a_out_src", 256), ("a_out_dst", 256), ("g_out", 256), ("beta_out", 256),
             ("bg", 8), ("bias", 8), ("b_lin", 256), ("br", 1)]
ROW_AT, _at = {}, 0
for _n, _s in ROW_SIZES:
    ROW_AT[_n] = (_at, _s)
    _at += _s
ROWS, ROWS_L0 = _at, 2600
W_SIZES = [("table", 14), ("fn_W1b", 4), ("router", 32), ("W_gat", 16), ("Wg", 8), ("wr", 1), ("W_conv", 128),
           ("W_heads", 512), ("gcn_W", 768)]
W_AT, _at = {}, 0
for _n, _s in W_SIZES:
    W_AT[_n] = (_at, _s)
    _at += _s
WCOLS = _at
COL_FFN = [0, 16, 32, 64]
COL_GCN, COL_CONV, COLS = 72, 76, 77


SEAM = 4
TILES_PER_NODE_TILE = NT1 // J


def usual_node_tiles(t):
    m, at = divmod(t, TILES_PER_NODE_TILE)
    return [k for k, near in ((m - 1, at < SEAM), (m, True), (m + 1, at >= TILES_PER_NODE_TILE - SEAM))
            if near and 0 <= k < J]


ROUNDS = 15
TOP = 8 * ROUNDS


def usual_node_tiles2(r):
    lo = (375, 250, 125, 125)[r // 8] if r < 32 else 0
    hi = 625 if r < 40 else 500 if r < 64 else 375 if r < 80 else 250 if r < 104 else 125
    return list(range(lo // P, hi // P))


def gnn_ffn_program(nc, a, out):
    import concourse.bass as bass
    from concourse import mybir
    from concourse.alu_op_type import AluOpType as ALU
    from contextlib import ExitStack

    F32, BF16, F16, I32 = mybir.dt.float32, mybir.dt.bfloat16, mybir.dt.float16, mybir.dt.int32
    ACT = mybir.ActivationFunctionType
    AX = mybir.AxisListType.X
    EPS = 1e-5
    ABSENT = -1e30
    ds = bass.ds

    ctx = ExitStack()
    with ctx:
        def sb(name, shape, dt=F32):
            return ctx.enter_context(nc.sbuf_tensor(name, shape, dt))

        ident = sb("ident", [128, 128])
        ident16 = sb("ident16", [128, 128], BF16)
        node_iota = sb("node_iota", [128, N], F16)
        node_id = sb("node_id", [128, J])
        before8 = sb("before8", [P, 8, 8])
        before4 = sb("before4", [P, 4, 4])
        rev32 = sb("rev32", [P, 32])
        ones_row = sb("ones_row", [1, N])
        ones_col = sb("ones_col", [128, 1])
        rows = sb("rows", [128, ROWS])
        cols = sb("cols", [128, COLS])
        wmat = sb("wmat", [128, 2, WCOLS])
        wout = sb("wout", [128, 4, D])
        wlin = sb("wlin", [128, D])
        w2rows = sb("w2rows", [32, 2, D])
        part = sb("part", [32, 4])
        b2 = sb("b2", [32, 4, D])
        id1 = sb("id1", [P, 2, NT1])
        id2 = sb("id2", [128, 2, TOP])
        is_usual = sb("is_usual", [1, 3], I32)
        usual = sb("usual", [128, 3])
        zero16 = sb("zero16", [128, 128], BF16)
        X = sb("X", [P, J, D])
        XN = sb("XN", [P, J, D])
        XT = sb("XT", [128, 2, N])
        TT = sb("TT", [P, J, D])
        stats = sb("stats", [P, J, 6])
        mv = sb("mv", [P, J, 2])
        veps = sb("veps", [P, J])
        std = sb("std", [P, J])
        rstd = sb("rstd", [P, J])
        C1 = sb("C1", [P, J, N])
        AH = sb("AH", [P, J, N])
        C2 = sb("C2", [P, J, N])
        C2T = sb("C2T", [P, J, N])
        big = sb("big", [128, 4, J * N])
        bounds = big[0:P, 2, 400:720].rearrange("p (a b) -> p a b", a=2)
        inside = big[0:P, 2, 720:880]
        inside2 = big[0:P, 2, 2000:2160]
        bounds2 = big[:, 2, 2200:2200 + 2 * TOP].rearrange("p (a b) -> p a b", a=2)
        key = big[:, 3, 0:NT2]
        top = big[:, 3, 300:300 + TOP]
        rest2 = big[:, 3, 500:500 + 2 * NT2].rearrange("p (a b) -> p a b", a=2)
        scr2 = big[:, 3, 1100:1100 + 2 * NT2].rearrange("p (a b) -> p a b", a=2)
        hid_all = sb("hid_all", [128, 4, 632])
        onehot = hid_all[:, :, :].rearrange("p b n -> p (b n)").bitcast(BF16).rearrange(
            "p (b s n) -> p b s n", b=4, s=2)
        HA = C2[:, :, :].rearrange("p j n -> p (j n)")[:, 0:J * 512].rearrange("p (j n) -> p j n", j=J)
        HB_ = C2T[:, :, :].rearrange("p j n -> p (j n)")[:, 0:J * 512].rearrange("p (j n) -> p j n", j=J)
        TAB = sb("TAB", [P, J, 14])
        tabf = sb("tabf", [P, 2, J, 10])
        tabr = sb("tabr", [P, 2, J, 10])
        tab16 = sb("tab16", [P, 2, J, 10, 3], BF16)
        idxrow = big[0:P, 1, 0:2000].bitcast(I32).rearrange("p (b c) -> p b c", b=2)
        idxrow16 = big[0:P, 1, 2000:3000].bitcast(F16).rearrange("p (b c) -> p b c", b=2)
        onehotT = big[0:P, 2:4, :].rearrange("p a c -> p (a c)")[:, 0:5000].bitcast(BF16).rearrange(
            "p (b s j c) -> p b s j c", b=2, s=2, j=J)
        in_AH = AH[:, :, :].rearrange("p j n -> p (j n)")
        in_C2T = C2T[:, :, :].rearrange("p j n -> p (j n)")
        gT = big[0:30, 2:4, :].rearrange("p a c -> p (a c)")[:, 5000:6000].rearrange("p (b c) -> p b c", b=2)
        GS = in_AH[:, 0:10 * NT1].rearrange("p (t c) -> p t c", c=10)
        h1 = in_AH[:, 1600:2240].rearrange("p (t c) -> p t c", c=4)
        h2 = in_AH[:, 2240:2880].rearrange("p (t c) -> p t c", c=4)
        FR = h1
        hs16 = in_C2T[:, 0:16 * NT1].bitcast(BF16).rearrange("p (t c) -> p t c", c=32)
        EX = in_C2T[:, 2560:2560 + NT1]
        in_TT = TT[:, :, :].rearrange("p j n -> p (j n)")
        foldS, foldT = in_TT[:, 0:520], in_TT[:, 520:1040]
        idx1 = big[0:P, 2, 0:2 * NT1].bitcast(I32).rearrange("p (a b) -> p a b", a=2)
        idx2 = big[:, 2, 1000:1000 + 2 * NT2].bitcast(I32).rearrange("p (a b) -> p a b", a=2)
        w2v = big[0:32, 0, 0:514].rearrange("p (a b) -> p a b", a=2)
        w2r = big[0:32, 0, 514:1028].rearrange("p (a b) -> p a b", a=2)
        w2h = big[0:32, 0, 1028:1285].bitcast(BF16).rearrange("p (a b) -> p a b", a=2)
        w2m = big[0:32, 0, 1285:1542].bitcast(BF16).rearrange("p (a b) -> p a b", a=2)
        w2s = sb("w2s", [32, 2, 257], BF16)
        hT = sb("hT", [32, 2, 500], BF16)
        EF = big[:, 2:4, :].rearrange("p a c -> p (a c)")[:, 0:2000].rearrange("p (b h c) -> p b h c", b=2, h=2)
        msg = big[0:P, 0, 0:4 * 257].rearrange("p (b c) -> p b c", b=4)
        msgr = big[0:P, 0, 1100:1100 + 4 * 257].rearrange("p (b c) -> p b c", b=4)
        msg16 = big[0:P, 1, 0:1548].bitcast(BF16).rearrange("p (b s c) -> p b s c", b=4, s=3)[:, :, :, 0:257]
        wtile = sb("wtile", [128, 4, 512])
        hid, hidg = hid_all[:, 0:2, 0:N], hid_all[:, 2:4, 0:N]
        gate = sb("gate", [P, J, 32])
        gateT = sb("gateT", [32, N])
        grow16 = big[:, 0:2, :].rearrange("p a c -> p (a c)")[:, 0:5000].bitcast(BF16).rearrange(
            "p (e n) -> p e n", e=16)
        grow = big[:, 0:2, :].rearrange("p a c -> p (a c)")[:, 0:5000].rearrange("p (e n) -> p e n", e=8)
        gateT16 = big[0:32, 2, 0:313].bitcast(BF16)[:, 0:N]
        pair16 = big[0:32, 2, 320:1344].bitcast(BF16).rearrange("p (e c) -> p e c", e=16)
        s32a = sb("s32a", [P, J, 32])
        s32b = sb("s32b", [P, J, 32])
        s5a = sb("s5a", [P, J])
        s5b = sb("s5b", [P, J])
        s40a = sb("s40a", [P, 40])
        s40b = sb("s40b", [P, 40])
        s320a = in_TT[:, 0:320].rearrange("p (j c) -> p j c", j=J)
        s320b = in_TT[:, 320:640].rearrange("p (j c) -> p j c", j=J)
        mx = sb("mx", [P, J, 4])
        bmax = sb("bmax", [P, J, 4])
        asrc = sb("asrc", [P, J, 8])
        adst = sb("adst", [P, J, 8])
        esrc = sb("esrc", [P, J, 8])
        nb02 = sb("nb02", [P, J, 8])
        pa02 = sb("pa02", [P, J, 4])
        hx = sb("hx", [P, J, 4, 5])
        dinv = sb("dinv", [P, J])
        wrow = big[0:P, 3, 0:N]

        PS = ctx.enter_context(nc.psum_tensor("PS", [128, 8, 512], F32))

        def wide(b, p=128):
            return PS[0:p, b:b + 2, :].rearrange("p b c -> p (b c)")[:, 0:640].rearrange(
                "p (j c) -> p j c", c=128)[:, :, 0:125]

        def yv(j):
            return PS[0:P, 4 + j // 2, (j % 2) * 256:(j % 2) * 256 + 256]

        def blocks(ap):
            return ap.rearrange("p (b c) -> p b c", c=125)

        def row(name, p=P):
            o, s = ROW_AT[name]
            return rows[0:p, o:o + s]

        def wm(name, h):
            o, s = W_AT[name]
            return wmat[:, h, o:o + s]

        def mid_b(ap, n):
            return ap.unsqueeze(1).to_broadcast([ap.shape[0], n, ap.shape[1]])

        def last_b(ap, n):
            return ap.unsqueeze(2).to_broadcast([ap.shape[0], ap.shape[1], n])

        names = """consts usual_ready usual_psum usual_known rest_onehot rest_used x_in idx_in l0_in rest_in out_done
            vector_step pool_step
            var_ready std_ready ln_rows xt_psum xt_sb
            table_ready tables_split onehot_ready onehot_used counts_out
            fold_var fold_std
            a1_row edge_max_ready rows_cast ids_onehot gathered gT_sb gT_psum gather_read
            logit_in edge_exp h1_ready
            hT_psum hT_sb fe_psum ef_act ef_dve fn1_psum fn1_read h2_ready
            hT2_psum hT2_sb fn2_psum msg_ready msg_hi msg_rest msg_mid msg_lo msg_used edges_done
            deg_ready deg_std b_ready bt_psum bt_act bt_dve
            t_ready t_act t_dve agg_psum h_act h_dve last_psum
            gat_h gat_a row_psum row_read rows2_psum gat_sum gat_sub gat_exp gat_mul gat_mm
            gat_var gat_std sm_in sm_out gates_ready gr_psum gr_act gr_dve gt_psum gt_sb
            h_psum h_sb h_gated y_used y_ready logits_ready
            hh_psum s_ready head_row esrc_ready relu_act relu_dve head_exp head_mul head_psum head_out head_read
            hln_var hln_std elu_in elu_exp x2_ready x2_psum x2_act x2_dve
            ho_psum so_ready o_row o_exp o_mul o_psum oelu_in oelu_exp
            w_col w_row_psum w_row_sb w_bcast x_final tri_ready""".split()
        S = {n: ctx.enter_context(nc.semaphore(n)) for n in names}
        idx_row_in = [ctx.enter_context(nc.semaphore(f"idx_row_in{u}")) for u in range(2)]
        w_in = [ctx.enter_context(nc.semaphore(f"w_in{u}")) for u in range(4)]

        def chunk_loops(eng, body, usual_order):
            if not usual_order:
                body(0, lambda u: range(J))
                body(1, lambda u: range(J))
                with eng.Fori(2, 20) as i:
                    body(i, lambda u: range(J))
                return
            for m in range(J):
                def at(i):
                    return lambda u: usual_node_tiles(4 * (2 * i + u) if u == 0 else 4 * (2 * i + u) + 3)
                if m == 0:
                    for i in range(3):
                        body(i, at(i))
                else:
                    body(4 * m, at(4 * m))
                    with eng.Fori(4 * m + 1, 4 * m + 3) as i:
                        body(i, lambda u: [m])
                body(4 * m + 3, at(4 * m + 3))

        block = ctx.enter_context(nc.Block())
        NCONST = 18

        @block.sync
        def _(sp):
            sp.dma_start(X[:], a["x"].rearrange("(j p) d -> p j d", p=P)).then_inc(S["x_in"], 16)
            sp.dma_start(idx2, a["idx2"]).then_inc(S["idx_in"], 16)
            sp.dma_start(idx1, a["idx1"]).then_inc(S["idx_in"], 16)
            sp.dma_start(bounds, a["bounds"].rearrange("a b -> (a b)").unsqueeze(0).to_broadcast([P, 2 * NT1])
                         .rearrange("p (a b) -> p a b", a=2)).then_inc(S["idx_in"], 16)
            sp.dma_start(bounds2, a["bounds2"].rearrange("a b -> (a b)").unsqueeze(0).to_broadcast([128, 2 * TOP])
                         .rearrange("p (a b) -> p a b", a=2)).then_inc(S["idx_in"], 16)
            sp.dma_start(wmat[:], a["wmat"]).then_inc(S["l0_in"], 16)
            sp.dma_start(w2rows[:], a["w2rows"]).then_inc(S["l0_in"], 16)
            sp.dma_start(part[:], a["part"]).then_inc(S["l0_in"], 16)
            sp.dma_start(rows[:], a["rows"].to_broadcast([128, ROWS])).then_inc(S["l0_in"], 16)
            sp.dma_start(cols[:], a["cols"]).then_inc(S["rest_in"], 16)
            sp.dma_start(wout[:], a["wout"].rearrange("(k p) n -> p k n", p=128)).then_inc(S["rest_in"], 16)
            sp.dma_start(wlin[:], a["wlin"]).then_inc(S["rest_in"], 16)
            sp.dma_start(b2[:], a["b2"]).then_inc(S["rest_in"], 16)
            for u in range(4):
                sp.dma_start(wtile[:, u, :], a["wffn"][u]).then_inc(w_in[u], 16)

            def id_rows(i, first):
                for u in range(2):
                    if not first:
                        sp.wait_ge(S["rows_cast"], 2 * i + u - 1)
                    sp.dma_start(idxrow[:, u, :], a["idxrow"][ds(2 * i + u, 1), :].to_broadcast([P, 1000])
                                 ).then_inc(idx_row_in[u], 16)
            sp.wait_ge(S["edge_max_ready"], 1)
            id_rows(0, True)
            with sp.Fori(1, 20) as i:
                id_rows(i, False)

            with sp.Fori(1, sum(FFN_TILES) // 4) as i:
                for u in range(4):
                    sp.wait_ge(S["y_used"], 4 * i + u - 3)
                    sp.dma_start(wtile[:, u, :], a["wffn"][ds(4 * i + u, 1), :, :].rearrange("a p c -> p (a c)")
                                 ).then_inc(w_in[u], 16)

            sp.wait_ge(S["x_final"], 1)
            sp.dma_start(out.rearrange("(j p) d -> p j d", p=P), X[:]).then_inc(S["out_done"], 16)
            sp.wait_ge(S["out_done"], 16)

        @block.gpsimd
        def _(pool):
            g = nc.gpsimd
            step = [0]

            def link(ins):
                step[0] += 1
                ins.then_inc(S["pool_step"], 1)
                pool.wait_ge(S["pool_step"], step[0])

            link(g.memset(ident[:], 0.0))
            link(g.memset(before8[:], 1.0))
            link(g.memset(before4[:], 1.0))
            c = S["consts"]
            g.affine_select(out=ident[:], in_=ident[:], compare_op=ALU.not_equal, fill=1.0, base=0,
                            pattern=[[-1, 128]], channel_multiplier=1).then_inc(c, 1)
            pool.wait_ge(c, 1)
            g.tensor_copy(ident16[:], ident[:]).then_inc(c, 1)
            g.iota(node_iota[:], pattern=[[1, N]], base=0, channel_multiplier=0,
                   allow_small_or_imprecise_dtypes=True).then_inc(c, 1)
            g.iota(node_id[:], pattern=[[P, J]], base=0, channel_multiplier=1,
                   allow_small_or_imprecise_dtypes=True).then_inc(c, 1)
            g.affine_select(out=before8[:], in_=before8[:], compare_op=ALU.is_gt, fill=0.0, base=0,
                            pattern=[[1, 8], [-1, 8]], channel_multiplier=0).then_inc(c, 1)
            g.affine_select(out=before4[:], in_=before4[:], compare_op=ALU.is_gt, fill=0.0, base=0,
                            pattern=[[1, 4], [-1, 4]], channel_multiplier=0).then_inc(c, 1)
            g.iota(rev32[:], pattern=[[-1, 32]], base=32, channel_multiplier=0,
                   allow_small_or_imprecise_dtypes=True).then_inc(c, 1)
            g.memset(ones_row[:], 1.0).then_inc(c, 1)
            g.memset(hs16, 0.0).then_inc(c, 1)
            pool.wait_ge(c, 9)
            g.memset(hs16[:, :, 24:27], 1.0).then_inc(c, 1)
            g.memset(hx[:, :, :, 4:5], 1.0).then_inc(c, 1)
            g.memset(tabf[:, 0, :, 9:10], 0.0).then_inc(c, 1)
            g.memset(tabf[:, 1, :, 5:9], 0.0).then_inc(c, 1)
            g.memset(ones_col[:], 1.0).then_inc(c, 1)
            g.memset(zero16[:], 0.0).then_inc(c, 1)
            g.memset(usual[:], 1.0).then_inc(c, 1)
            g.memset(s5b[:], 0.0).then_inc(c, 1)
            g.memset(std[:], 0.0).then_inc(c, 1)

            def rest(t, b):
                pool.wait_ge(S["msg_hi"], t + 1)
                g.tensor_tensor(msgr[:, b, :], msg[:, b, :], msg16[:, b, 0, :], ALU.subtract
                                ).then_inc(S["msg_rest"], 1)

            def rests(i, last):
                for q in range(8):
                    t = 8 * i + q
                    b = q % 4
                    if not (last and q == 7):
                        rest(t + 1, (q + 1) % 4)
                    pool.wait_ge(S["msg_mid"], t + 1)
                    g.tensor_tensor(msg16[:, b, 2, :], msgr[:, b, :], msg16[:, b, 1, :], ALU.subtract
                                    ).then_inc(S["msg_lo"], 1)
            rest(0, 0)
            with pool.Fori(0, 19) as i:
                rests(i, False)
            rests(19, True)

            tri = big[0:P, 0, :]
            pool.wait_ge(S["y_ready"], 3)
            g.memset(tri, 1.0).then_inc(S["tri_ready"], 1)
            pool.wait_ge(S["tri_ready"], 1)
            triv = tri.rearrange("p (j n) -> p j n", j=J)
            g.affine_select(out=triv, in_=triv, compare_op=ALU.is_gt, fill=0.0, base=0,
                            pattern=[[P, J], [-1, N]], channel_multiplier=1).then_inc(S["tri_ready"], 1)
            pool.wait_ge(S["w_row_sb"], 1)
            g.partition_broadcast(wrow, gateT[0:1, :], channels=P).then_inc(S["w_bcast"], 1)

        @block.scalar
        def _(act):
            s = nc.scalar

            def layernorm(k):
                act.wait_ge(S["var_ready"], k + 1)
                s.activation(std[:], veps[:], ACT.Sqrt).then_inc(S["std_ready"], 1)
                act.wait_ge(S["xt_psum"], 2 * k + 1)
                s.copy(blocks(XT[:, 0, :]), wide(0)).then_inc(S["xt_sb"], 1)

            def evacuate_counts(C):
                s.copy(C[:, :, 0:500], PS[0:P, 0:5, 0:500])
                s.copy(C[:, 0:4, 500:625], PS[0:P, 5, 0:500].rearrange("p (m c) -> p m c", m=4))
                s.copy(C[:, 4, 500:625], PS[0:P, 6, 0:125]).then_inc(S["counts_out"], 1)

            act.wait_ge(S["consts"], NCONST)
            layernorm(0)
            act.wait_ge(S["fold_var"], 1)
            s.activation(foldS, foldS, ACT.Sqrt).then_inc(S["fold_std"], 1)
            act.wait_ge(S["onehot_used"], TOP)
            evacuate_counts(C2)
            act.wait_ge(S["onehot_used"], TOP + NT1)
            evacuate_counts(C1)

            def cast_ids(t, u, arrivals, first):
                act.wait_ge(idx_row_in[u], 16 * arrivals)
                if not first:
                    act.wait_ge(S["ids_onehot"], t - 1)
                s.copy(idxrow16[:, u, :], idxrow[:, u, :]).then_inc(S["rows_cast"], 1)

            def take_gathered(t, u, first):
                act.wait_ge(S["gathered"], t + 1)
                if not first:
                    act.wait_ge(S["gT_psum"], t - 1)
                s.copy(gT[:, u, :], PS[0:30, u, 0:500]).then_inc(S["gT_sb"], 1)

            def two_chunks(i):
                cast_ids(2 * i + 1, 1, i + 1, isinstance(i, int) and i == 0)
                if not (isinstance(i, int) and i == 0):
                    take_gathered(2 * i - 1, 1, isinstance(i, int) and i == 1)
                if not (isinstance(i, int) and i == 19):
                    cast_ids(2 * i + 2, 0, i + 2, False)
                take_gathered(2 * i, 0, isinstance(i, int) and i == 0)
            cast_ids(0, 0, 1, True)
            two_chunks(0)
            two_chunks(1)
            with act.Fori(2, 19) as i:
                two_chunks(i)
            two_chunks(19)
            take_gathered(39, 1, False)

            act.wait_ge(S["logit_in"], 1)
            s.activation(EX, EX, ACT.Exp).then_inc(S["edge_exp"], 1)

            hTp = [blocks(PS[0:32, b, 0:500]) for b in range(8)]

            def edge_hT(t, u):
                act.wait_ge(S["hT_psum"], t + 1)
                s.copy(blocks(hT[:, u, :]), hTp[u]).then_inc(S["hT_sb"], 1)

            def edge_relu(t, u):
                act.wait_ge(S["fe_psum"], t + 1)
                s.activation(EF[:, u, 0, :], PS[:, 2 + 2 * u, 0:500], ACT.Relu).then_inc(S["ef_act"], 1)

            edge_hT(0, 0)

            def loop_a(i, last):
                for u in range(2):
                    if not (last and u == 1):
                        edge_hT(2 * i + u + 1, 1 - u)
                    edge_relu(2 * i + u, u)
            loop_a(0, False)
            with act.Fori(1, 19) as i:
                loop_a(i, False)
            loop_a(19, True)

            def msg_high(t, b):
                act.wait_ge(S["msg_ready"], t + 1)
                s.copy(msg16[:, b, 0, :], msg[:, b, :]).then_inc(S["msg_hi"], 1)

            def loop_b(i, last):
                for q in range(8):
                    t = 8 * i + q
                    b = q % 4
                    if not (last and q == 7):
                        msg_high(t + 1, (q + 1) % 4)
                    act.wait_ge(S["msg_rest"], t + 1)
                    s.copy(msg16[:, b, 1, :], msgr[:, b, :]).then_inc(S["msg_mid"], 1)
                    if q % 4 == 0 and not last:
                        act.wait_ge(S["hT2_psum"], 2 * i + q // 4 + 3)
                        s.copy(blocks(hT[:, q // 4, :]), hTp[5]).then_inc(S["hT2_sb"], 1)
            act.wait_ge(S["hT2_psum"], 1)
            s.copy(blocks(hT[:, 0, :]), hTp[5]).then_inc(S["hT2_sb"], 1)
            act.wait_ge(S["hT2_psum"], 2)
            s.copy(blocks(hT[:, 1, :]), hTp[5]).then_inc(S["hT2_sb"], 1)
            msg_high(0, 0)
            loop_b(0, False)
            with act.Fori(1, 19) as i:
                loop_b(i, False)
            loop_b(19, True)

            def gate_rows(n, done):
                tiles = 16 if n == 0 else FFN_EXPERTS[n]
                dst = grow16 if n == 0 else grow
                for e in range(0, tiles, 2):
                    act.wait_ge(S["gr_psum"], done + e + 1)
                    s.copy(blocks(dst[:, e, :]), wide(0)).then_inc(S["gr_act"], 1)

            def hidden(n, func):
                base, T = FFN_BASE[n], FFN_TILES[n]

                def body(i, first):
                    for u in range(4):
                        t = base + 4 * i + u
                        act.wait_ge(S["h_psum"], t + 1)
                        if not (first and u < 2):
                            act.wait_ge(S["h_gated"] if n < 3 else S["y_used"], t - 1)
                        s.activation(blocks(hid[:, u % 2, :]), wide(2 * (u % 2)), func,
                                     bias=cols[:, ds(COL_FFN[n] + 4 * i + u, 1)]).then_inc(S["h_sb"], 1)
                body(0, True)
                with act.Fori(1, T // 4) as i:
                    body(i, False)

            act.wait_ge(S["rest_in"], 64)
            layernorm(1)
            gate_rows(0, 0)
            hidden(0, ACT.Relu)

            act.wait_ge(S["deg_ready"], 1)
            s.activation(dinv[:], dinv[:], ACT.Sqrt).then_inc(S["deg_std"], 1)
            for i in range(0, 10, 2):
                act.wait_ge(S["bt_psum"], i + 1)
                if i < 5:
                    s.activation(blocks(AH[:, i, :]), wide(0, P), ACT.Copy, scale=dinv[:, i:i + 1]).then_inc(S["bt_act"], 1)
                else:
                    s.copy(blocks(C2T[:, i - 5, :]), wide(0, P)).then_inc(S["bt_act"], 1)
            layernorm(2)
            tps = PS[0:P, 4:7, :].rearrange("p b c -> p (b c)")
            for l in range(3):
                act.wait_ge(S["t_ready"], l + 1)
                s.copy(TT[:, 0:2, :], tps[:, 0:512].rearrange("p (j c) -> p j c", c=D)).then_inc(S["t_act"], 1)
                if l < 2:
                    act.wait_ge(S["agg_psum"], 2 * l + 1)
                    s.activation(blocks(XT[:, 0, :]), wide(0), ACT.Relu,
                                 bias=cols[:, COL_GCN + 2 * l:COL_GCN + 2 * l + 1]).then_inc(S["h_act"], 1)

            layernorm(3)

            def z(b):
                return big[0:P, b, :].rearrange("p (j n) -> p j n", j=J)

            def scores(h):
                act.wait_ge(S["rows2_psum"], 2 * h + 1)
                for j in range(J):
                    ins = s.activation(blocks(z(h)[:, j, :]), wide(0, P), ACT.Relu,
                                       bias=asrc[:, j, h:h + 1])
                ins.then_inc(S["gat_sum"], 1)

            def exps(h):
                act.wait_ge(S["gat_sub"], h + 1)
                for j in range(J):
                    ins = s.activation(z(h)[:, j, :], z(h)[:, j, :], ACT.Exp, bias=pa02[:, j, h:h + 1])
                ins.then_inc(S["gat_exp"], 1)
            scores(0)
            for h in range(4):
                if h < 3:
                    scores(h + 1)
                exps(h)
            act.wait_ge(S["gat_var"], 1)
            s.activation(s5a[:], s5a[:], ACT.Sqrt).then_inc(S["gat_std"], 1)
            act.wait_ge(S["sm_in"], 1)
            s.activation(s32a[:, :, 0:4], s32a[:, :, 0:4], ACT.Exp).then_inc(S["sm_out"], 1)
            gate_rows(1, 16)
            hidden(1, ACT.Gelu)

            layernorm(4)
            act.wait_ge(S["s_ready"], 1)
            s.activation(esrc[:], asrc[:], ACT.Exp, scale=-0.2).then_inc(S["esrc_ready"], 1)

            def head_relu(h):
                act.wait_ge(S["head_row"], h + 1)
                if h >= 4:
                    act.wait_ge(S["head_psum"], h - 3)
                for j in range(J):
                    ins = s.activation(blocks(z(h % 4)[:, j, :]), wide(2 * (h % 2), P), ACT.Relu,
                                       bias=adst[:, j, h:h + 1])
                ins.then_inc(S["relu_act"], 1)

            def head_exp(h):
                act.wait_ge(S["relu_dve" if h % 2 else "relu_act"], h // 2 + 1)
                for j in range(J):
                    ins = s.activation(z(h % 4)[:, j, :], z(h % 4)[:, j, :], ACT.Exp, scale=-0.8,
                                       bias=nb02[:, j, h:h + 1])
                ins.then_inc(S["head_exp"], 1)
            head_relu(0)
            for h in range(8):
                if h % 2 and h < 7:
                    head_relu(h + 1)
                head_exp(h)
            act.wait_ge(S["hln_var"], 1)
            s.activation(s40a[:], s40a[:], ACT.Sqrt).then_inc(S["hln_std"], 1)
            act.wait_ge(S["elu_in"], 1)
            s.activation(HA, HA, ACT.Exp).then_inc(S["elu_exp"], 1)
            x2t = big[:, 3, 0:2500].rearrange("p (k n) -> p k n", k=4)
            for k in range(0, 4, 2):
                act.wait_ge(S["x2_psum"], k + 1)
                s.copy(blocks(x2t[:, k, :]), wide(0)).then_inc(S["x2_act"], 1)
            act.wait_ge(S["so_ready"], 1)
            s.activation(esrc[:, :, 0], asrc[:, :, 0], ACT.Exp, scale=-0.2).then_inc(S["esrc_ready"], 1)
            act.wait_ge(S["o_row"], 1)
            for j in range(J):
                ins = s.activation(blocks(z(0)[:, j, :]), wide(0, P), ACT.Relu, bias=adst[:, j, 0:1])
            ins.then_inc(S["relu_act"], 1)
            act.wait_ge(S["relu_act"], 5)
            for j in range(J):
                ins = s.activation(z(0)[:, j, :], z(0)[:, j, :], ACT.Exp, scale=-0.8, bias=nb02[:, j, 0:1])
            ins.then_inc(S["o_exp"], 1)
            act.wait_ge(S["hln_var"], 2)
            s.activation(std[:], veps[:], ACT.Sqrt).then_inc(S["hln_std"], 1)
            act.wait_ge(S["oelu_in"], 1)
            s.activation(XN[:], XN[:], ACT.Exp).then_inc(S["oelu_exp"], 1)

            layernorm(5)
            act.wait_ge(S["sm_in"], 2)
            s.activation(s32a[:, :, 0:8], s32a[:, :, 0:8], ACT.Exp).then_inc(S["sm_out"], 1)
            gate_rows(2, 20)
            hidden(2, ACT.Relu)

            layernorm(6)
            act.wait_ge(S["t_ready"], 4)
            s.copy(TT[:, :, 0:128], PS[0:P, 4:6, :].rearrange("p b c -> p (b c)")[:, 0:640].rearrange(
                "p (j c) -> p j c", c=128)).then_inc(S["t_act"], 1)
            act.wait_ge(S["agg_psum"], 5)
            s.activation(blocks(XT[:, 0, :]), wide(0), ACT.Identity, bias=cols[:, COL_CONV:COL_CONV + 1]
                         ).then_inc(S["h_act"], 1)

            layernorm(7)
            act.wait_ge(S["w_row_psum"], 1)
            s.copy(blocks(gateT[0:1, :]), wide(0, 1)).then_inc(S["w_row_sb"], 1)
            hidden(3, ACT.Gelu_apprx_tanh)

        @block.tensor
        def _(pe):
            mm = nc.tensor.matmul
            idn = ident[0:P, 0:P]

            def layernorm(k):
                pe.wait_ge(S["ln_rows"], J * (k + 1))
                for h in range(2):
                    for j in range(J):
                        ins = nc.tensor.transpose(wide(2 * h)[:, j, :], XN[:, j, h * 128:h * 128 + 128], idn)
                    ins.then_inc(S["xt_psum"], 1)
                pe.wait_ge(S["xt_sb"], 2 * (k + 1))

            def project(name, outs, done):
                for j in range(J):
                    for h in range(2):
                        ins = mm(outs[j], XT[:, h, j * P:j * P + P], wm(name, h), start=(h == 0), stop=(h == 1))
                ins.then_inc(done, 1)

            def spread(b, col, p, done):
                for j in range(J):
                    ins = mm(wide(b, p)[:, j, :], col(j), idn, start=True, stop=True)
                ins.then_inc(done, 1)

            pe.wait_ge(S["consts"], NCONST)
            pe.wait_ge(S["l0_in"], 64)
            layernorm(0)
            project("table", [PS[0:P, 4, 16 * j:16 * j + 14] for j in range(J)], S["table_ready"])

            def clear(banks):
                for b in banks:
                    mm(PS[0:P, b, 0:500], zero16[:, 0:P], zero16[:, 0:1].to_broadcast([128, 500]), start=True,
                       stop=False, skip_group_check=True)

            def count(t, u, rows_, nodes, ready="onehot_ready", used="onehot_used"):
                pe.wait_ge(S[ready], t + 1)
                for m in nodes:
                    w = onehot[0:rows_, u, 1, m * P:m * P + P]
                    mm(PS[0:P, m, 0:500], w, onehot[0:rows_, u, 0, 0:500], start=False, stop=False,
                       skip_group_check=True)
                    b, c = (5, m * P) if m < 4 else (6, 0)
                    ins = mm(PS[0:P, b, c:c + P], w, onehot[0:rows_, u, 0, 500:625], start=False, stop=False,
                             skip_group_check=True)
                ins.then_inc(S[used], 1)

            pe.wait_ge(S["usual_ready"], 1)
            mm(PS[0:1, 7, 0:3], ones_col[:], usual[:], start=True, stop=True).then_inc(S["usual_psum"], 1)
            pe.wait_ge(S["usual_known"], 1)
            flag = pe.value_load(is_usual[:, 0:1], min_val=0, max_val=1)
            none_left = pe.value_load(is_usual[:, 1:2], min_val=0, max_val=1)
            even2 = pe.value_load(is_usual[:, 2:3], min_val=0, max_val=1)
            clear(range(7))
            with pe.If(none_left < 1):
                with pe.Fori(0, NT2 // 4) as i:
                    for u in range(4):
                        count(4 * i + u, u, 128, range(J), "rest_onehot", "rest_used")
            with pe.If(even2 > 0):
                for r in range(0, TOP, 8):
                    with pe.Fori(r // 4, r // 4 + 2) as i:
                        for u in range(4):
                            count(4 * i + u, u, 128, usual_node_tiles2(r))
            with pe.Else():
                with pe.Fori(0, TOP // 4) as i:
                    for u in range(4):
                        count(4 * i + u, u, 128, range(J))
            pe.wait_ge(S["counts_out"], 1)
            clear(range(7))
            with pe.If(flag > 0):
                for m in range(J):
                    t0 = m * TILES_PER_NODE_TILE
                    for u in range(4):
                        count(TOP + t0 + u, u, P, usual_node_tiles(t0 + u))
                    with pe.Fori(t0 // 4 + 1, t0 // 4 + TILES_PER_NODE_TILE // 4 - 1) as i:
                        for u in range(4):
                            count(4 * i + u + TOP, u, P, [m])
                    for u in range(4):
                        t = t0 + TILES_PER_NODE_TILE - 4 + u
                        count(TOP + t, u, P, usual_node_tiles(t))
            with pe.Else():
                with pe.Fori(0, NT1 // 4) as i:
                    for u in range(4):
                        count(4 * i + u + TOP, u, P, range(J))

            pe.wait_ge(S["counts_out"], 2)
            spread(0, lambda j: TAB[:, j, 4:5].to_broadcast([P, P]), P, S["a1_row"])
            pe.wait_ge(S["tables_split"], 1)

            def gather(i, nodes):
                for u in range(2):
                    t = 2 * i + u
                    pe.wait_ge(S["ids_onehot"], t + 1)
                    if not (isinstance(t, int) and t < 2):
                        pe.wait_ge(S["gT_sb"], t - 1)
                    sides = [(0, j) for j in range(J)] + [(1, j) for j in nodes(u)]
                    for n, (sd, j) in enumerate(sides):
                        ins = mm(PS[0:30, u, 0:500], tab16[:, sd, j, :, :].rearrange("p a b -> p (a b)"),
                                 onehotT[:, u, sd, j, :], start=(n == 0), stop=(n == len(sides) - 1))
                    ins.then_inc(S["gathered"], 1)
                    if not (isinstance(t, int) and t < 1):
                        turn(t - 1, 1 - u)

            def turn(t, u):
                pe.wait_ge(S["gT_sb"], t + 1)
                if not (isinstance(t, int) and t < 2):
                    pe.wait_ge(S["gather_read"], t - 1)
                mm(PS[0:P, 2 + u, 0:30], gT[:, u, 0:P], ident[0:30, 0:30], start=True, stop=True)
                for q in range(1, 4):
                    ins = nc.tensor.transpose(PS[0:P, 2 + u, 30 * q:30 * q + 30], gT[:, u, q * P:q * P + P],
                                              ident[0:30, 0:30])
                ins.then_inc(S["gT_psum"], 1)
            with pe.If(flag > 0):
                chunk_loops(pe, gather, True)
            with pe.Else():
                chunk_loops(pe, gather, False)
            turn(39, 1)

            hTp = [blocks(PS[0:32, b, 0:500]) for b in range(8)]

            def edge_transpose(t, u, first):
                if not first:
                    pe.wait_ge(S["hT_sb"], t - 1)
                for q in range(4):
                    ins = mm(hTp[u][:, q, :], hs16[:, ds(4 * t + q, 1), :].rearrange("p a c -> p (a c)"),
                             ident16[0:P, 0:P], start=True, stop=True)
                ins.then_inc(S["hT_psum"], 1)

            def edge_up(t, u, first):
                pe.wait_ge(S["hT_sb"], t + 1)
                if not first:
                    pe.wait_ge(S["ef_act"], t - 1)
                    pe.wait_ge(S["ef_dve"], t - 1)
                for h in range(2):
                    ins = mm(PS[:, 2 + 2 * u + h, 0:500], w2s[:, 0, h * 128:h * 128 + 128], hT[:, u, :],
                             start=True, stop=True)
                ins.then_inc(S["fe_psum"], 1)

            def edge_down(t, u, first):
                pe.wait_ge(S["ef_act"], t + 1)
                pe.wait_ge(S["ef_dve"], t + 1)
                if not first:
                    pe.wait_ge(S["fn1_read"], t - 1)
                for q in range(4):
                    for h in range(2):
                        ins = mm(PS[0:P, 6 + u, 4 * q:4 * q + 4], EF[:, u, h, q * P:q * P + P], wm("fn_W1b", h),
                                 start=(h == 0), stop=(h == 1))
                ins.then_inc(S["fn1_psum"], 1)

            pe.wait_ge(S["h1_ready"], 1)
            edge_transpose(0, 0, True)

            def loop_a(i, first, last):
                for u in range(2):
                    t = 2 * i + u
                    if not (last and u == 1):
                        edge_transpose(t + 1, 1 - u, first and u == 0)
                    edge_up(t, u, first)
                    if not (first and u == 0):
                        edge_down(t - 1, 1 - u, first)
            loop_a(0, True, False)
            with pe.Fori(1, 2) as i:
                for u in range(2):
                    t = 2 * i + u
                    edge_transpose(t + 1, 1 - u, False)
                    edge_up(t, u, False)
                    edge_down(t - 1, 1 - u, u == 0)
            with pe.Fori(2, 19) as i:
                loop_a(i, False, False)
            loop_a(19, False, True)
            edge_down(39, 1, False)

            pe.wait_ge(S["h2_ready"], 1)

            def msg_transpose(g, first):
                if not first:
                    pe.wait_ge(S["hT2_sb"], g)
                for q in range(4):
                    ins = mm(hTp[5][:, q, :], hs16[:, ds(4 * g + q, 1), :].rearrange("p a c -> p (a c)"),
                             ident16[0:P, 0:P], start=True, stop=True)
                ins.then_inc(S["hT2_psum"], 1)

            def msg_up(q):
                mm(PS[0:P, 6 + q % 2, 0:257], hT[:, q // 4, (q % 4) * P:(q % 4) * P + P], w2s[:, 1, :],
                   start=True, stop=True).then_inc(S["fn2_psum"], 1)

            def msg_sum(t, q, nodes):
                pe.wait_ge(S["onehot_ready"], TOP + NT1 + 1 + t)
                pe.wait_ge(S["msg_lo"], t + 1)
                for m in nodes:
                    for c in range(3):
                        ins = mm(PS[0:P, m, 0:257], onehot[0:P, q % 4, 1, m * P:m * P + P], msg16[:, q % 4, c, :],
                                 start=False, stop=False, skip_group_check=True)
                ins.then_inc(S["msg_used"], 1)

            def eight(i, nodes, last):
                for q in range(8):
                    t = 8 * i + q
                    if not (last and q >= 5):
                        if q % 4 == 1:
                            pe.wait_ge(S["hT2_sb"], 2 * i + (2 if q == 1 else 3))
                        pe.wait_ge(S["msg_ready"], t + 2)
                        msg_up((q + 3) % 8)
                    if q % 4 == 0 and not last:
                        msg_transpose(2 * i + q // 4 + 2, False)
                    msg_sum(t, q, nodes(q))

            msg_transpose(0, True)
            clear(range(J))
            msg_transpose(1, False)
            msg_up(0)
            msg_up(1)
            pe.wait_ge(S["msg_ready"], 1)
            msg_up(2)
            with pe.If(flag > 0):
                per = TILES_PER_NODE_TILE // 8
                for m in range(J):
                    eight(per * m, lambda q: usual_node_tiles(8 * per * m + q), False)
                    with pe.Fori(per * m + 1, per * m + per - 1) as i:
                        eight(i, lambda q: [m], False)
                    end = per * m + per - 1
                    eight(end, lambda q: usual_node_tiles(8 * end + q), m == J - 1)
            with pe.Else():
                with pe.Fori(0, 19) as i:
                    eight(i, lambda q: range(J), False)
                eight(19, lambda q: range(J), True)

            def gate_rows(n, done):
                pe.wait_ge(S["gates_ready"], n + 1)
                E = FFN_EXPERTS[n]
                for j in range(J):
                    ins = nc.tensor.transpose(wide(4, E)[:, j, :], gate[:, j, 0:E], idn)
                ins.then_inc(S["gt_psum"], 1)
                if n == 0:
                    pe.wait_ge(S["gt_sb"], 1)
                for e in range(16 if n == 0 else E):
                    if e >= 2:
                        pe.wait_ge(S["gr_dve" if e % 2 else "gr_act"], done // 2 + e // 2)
                    if n == 0:
                        for c0, c1 in ((0, 4), (4, 5)):
                            ins = mm(wide(2 * (e % 2))[:, c0:c1, :], pair16[:, e, :], gateT16[:, c0 * P:c1 * P],
                                     start=True, stop=True)
                        ins.then_inc(S["gr_psum"], 1)
                    else:
                        spread(2 * (e % 2), lambda j: gate[:, j, e:e + 1].to_broadcast([P, 128]), 128, S["gr_psum"])
                k = (16 if n == 0 else E) + done
                pe.wait_ge(S["gr_dve"], k // 2)
                pe.wait_ge(S["gr_act"], k // 2)
                pe.wait_ge(S["gt_sb"], n + 1)

            def ffn(n):
                base, T, E = FFN_BASE[n], FFN_TILES[n], FFN_EXPERTS[n]

                def up(i, u, first):
                    t = base + 4 * i + u
                    pe.wait_ge(w_in[u], 16 * (base // 4 + i) + 16)
                    if not first:
                        pe.wait_ge(S["h_sb"], t - 1)
                    for c0, c1 in ((0, 4), (4, 5)):
                        for h in range(2):
                            ins = mm(wide(2 * (u % 2))[:, c0:c1, :], wtile[:, u, h * 128:h * 128 + 128],
                                     XT[:, h, c0 * P:c1 * P], start=(h == 0), stop=(h == 1))
                    ins.then_inc(S["h_psum"], 1)

                src, ready = (hidg, S["h_gated"]) if n < 3 else (hid, S["h_sb"])

                def down(i, u, first):
                    t = base + 4 * i + u
                    pe.wait_ge(ready, t + 1)
                    for j in range(J):
                        ins = mm(yv(j), src[:, u % 2, j * P:j * P + P], wtile[:, u, 256:512],
                                 start=first and j % 2 == 0, stop=False, skip_group_check=True)
                    ins.then_inc(S["y_used"], 1)

                def body(i, first, last):
                    for u in range(4):
                        if u < 3:
                            up(i, u + 1, first and u == 0)
                        elif not last:
                            up(i + 1, 0, False)
                        down(i, u, first and u == 0)
                up(0, 0, True)
                body(0, True, False)
                if T > 8:
                    with pe.Fori(1, T // 4 - 1) as i:
                        body(i, False, False)
                body(T // 4 - 1, False, True)
                lhs = gateT if n < 3 else ones_row
                for j in range(J):
                    ins = mm(yv(j), lhs[0:E, j * P:j * P + P], b2[0:E, n, :], start=False, stop=True,
                             skip_group_check=True)
                ins.then_inc(S["y_ready"], 1)

            pe.wait_ge(S["rest_in"], 64)
            small = [PS[0:P, 7, 32 * j:32 * j + 32] for j in range(J)]
            layernorm(1)
            project("router", small, S["logits_ready"])
            gate_rows(0, 0)
            ffn(0)

            pe.wait_ge(S["b_ready"], 1)
            b1 = big[0:P, 2, :].rearrange("p (j n) -> p j n", j=J)
            for i in range(10):
                src = b1 if i < 5 else C2
                if i >= 2:
                    pe.wait_ge(S["bt_dve" if i % 2 else "bt_act"], i // 2)
                for j in range(J):
                    ins = nc.tensor.transpose(wide(2 * (i % 2), P)[:, j, :], src[:, j, (i % 5) * P:(i % 5) * P + P], idn)
                ins.then_inc(S["bt_psum"], 1)
            pe.wait_ge(S["bt_dve"], 5)
            pe.wait_ge(S["bt_act"], 5)
            layernorm(2)

            def aggregate(h, width, done):
                for c0, c1 in ((0, 4), (4, 5)):
                    for i in range(J):
                        ins = mm(wide(2 * h)[:, c0:c1, :], TT[:, i, h * 128:h * 128 + 128], AH[:, i, c0 * P:c1 * P],
                                 start=(i == 0), stop=(i == J - 1))
                ins.then_inc(done, 1)

            for l in range(3):
                if l > 0:
                    pe.wait_ge(S["h_act"], l)
                    pe.wait_ge(S["h_dve"], l)
                for j in range(J):
                    for h in range(2):
                        o = W_AT["gcn_W"][0] + l * D
                        ins = mm(yv(j), XT[:, h, j * P:j * P + P], wmat[:, h, o:o + D], start=(h == 0), stop=(h == 1))
                ins.then_inc(S["t_ready"], 1)
                pe.wait_ge(S["t_act"], l + 1)
                pe.wait_ge(S["t_dve"], l + 1)
                if l < 2:
                    for h in range(2):
                        aggregate(h, 256, S["agg_psum"])
                else:
                    for j in range(J):
                        for i in range(J):
                            ins = mm(yv(j), AH[:, i, j * P:j * P + P], TT[:, i, :], start=(i == 0), stop=(i == J - 1))
                    ins.then_inc(S["last_psum"], 1)

            def z(b):
                return big[0:P, b, :].rearrange("p (j n) -> p j n", j=J)

            layernorm(3)
            project("W_gat", [v[:, 0:16] for v in small], S["gat_h"])
            pe.wait_ge(S["gat_a"], 1)
            for h in range(4):
                if h >= 2:
                    pe.wait_ge(S["row_read"], h - 1)
                spread(2 * (h % 2), lambda j: asrc[:, j, h:h + 1].to_broadcast([P, P]), P, S["row_psum"])
            pe.wait_ge(S["gat_a"], 2)

            def two_rows(h):
                if h:
                    pe.wait_ge(S["gat_sum"], h)
                spread(0, lambda j: adst[:, j, h:h + 1].to_broadcast([P, P]), P, S["rows2_psum"])
                if h:
                    pe.wait_ge(S["gat_sub"], h)
                spread(2, lambda j: bmax[:, j, h:h + 1].to_broadcast([P, P]), P, S["rows2_psum"])
            two_rows(0)
            for h in range(4):
                if h < 3:
                    two_rows(h + 1)
                pe.wait_ge(S["gat_mul"], h + 1)
                for i in range(J):
                    for j in range(J):
                        ins = mm(PS[0:P, 7, (i * 4 + h) * 5:(i * 4 + h) * 5 + 5], z(h)[:, j, i * P:i * P + P],
                                 hx[:, j, h, :], start=(j == 0), stop=(j == J - 1))
                ins.then_inc(S["gat_mm"], 1)
            gate_rows(1, 16)
            ffn(1)

            layernorm(4)
            project("W_heads", [PS[0:P, 3 + j, :] for j in range(J)], S["hh_psum"])
            pe.wait_ge(S["s_ready"], 1)

            def head_row(h):
                if h >= 2:
                    pe.wait_ge(S["relu_dve" if h % 2 else "relu_act"], h // 2)
                spread(2 * (h % 2), lambda j: asrc[:, j, h:h + 1].to_broadcast([P, P]), P, S["head_row"])
            head_row(0)
            head_row(1)
            for h in range(8):
                if h < 6:
                    head_row(h + 2)
                pe.wait_ge(S["head_mul"], h + 1)
                if h >= 2:
                    pe.wait_ge(S["head_out"], h - 1)
                for i in range(J):
                    for j in range(J):
                        ins = mm(PS[0:P, 4 + h % 2, i * 64:i * 64 + 64], z(h % 4)[:, j, i * P:i * P + P],
                                 HA[:, j, h * 64:h * 64 + 64], start=(j == 0), stop=(j == J - 1))
                ins.then_inc(S["head_psum"], 1)
            pe.wait_ge(S["x2_ready"], 1)
            x2t = big[:, 3, 0:2500].rearrange("p (k n) -> p k n", k=4)
            for k in range(4):
                if k >= 2:
                    pe.wait_ge(S["x2_dve" if k % 2 else "x2_act"], k // 2)
                for j in range(J):
                    ins = nc.tensor.transpose(wide(2 * (k % 2))[:, j, :], HB_[:, j, k * 128:k * 128 + 128], idn)
                ins.then_inc(S["x2_psum"], 1)
            pe.wait_ge(S["x2_act"], 2)
            pe.wait_ge(S["x2_dve"], 2)
            for j in range(J):
                for k in range(4):
                    ins = mm(yv(j), x2t[:, k, j * P:j * P + P], wout[:, k, :], start=(k == 0), stop=(k == 3))
            ins.then_inc(S["ho_psum"], 1)
            pe.wait_ge(S["so_ready"], 1)
            spread(0, lambda j: asrc[:, j, 0:1].to_broadcast([P, P]), P, S["o_row"])
            pe.wait_ge(S["o_mul"], 1)
            for i in range(J):
                for j in range(J):
                    ins = mm(yv(i), z(0)[:, j, i * P:i * P + P], TT[:, j, :], start=(j == 0), stop=(j == J - 1))
            ins.then_inc(S["o_psum"], 1)

            layernorm(5)
            project("Wg", [v[:, 0:8] for v in small], S["logits_ready"])
            gate_rows(2, 20)
            ffn(2)

            layernorm(6)
            tps = PS[0:P, 4:6, :].rearrange("p b c -> p (b c)")
            project("W_conv", [tps[:, 128 * j:128 * j + 128] for j in range(J)], S["t_ready"])
            pe.wait_ge(S["t_act"], 4)
            aggregate(0, 128, S["agg_psum"])
            pe.wait_ge(S["h_act"], 3)
            for j in range(J):
                ins = mm(yv(j), XT[:, 0, j * P:j * P + P], wlin[:], start=True, stop=True)
            ins.then_inc(S["last_psum"], 1)

            layernorm(7)
            project("wr", [PS[0:P, 7, j:j + 1] for j in range(J)], S["logits_ready"])
            pe.wait_ge(S["w_col"], 1)
            for j in range(J):
                ins = nc.tensor.transpose(wide(0, 1)[:, j, :], s5a[:, j:j + 1], idn)
            ins.then_inc(S["w_row_psum"], 1)
            pe.wait_ge(S["w_row_sb"], 1)
            ffn(3)

        @block.vector
        def _(dve):
            v = nc.vector
            step = [0]

            def link(ins):
                step[0] += 1
                ins.then_inc(S["vector_step"], 1)
                dve.wait_ge(S["vector_step"], step[0])

            def split(parts, x, rest):
                link(v.tensor_copy(parts[0], x))
                link(v.tensor_tensor(rest, x, parts[0], ALU.subtract))
                link(v.tensor_copy(parts[1], rest))
                link(v.tensor_tensor(parts[2], rest, parts[1], ALU.subtract))

            def moments(src):
                for j in range(J):
                    ins = v.bn_stats(stats[:, j, :], src(j))
                link(ins)
                for j in range(J):
                    ins = v.bn_aggr(mv[:, j, :], stats[:, j, :])
                link(ins)

            def layernorm(k):
                moments(lambda j: X[:, j, :])
                v.tensor_scalar_add(veps[:], mv[:, :, 1], EPS).then_inc(S["var_ready"], 1)
                dve.wait_ge(S["std_ready"], k + 1)
                link(v.reciprocal(rstd[:], std[:]))
                for j in range(J):
                    ins = v.tensor_scalar(XN[:, j, :], X[:, j, :], mv[:, j, 0:1], rstd[:, j:j + 1], ALU.subtract,
                                          ALU.mult)
                    ins.then_inc(S["ln_rows"], 1)
                dve.wait_ge(S["xt_psum"], 2 * k + 2)
                v.tensor_copy(blocks(XT[:, 1, :]), wide(2)).then_inc(S["xt_sb"], 1)

            dve.wait_ge(S["consts"], NCONST)
            dve.wait_ge(S["x_in"], 16)
            layernorm(0)

            dve.wait_ge(S["l0_in"], 64)
            v.tensor_scalar_add(foldS, row("v"), EPS).then_inc(S["fold_var"], 1)
            dve.wait_ge(S["fold_std"], 1)
            link(v.reciprocal(foldS, foldS))
            link(v.tensor_tensor(foldS, foldS, row("g"), ALU.mult))
            link(v.tensor_tensor(foldT, row("b"), row("m"), ALU.subtract))
            link(v.tensor_tensor(foldT, foldT, foldS, ALU.mult))
            link(v.tensor_tensor(foldT, foldT, row("be"), ALU.add))
            for n, o in ((0, 4), (1, 264)):
                link(v.tensor_tensor(w2v[:, n, 0:D], w2rows[:, n, :], foldS[0:32, o:o + D], ALU.mult))
                link(v.scalar_tensor_tensor(out=w2v[:, n, 0:D], in0=foldT[0:32, o:o + D], scalar=part[:, 3:4],
                                            in1=w2v[:, n, 0:D], op0=ALU.mult, op1=ALU.add))
                link(v.tensor_copy(w2v[:, n, D:D + 1], part[:, 3:4]))
            link(v.tensor_copy(w2h, w2v))
            link(v.tensor_tensor(w2r, w2v, w2h, ALU.subtract))
            link(v.tensor_copy(w2m, w2r))
            link(v.tensor_tensor(w2r, w2r, w2m, ALU.subtract))
            link(v.tensor_scalar(w2r, w2r, part[:, 2:3], None, ALU.mult))
            link(v.scalar_tensor_tensor(out=w2r, in0=w2m, scalar=part[:, 1:2], in1=w2r, op0=ALU.mult,
                                        op1=ALU.add))
            link(v.scalar_tensor_tensor(out=w2s[:], in0=w2h, scalar=part[:, 0:1], in1=w2r, op0=ALU.mult,
                                        op1=ALU.add))
            dve.wait_ge(S["table_ready"], 1)
            link(v.tensor_copy(TAB[:], PS[0:P, 4, 0:80].rearrange("p (j c) -> p j c", c=16)[:, :, 0:14]))

            dve.wait_ge(S["idx_in"], 64)
            link(v.tensor_copy(id1[:], idx1))
            link(v.tensor_tensor(inside, id1[:, 1, :], bounds[:, 0, :], ALU.is_ge))
            link(v.tensor_tensor(inside2, id1[:, 1, :], bounds[:, 1, :], ALU.is_lt))
            link(v.tensor_tensor(inside, inside, inside2, ALU.mult))
            link(v.tensor_reduce(usual[0:P, 0:1], inside, AX, ALU.min))
            link(v.tensor_copy(rest2, idx2))
            link(v.tensor_scalar(rest2[:, 0, :], rest2[:, 0, :], float(N - 1), 1.0, ALU.min, ALU.add))
            link(v.scalar_tensor_tensor(out=key, in0=rest2[:, 1, :], scalar=float(N), in1=rest2[:, 0, :],
                                        op0=ALU.mult, op1=ALU.add))
            link(v.tensor_scalar(rest2[:, 1, :], rest2[:, 1, :], N - 0.5, None, ALU.is_lt))
            link(v.tensor_tensor(key, key, rest2[:, 1, :], ALU.mult))
            link(v.tensor_scalar(key, key, -1.0, None, ALU.add))
            for r in range(ROUNDS):
                link(v.max(out=top[:, 8 * r:8 * r + 8], in_=key))
                link(v.match_replace(out=key, in_to_replace=top[:, 8 * r:8 * r + 8], in_values=key, imm_value=-1.0))

            def decode(ids, keys):
                ROUND = 1.5 * 2.0 ** 23
                link(v.tensor_scalar(ids[:, 1, :], keys, 1.0 / N, -0.5 + 0.5 / N, ALU.mult, ALU.add))
                link(v.tensor_scalar(ids[:, 1, :], ids[:, 1, :], ROUND, None, ALU.add))
                link(v.tensor_scalar(ids[:, 1, :], ids[:, 1, :], -ROUND, None, ALU.add))
                link(v.scalar_tensor_tensor(out=ids[:, 0, :], in0=ids[:, 1, :], scalar=-float(N), in1=keys,
                                            op0=ALU.mult, op1=ALU.add))
            decode(id2, top)
            decode(rest2, key)
            link(v.tensor_reduce(usual[:, 1:2], key, AX, ALU.max))
            link(v.tensor_scalar(usual[:, 1:2], usual[:, 1:2], 0.0, None, ALU.is_lt))
            s_ge, s_lt = scr2[:, 0, 0:TOP], scr2[:, 1, 0:TOP]
            link(v.tensor_tensor(s_ge, id2[:, 1, :], bounds2[:, 0, :], ALU.is_ge))
            link(v.tensor_scalar(s_lt, id2[:, 1, :], 0.0, None, ALU.is_lt))
            link(v.tensor_tensor(s_ge, s_ge, s_lt, ALU.max))
            link(v.tensor_tensor(s_lt, id2[:, 1, :], bounds2[:, 1, :], ALU.is_lt))
            link(v.tensor_tensor(s_ge, s_ge, s_lt, ALU.mult))
            v.tensor_reduce(usual[:, 2:3], s_ge, AX, ALU.min).then_inc(S["usual_ready"], 1)
            dve.wait_ge(S["usual_psum"], 1)
            v.tensor_scalar(is_usual[:], PS[0:1, 7, 0:3], 128 - 0.5, None, ALU.is_gt).then_inc(S["usual_known"], 1)
            dve.wait_ge(S["usual_known"], 1)
            none_left = dve.value_load(is_usual[:, 1:2], min_val=0, max_val=1)

            def onehots(ids, t, u, rows_, sides, wait):
                if wait is not None:
                    dve.wait_ge(S["onehot_used"], wait)
                for sd in sides:
                    ins = v.tensor_scalar(onehot[0:rows_, u, sd, 0:N], node_iota[0:rows_, :], ids[0:rows_, sd, ds(t, 1)],
                                          None, ALU.is_equal)
                ins.then_inc(S["onehot_ready"], 1)
            with dve.If(none_left < 1):
                def rest_onehots(i, first):
                    for u in range(4):
                        if not first:
                            dve.wait_ge(S["rest_used"], 4 * i + u - 3)
                        for sd in range(2):
                            ins = v.tensor_scalar(onehot[:, u, sd, 0:N], node_iota[:], rest2[:, sd, ds(4 * i + u, 1)],
                                                  None, ALU.is_equal)
                        ins.then_inc(S["rest_onehot"], 1)
                rest_onehots(0, True)
                with dve.Fori(1, NT2 // 4) as i:
                    rest_onehots(i, False)
                dve.wait_ge(S["rest_used"], NT2)
            for u in range(4):
                onehots(id2, u, u, 128, (0, 1), None)
            with dve.Fori(1, TOP // 4) as i:
                for u in range(4):
                    onehots(id2, 4 * i + u, u, 128, (0, 1), 4 * i + u - 3)
            with dve.Fori(0, NT1 // 4) as i:
                for u in range(4):
                    onehots(id1, 4 * i + u, u, P, (0, 1), 4 * i + u + TOP - 3)

            def z(b):
                return big[0:P, b, :].rearrange("p (j n) -> p j n", j=J)

            dve.wait_ge(S["counts_out"], 2)
            link(v.tensor_scalar(z(0), C1[:], 0.0, ABSENT, ALU.is_equal, ALU.mult))
            dve.wait_ge(S["a1_row"], 1)

            def masked_max(dst, mask, scratch, scores):
                for j in range(J):
                    ins = v.tensor_tensor_reduce(out=blocks(scratch[:, j, :]), in0=blocks(mask[:, j, :]), in1=scores,
                                                 scale=1.0, scalar=-3e38, op0=ALU.add, op1=ALU.max, accum_out=dst[j])
                return ins
            link(masked_max([s5a[:, j:j + 1] for j in range(J)], z(0), z(1), wide(0, P)))
            link(v.tensor_tensor(s5a[:], s5a[:], TAB[:, :, 13], ALU.add))
            link(v.scalar_tensor_tensor(out=tabf[:, 1, :, 9], in0=s5a[:], scalar=0.2, in1=s5a[:], op0=ALU.mult,
                                        op1=ALU.max))
            link(v.tensor_copy(tabf[:, 0, :, 0:9], TAB[:, :, 0:9]))
            link(v.tensor_copy(tabf[:, 1, :, 0:5], TAB[:, :, 9:14]))
            split([tab16[:, :, :, :, c] for c in range(3)], tabf[:], tabr[:])
            v.tensor_copy(s5b[:], s5a[:]).then_inc(S["tables_split"], 1)
            dve.wait_ge(S["tables_split"], 1)
            v.tensor_copy(s5b[:], s5a[:]).then_inc(S["edge_max_ready"], 1)

            def add_parts(t, u):
                dve.wait_ge(S["gT_psum"], t + 1)
                v.tensor_reduce(GS[:, ds(4 * t, 4), :], PS[0:P, 2 + u, 0:120].rearrange(
                    "p (q a b) -> p q a b", q=4, b=3), AX, ALU.add).then_inc(S["gather_read"], 1)

            def gathers(i, nodes):
                for u in range(2):
                    t = 2 * i + u
                    dve.wait_ge(S["rows_cast"], t + 1)
                    if not (isinstance(t, int) and t < 2):
                        dve.wait_ge(S["gathered"], t - 1)
                    for sd, j in [(0, j) for j in range(J)] + [(1, j) for j in nodes(u)]:
                        ins = v.tensor_scalar(onehotT[:, u, sd, j, :], idxrow16[:, u, 500 * sd:500 * sd + 500],
                                              node_id[0:P, j:j + 1], None, ALU.is_equal)
                    ins.then_inc(S["ids_onehot"], 1)
                    if not (isinstance(t, int) and t < 2):
                        add_parts(t - 2, u)
            in_order = dve.value_load(is_usual[:, 0:1], min_val=0, max_val=1)
            with dve.If(in_order > 0):
                chunk_loops(dve, gathers, True)
            with dve.Else():
                chunk_loops(dve, gathers, False)
            add_parts(38, 0)
            add_parts(39, 1)
            dve.wait_ge(S["gather_read"], 40)

            link(v.scalar_tensor_tensor(out=EX, in0=GS[:, :, 4], scalar=0.2, in1=GS[:, :, 4], op0=ALU.mult,
                                        op1=ALU.max))
            link(v.tensor_tensor(EX, EX, GS[:, :, 9], ALU.subtract))
            v.tensor_copy(s5b[:], s5a[:]).then_inc(S["logit_in"], 1)

            def stack(h, pre, o):
                link(v.tensor_tensor(h, pre, mid_b(foldS[0:P, o:o + 4], NT1), ALU.mult))
                link(v.tensor_tensor(h, h, mid_b(foldT[0:P, o:o + 4], NT1), ALU.add))
                link(v.scalar_tensor_tensor(out=h, in0=h, scalar=0.01, in1=h, op0=ALU.mult, op1=ALU.max))
                for c in range(3):
                    ins = v.tensor_copy(hs16[:, :, 4 * c:4 * c + 4], h)
                link(ins)
                link(v.tensor_tensor(h, h, hs16[:, :, 0:4], ALU.subtract))
                for c in range(3, 5):
                    ins = v.tensor_copy(hs16[:, :, 4 * c:4 * c + 4], h)
                link(ins)
                return v.tensor_tensor(hs16[:, :, 20:24], h, hs16[:, :, 12:16], ALU.subtract)
            stack(h1, GS[:, :, 0:4], 0).then_inc(S["h1_ready"], 1)

            def edge_relu(t, u):
                dve.wait_ge(S["fe_psum"], t + 1)
                v.tensor_scalar(EF[:, u, 1, :], PS[:, 3 + 2 * u, 0:500], 0.0, None, ALU.max).then_inc(S["ef_dve"], 1)

            def edge_add(t, u):
                dve.wait_ge(S["fn1_psum"], t + 1)
                v.tensor_tensor(FR[:, ds(4 * t, 4), :], PS[0:P, 6 + u, 0:16].rearrange("p (q c) -> p q c", q=4),
                                GS[:, ds(4 * t, 4), 5:9], ALU.add).then_inc(S["fn1_read"], 1)

            def loop_a(i, first):
                for u in range(2):
                    edge_relu(2 * i + u, u)
                    if not (first and u == 0):
                        edge_add(2 * i + u - 1, 1 - u)
            loop_a(0, True)
            with dve.Fori(1, 20) as i:
                loop_a(i, False)
            edge_add(39, 1)
            dve.wait_ge(S["fn1_read"], 40)
            stack(h2, FR, 260).then_inc(S["h2_ready"], 1)
            dve.wait_ge(S["edge_exp"], 1)

            def message(i, q, first):
                t = 8 * i + q
                onehots(id1, t, q % 4, P, (1,), None if first and q < 4 else TOP + NT1)
                dve.wait_ge(S["fn2_psum"], t + 1)
                v.tensor_scalar(msg[:, q % 4, :], PS[0:P, 6 + q % 2, 0:257], 0.0, EX[:, ds(t, 1)], ALU.max,
                                ALU.mult).then_inc(S["msg_ready"], 1)

            def loop_m(i, first):
                for q in range(8):
                    if not (first and q < 4):
                        dve.wait_ge(S["msg_used"], 8 * i + q - 3)
                    else:
                        dve.wait_ge(S["onehot_used"], TOP + NT1)
                    message(i, q, first)
            loop_m(0, True)
            with dve.Fori(1, 20) as i:
                loop_m(i, False)
            dve.wait_ge(S["msg_used"], NT1)
            for j in range(J):
                link(v.tensor_scalar(s5a[:, j:j + 1], PS[0:P, j, 256:257], 0.5, None, ALU.max))
            link(v.reciprocal(s5a[:], s5a[:]))
            for j in range(J):
                ins = v.scalar_tensor_tensor(out=XN[:, j, :], in0=PS[0:P, j, 0:D], scalar=s5a[:, j:j + 1],
                                             in1=XN[:, j, :], op0=ALU.mult, op1=ALU.add)
            link(ins)
            link(v.tensor_tensor(X[:], X[:], XN[:], ALU.add))

            def gate_rows(n, done):
                v.tensor_copy(s5b[:], s5a[:]).then_inc(S["gates_ready"], 1)
                E = FFN_EXPERTS[n]
                tiles = 16 if n == 0 else E
                dst = grow16 if n == 0 else grow
                dve.wait_ge(S["gt_psum"], n + 1)
                if n == 0:
                    v.tensor_copy(blocks(gateT16), wide(4, E))
                    v.tensor_copy(pair16.rearrange("p e (a b) -> p (e a) b", a=2), last_b(ident[0:32, 0:32], 64))
                v.tensor_copy(blocks(gateT[0:E, :]), wide(4, E)).then_inc(S["gt_sb"], 1)
                for e in range(1, tiles, 2):
                    dve.wait_ge(S["gr_psum"], done + e + 1)
                    v.tensor_copy(blocks(dst[:, e, :]), wide(2)).then_inc(S["gr_dve"], 1)
                dve.wait_ge(S["gr_dve"], (done + tiles) // 2)
                dve.wait_ge(S["gr_act"], (done + tiles) // 2)

            def gating(n):
                base, T = FFN_BASE[n], FFN_TILES[n]

                def body(i, first):
                    for u in range(4):
                        t = base + 4 * i + u
                        dve.wait_ge(S["h_sb"], t + 1)
                        if not (first and u < 2):
                            dve.wait_ge(S["y_used"], t - 1)
                        g = grow16[:, ds(4 * i + u, 1), :] if n == 0 else grow[:, ds(i, 1), :]
                        v.tensor_tensor(hidg[:, u % 2, :], hid[:, u % 2, :], g.rearrange("p a n -> p (a n)"), ALU.mult
                                        ).then_inc(S["h_gated"], 1)
                body(0, True)
                with dve.Fori(1, T // 4) as i:
                    body(i, False)
                dve.wait_ge(S["y_ready"], n + 1)

            def add_y():
                for j in range(J):
                    ins = v.tensor_tensor(X[:, j, :], X[:, j, :], yv(j), ALU.add)
                link(ins)

            def top_two(E, before, k):
                sc = s32a[:, :, 0:E]
                s3 = s320a[:, :, 0:E * E].rearrange("p j (e f) -> p j e f", e=E)
                s4 = s320b[:, :, 0:E * E].rearrange("p j (e f) -> p j e f", e=E)
                other = sc.unsqueeze(2).to_broadcast([P, J, E, E])
                own = sc.unsqueeze(3).to_broadcast([P, J, E, E])
                link(v.tensor_tensor(s3, other, own, ALU.is_equal))
                link(v.tensor_tensor(s3, s3, before[:].unsqueeze(1).to_broadcast([P, J, E, E]), ALU.mult))
                link(v.tensor_tensor(s4, other, own, ALU.is_gt))
                link(v.tensor_tensor(s3, s3, s4, ALU.add))
                rank = s32b[:, :, 0:E]
                link(v.tensor_reduce(rank, s3, AX, ALU.add))
                link(v.tensor_reduce(s5a[:], sc, AX, ALU.max))
                link(v.tensor_scalar(rank, rank, 1.5, None, ALU.is_lt))
                link(v.tensor_tensor(sc, sc, last_b(s5a[:], E), ALU.subtract))
                v.tensor_copy(s5b[:], s5a[:]).then_inc(S["sm_in"], 1)
                dve.wait_ge(S["sm_out"], k)
                link(v.tensor_tensor(sc, sc, rank, ALU.mult))
                link(v.tensor_reduce(s5a[:], sc, AX, ALU.add))
                link(v.reciprocal(s5a[:], s5a[:]))
                link(v.tensor_tensor(gate[:, :, 0:E], sc, last_b(s5a[:], E), ALU.mult))

            layernorm(1)
            small = PS[0:P, 7, 0:160].rearrange("p (j c) -> p j c", c=32)
            dve.wait_ge(S["logits_ready"], 1)
            link(v.tensor_tensor(s32a[:], small, mid_b(row("router_b"), J), ALU.add))
            link(v.tensor_reduce(s5a[:], s32a[:], AX, ALU.max))
            link(v.tensor_tensor(s32b[:], s32a[:], last_b(s5a[:], 32), ALU.is_equal))
            link(v.tensor_tensor(s32b[:], s32b[:], mid_b(rev32[:], J), ALU.mult))
            link(v.tensor_reduce(s5a[:], s32b[:], AX, ALU.max))
            link(v.tensor_tensor(gate[:], s32b[:], last_b(s5a[:], 32), ALU.is_equal))
            gate_rows(0, 0)
            gating(0)
            for j in range(J):
                ins = v.scalar_tensor_tensor(out=X[:, j, :], in0=yv(j), scalar=0.0, in1=X[:, j, :], op0=ALU.max,
                                             op1=ALU.add)
            link(ins)

            link(v.tensor_reduce(dinv[:], C1[:], AX, ALU.add))
            v.tensor_scalar_add(dinv[:], dinv[:], 1.0).then_inc(S["deg_ready"], 1)
            dve.wait_ge(S["deg_std"], 1)
            link(v.reciprocal(dinv[:], dinv[:]))
            for j in range(J):
                ins = v.tensor_scalar(z(2)[:, j, :], C1[:, j, :], dinv[:, j:j + 1], None, ALU.mult)
            link(ins)
            for j in range(J):
                dg = slice(j * P, j * P + P)
                v.scalar_tensor_tensor(out=z(2)[:, j, dg], in0=ident[0:P, 0:P], scalar=dinv[:, j:j + 1],
                                       in1=z(2)[:, j, dg], op0=ALU.mult, op1=ALU.add)
                ins = v.tensor_tensor(C2[:, j, dg], C2[:, j, dg], ident[0:P, 0:P], ALU.add)
            ins.then_inc(S["b_ready"], 1)
            for i in range(1, 10, 2):
                dve.wait_ge(S["bt_psum"], i + 1)
                if i < 5:
                    v.tensor_scalar(blocks(AH[:, i, :]), wide(2, P), dinv[:, i:i + 1], None, ALU.mult
                                    ).then_inc(S["bt_dve"], 1)
                else:
                    v.tensor_copy(blocks(C2T[:, i - 5, :]), wide(2, P)).then_inc(S["bt_dve"], 1)
            layernorm(2)
            tps = PS[0:P, 4:7, :].rearrange("p b c -> p (b c)")
            for l in range(3):
                dve.wait_ge(S["t_ready"], l + 1)
                v.tensor_copy(TT[:, 2:5, :], tps[:, 512:1280].rearrange("p (j c) -> p j c", c=D)
                              ).then_inc(S["t_dve"], 1)
                if l < 2:
                    dve.wait_ge(S["agg_psum"], 2 * l + 2)
                    v.tensor_scalar(blocks(XT[:, 1, :]), wide(2), cols[:, COL_GCN + 2 * l + 1:COL_GCN + 2 * l + 2],
                                    0.0, ALU.add, ALU.max).then_inc(S["h_dve"], 1)
            dve.wait_ge(S["last_psum"], 1)
            for j in range(J):
                ins = v.tensor_tensor(XN[:, j, :], yv(j), row("gcn_b2"), ALU.add)
            link(ins)
            link(v.scalar_tensor_tensor(out=X[:], in0=XN[:], scalar=0.0, in1=X[:], op0=ALU.max, op1=ALU.add))

            layernorm(3)
            dve.wait_ge(S["gat_h"], 1)
            link(v.tensor_copy(hx[:, :, :, 0:4], small[:, :, 0:16].rearrange("p j (h e) -> p j h e", h=4)))
            for name, dst in (("att_src", asrc), ("att_dst", adst)):
                link(v.tensor_tensor(s32a[:, :, 0:16], small[:, :, 0:16], mid_b(row(name), J), ALU.mult))
                link(v.tensor_reduce(dst[:, :, 0:4], s32a[:, :, 0:16].rearrange("p j (h e) -> p j h e", h=4), AX,
                                     ALU.add))
            v.tensor_copy(s5b[:], s5a[:]).then_inc(S["gat_a"], 1)
            link(v.tensor_scalar(z(2), C2[:], 0.0, ABSENT, ALU.is_equal, ALU.mult))
            for h in range(4):
                dve.wait_ge(S["row_psum"], h + 1)
                masked_max([mx[:, j, h:h + 1] for j in range(J)], z(2), z(3), wide(2 * (h % 2), P)
                           ).then_inc(S["row_read"], 1)
                dve.wait_ge(S["row_read"], h + 1)
            link(v.tensor_tensor(mx[:], mx[:], adst[:, :, 0:4], ALU.add))
            link(v.scalar_tensor_tensor(out=mx[:], in0=mx[:], scalar=0.2, in1=mx[:], op0=ALU.mult, op1=ALU.max))
            link(v.tensor_scalar(pa02[:], asrc[:, :, 0:4], 0.2, None, ALU.mult))
            v.scalar_tensor_tensor(out=bmax[:], in0=adst[:, :, 0:4], scalar=0.2, in1=mx[:], op0=ALU.mult,
                                   op1=ALU.subtract).then_inc(S["gat_a"], 1)

            def sub_max(h):
                dve.wait_ge(S["rows2_psum"], 2 * h + 2)
                dve.wait_ge(S["gat_sum"], h + 1)
                for j in range(J):
                    zj = blocks(z(h)[:, j, :])
                    ins = v.scalar_tensor_tensor(out=zj, in0=zj, scalar=0.8, in1=wide(2, P), op0=ALU.mult,
                                                 op1=ALU.add)
                ins.then_inc(S["gat_sub"], 1)

            sub_max(0)
            for h in range(4):
                if h < 3:
                    sub_max(h + 1)
                dve.wait_ge(S["gat_exp"], h + 1)
                v.tensor_tensor(z(h), z(h), C2T[:], ALU.mult).then_inc(S["gat_mul"], 1)
            dve.wait_ge(S["gat_mm"], 4)
            agg = PS[0:P, 7, 0:100].rearrange("p (i c) -> p i c", c=5)
            den = s40a[:, 0:20]
            g16 = s320a[:, :, 0:16]
            g20 = g16.rearrange("p j (h e) -> p j h e", h=4)
            link(v.tensor_scalar(den, agg[:, :, 4], 1e-16, None, ALU.add))
            link(v.reciprocal(den, den))
            link(v.tensor_tensor(g20, PS[0:P, 7, 0:100].rearrange("p (j h c) -> p j h c", j=J, c=5)[:, :, :, 0:4],
                                 den.rearrange("p (j h) -> p j h", j=J).unsqueeze(3).to_broadcast([P, J, 4, 4]),
                                 ALU.mult))
            link(v.tensor_tensor(g16, g16, mid_b(row("b_gat"), J), ALU.add))
            moments(lambda j: s320a[:, j, 0:16])
            v.tensor_scalar_add(s5a[:], mv[:, :, 1], EPS).then_inc(S["gat_var"], 1)
            dve.wait_ge(S["gat_std"], 1)
            link(v.reciprocal(s5a[:], s5a[:]))
            for j in range(J):
                ins = v.tensor_scalar(s320a[:, j, 0:16], s320a[:, j, 0:16], mv[:, j, 0:1], s5a[:, j:j + 1],
                                      ALU.subtract, ALU.mult)
            link(ins)
            link(v.tensor_tensor(g16, g16, mid_b(row("ln_gamma"), J), ALU.mult))
            link(v.tensor_tensor(g16, g16, mid_b(row("ln_beta"), J), ALU.add))
            link(v.tensor_reduce(s32a[:, :, 0:4], g16.rearrange("p j (h e) -> p j e h", h=4), AX, ALU.add))
            link(v.tensor_scalar(s32a[:, :, 0:4], s32a[:, :, 0:4], 0.25, None, ALU.mult))
            top_two(4, before4, 1)
            gate_rows(1, 16)
            gating(1)
            add_y()

            layernorm(4)
            dve.wait_ge(S["hh_psum"], 1)
            for j in range(J):
                ins = v.tensor_tensor(HA[:, j, :], PS[0:P, 3 + j, :], row("b_heads"), ALU.add)
            link(ins)
            tmp = z(2).rearrange("p j n -> p (j n)")[:, 0:J * 512].rearrange("p (j n) -> p j n", j=J)
            for name, dst in (("a_src", asrc), ("a_dst", adst)):
                link(v.tensor_tensor(tmp, HA, mid_b(row(name), J), ALU.mult))
                link(v.tensor_reduce(dst[:], tmp.rearrange("p j (h e) -> p j h e", h=8), AX, ALU.add))
            v.tensor_scalar(nb02[:], adst[:], -0.2, None, ALU.mult).then_inc(S["s_ready"], 1)

            dve.wait_ge(S["esrc_ready"], 1)

            def head_out(h):
                dve.wait_ge(S["head_psum"], h + 1)
                v.tensor_tensor(HB_[:, :, h * 64:h * 64 + 64], PS[0:P, 4 + h % 2, 0:320].rearrange(
                    "p (i c) -> p i c", c=64), last_b(esrc[:, :, h], 64), ALU.mult).then_inc(S["head_out"], 1)

            def head_relu(h):
                dve.wait_ge(S["head_row"], h + 1)
                if h >= 4:
                    dve.wait_ge(S["head_psum"], h - 3)
                for j in range(J):
                    ins = v.tensor_scalar(blocks(z(h % 4)[:, j, :]), wide(2, P), adst[:, j, h:h + 1], 0.0, ALU.add,
                                          ALU.max)
                ins.then_inc(S["relu_dve"], 1)
            for h in range(8):
                if h % 2 == 0:
                    head_relu(h + 1)
                dve.wait_ge(S["head_exp"], h + 1)
                v.tensor_tensor(z(h % 4), z(h % 4), C1[:], ALU.mult).then_inc(S["head_mul"], 1)
                if h >= 1:
                    head_out(h - 1)
            head_out(7)
            dve.wait_ge(S["head_out"], 8)
            hp = HB_.rearrange("p j (h e) -> p (j h) e", h=8)
            hq = HA.rearrange("p j (h e) -> p (j h) e", h=8)
            link(v.tensor_reduce(s40a[:], hp, AX, ALU.add))
            link(v.tensor_scalar(s40a[:], s40a[:], 1.0 / 64, None, ALU.mult))
            link(v.tensor_tensor(hp, hp, last_b(s40a[:], 64), ALU.subtract))
            link(v.tensor_tensor(hq, hp, hp, ALU.mult))
            link(v.tensor_reduce(s40a[:], hq, AX, ALU.add))
            v.tensor_scalar(s40a[:], s40a[:], 1.0 / 64, EPS, ALU.mult, ALU.add).then_inc(S["hln_var"], 1)
            dve.wait_ge(S["hln_std"], 1)
            link(v.reciprocal(s40a[:], s40a[:]))
            link(v.tensor_tensor(hp, hp, last_b(s40a[:], 64), ALU.mult))
            link(v.tensor_tensor(HB_, HB_, mid_b(row("g_heads"), J), ALU.mult))
            link(v.tensor_tensor(HB_, HB_, mid_b(row("beta_heads"), J), ALU.add))
            v.tensor_scalar(HA, HB_, 0.0, None, ALU.min).then_inc(S["elu_in"], 1)
            dve.wait_ge(S["elu_in"], 1)
            dve.wait_ge(S["elu_exp"], 1)
            link(v.tensor_scalar(HA, HA, -1.0, None, ALU.add))
            v.scalar_tensor_tensor(out=HB_, in0=HB_, scalar=0.0, in1=HA, op0=ALU.max, op1=ALU.add
                                   ).then_inc(S["x2_ready"], 1)
            x2t = big[:, 3, 0:2500].rearrange("p (k n) -> p k n", k=4)
            for k in range(1, 4, 2):
                dve.wait_ge(S["x2_psum"], k + 1)
                v.tensor_copy(blocks(x2t[:, k, :]), wide(2)).then_inc(S["x2_dve"], 1)
            dve.wait_ge(S["ho_psum"], 1)
            for j in range(J):
                ins = v.tensor_tensor(TT[:, j, :], yv(j), row("b_out"), ALU.add)
            link(ins)
            for name, dst in (("a_out_src", asrc), ("a_out_dst", adst)):
                link(v.tensor_tensor(XN[:], TT[:], mid_b(row(name), J), ALU.mult))
                link(v.tensor_reduce(dst[:, :, 0], XN[:], AX, ALU.add))
            v.tensor_scalar(nb02[:, :, 0], adst[:, :, 0], -0.2, None, ALU.mult).then_inc(S["so_ready"], 1)
            dve.wait_ge(S["o_exp"], 1)
            v.tensor_tensor(z(0), z(0), C1[:], ALU.mult).then_inc(S["o_mul"], 1)
            dve.wait_ge(S["o_psum"], 1)
            dve.wait_ge(S["esrc_ready"], 2)
            for j in range(J):
                ins = v.tensor_scalar(TT[:, j, :], yv(j), esrc[:, j, 0:1], None, ALU.mult)
            link(ins)
            moments(lambda j: TT[:, j, :])
            v.tensor_scalar_add(veps[:], mv[:, :, 1], EPS).then_inc(S["hln_var"], 1)
            dve.wait_ge(S["hln_std"], 2)
            link(v.reciprocal(rstd[:], std[:]))
            for j in range(J):
                ins = v.tensor_scalar(TT[:, j, :], TT[:, j, :], mv[:, j, 0:1], rstd[:, j:j + 1], ALU.subtract, ALU.mult)
            link(ins)
            link(v.tensor_tensor(TT[:], TT[:], mid_b(row("g_out"), J), ALU.mult))
            link(v.tensor_tensor(TT[:], TT[:], mid_b(row("beta_out"), J), ALU.add))
            v.tensor_scalar(XN[:], TT[:], 0.0, None, ALU.min).then_inc(S["oelu_in"], 1)
            dve.wait_ge(S["oelu_exp"], 1)
            link(v.tensor_scalar(XN[:], XN[:], -1.0, None, ALU.add))
            link(v.scalar_tensor_tensor(out=XN[:], in0=TT[:], scalar=0.0, in1=XN[:], op0=ALU.max, op1=ALU.add))
            link(v.tensor_tensor(X[:], X[:], XN[:], ALU.add))

            layernorm(5)
            dve.wait_ge(S["logits_ready"], 2)
            link(v.tensor_tensor(s32a[:, :, 0:8], small[:, :, 0:8], mid_b(row("bg"), J), ALU.add))
            link(v.tensor_tensor(s32a[:, :, 0:8], s32a[:, :, 0:8], mid_b(row("bias"), J), ALU.add))
            top_two(8, before8, 2)
            gate_rows(2, 20)
            gating(2)
            add_y()

            layernorm(6)
            dve.wait_ge(S["last_psum"], 2)
            add_y()
            link(v.tensor_tensor(X[:], X[:], mid_b(row("b_lin"), J), ALU.add))

            layernorm(7)
            dve.wait_ge(S["logits_ready"], 3)
            v.tensor_scalar(s5a[:], PS[0:P, 7, 0:5], row("br"), None, ALU.add).then_inc(S["w_col"], 1)
            dve.wait_ge(S["w_col"], 1)
            dve.wait_ge(S["w_bcast"], 1)
            dve.wait_ge(S["tri_ready"], 2)
            for j in range(J):
                link(v.tensor_scalar(z(1)[:, j, :], wrow, s5a[:, j:j + 1], None, ALU.is_gt))
                link(v.scalar_tensor_tensor(out=z(2)[:, j, :], in0=wrow, scalar=s5a[:, j:j + 1], in1=z(0)[:, j, :],
                                            op0=ALU.is_equal, op1=ALU.mult))
            link(v.tensor_tensor(z(1), z(1), z(2), ALU.add))
            link(v.tensor_reduce(s5b[:], z(1), AX, ALU.add))
            link(v.tensor_scalar(s5b[:], s5b[:], int(0.5 * N) - 1 - 0.5, None, ALU.is_lt))
            link(v.tensor_tensor(s5b[:], s5b[:], s5a[:], ALU.mult))
            link(v.tensor_tensor(X[:], X[:], XN[:], ALU.add))
            dve.wait_ge(S["y_ready"], 4)
            for j in range(J):
                ins = v.scalar_tensor_tensor(out=X[:, j, :], in0=yv(j), scalar=s5b[:, j:j + 1], in1=X[:, j, :],
                                             op0=ALU.mult, op1=ALU.add)
            ins.then_inc(S["x_final"], 1)


def kernel(**inputs):
    import concourse.bacc as _bacc
    from concourse import mybir as _mybir
    from concourse.bass_utils import run_bass_kernel_spmd as _run

    i = {k: np.asarray(v) for k, v in inputs.items()}
    w1 = np.concatenate([i["L0_ffn_W1"].transpose(1, 0, 2).reshape(D, -1), i["L1_ffn_W1"].transpose(1, 0, 2).reshape(D, -1),
                         i["L2_ffn_W1"].transpose(1, 0, 2).reshape(D, -1), i["L3_ffn_w1"]], axis=1)
    w2 = np.concatenate([i["L0_ffn_W2"].reshape(-1, D), i["L1_ffn_W2"].reshape(-1, D), i["L2_ffn_W2"].reshape(-1, D),
                         i["L3_ffn_w2"]], axis=0)
    T = sum(FFN_TILES)
    w1 = w1.reshape(2, 128, T, 128).transpose(2, 1, 0, 3).reshape(T, 128, 256)
    wffn = np.concatenate([w1, w2.reshape(T, 128, 256)], axis=2)
    fe1, fn1 = i["L0_gnn_fe_W1"], i["L0_gnn_fn_W1"]
    table = np.concatenate([fe1[:D], i["L0_gnn_attn_l"][:, None], fn1[:D], fe1[D:], i["L0_gnn_attn_r"][:, None]], axis=1)
    wmat = np.concatenate([table, fn1[D:], i["L0_ffn_router_w"].T, i["L1_ffn_W_gat"], i["L2_ffn_Wg"], i["L3_ffn_wr"],
                           i["L3_gnn_W_conv"], i["L2_gnn_W_heads"].reshape(512, D).T,
                           i["L1_gnn_W"].transpose(1, 0, 2).reshape(D, 768)], axis=1)
    wmat = wmat.reshape(2, 128, WCOLS).transpose(1, 0, 2)
    f = {}
    for k, n in (("b", "b"), ("g", "g"), ("be", "be"), ("m", "m"), ("v", "v")):
        f[k] = np.concatenate([i[f"L0_gnn_fe_{n}1"], i[f"L0_gnn_fe_{n}2"], i[f"L0_gnn_fn_{n}1"], i[f"L0_gnn_fn_{n}2"]])
    f["router_b"] = i["L0_ffn_router_b"]
    f["gcn_b2"] = i["L1_gnn_b"][2]
    for n in ("att_src", "att_dst", "b_gat", "ln_gamma", "ln_beta"):
        f[n] = i["L1_ffn_" + n].reshape(-1)
    for n in ("b_heads", "g_heads", "beta_heads", "b_out", "g_out", "beta_out"):
        f[n] = i["L2_gnn_" + n].reshape(-1)
    f["a_src"], f["a_dst"] = i["L2_gnn_a_heads"][:, :64].reshape(-1), i["L2_gnn_a_heads"][:, 64:].reshape(-1)
    f["a_out_src"], f["a_out_dst"] = i["L2_gnn_a_out"][:D], i["L2_gnn_a_out"][D:]
    f["bg"], f["bias"], f["b_lin"], f["br"] = i["L2_ffn_bg"], i["L2_ffn_bias"], i["L3_gnn_b_lin"], i["L3_ffn_br"]
    rows = np.concatenate([f[n] for n, _ in ROW_SIZES])[None]
    cols = np.concatenate([i["L0_ffn_b1"].reshape(-1), i["L1_ffn_b1"].reshape(-1), i["L2_ffn_b1"].reshape(-1),
                           i["L3_ffn_b1"], i["L1_gnn_b"][:2].reshape(-1), i["L3_gnn_b_conv"]]).reshape(COLS, 128).T
    w2rows = np.zeros((32, 2, D), np.float32)
    w2rows[:24, 0] = np.tile(i["L0_gnn_fe_W2"], (6, 1))
    w2rows[:24, 1] = np.tile(i["L0_gnn_fn_W2"], (6, 1))
    part = np.zeros((32, 4), np.float32)
    part[[0, 1, 2, 3, 12, 13, 14, 15, 20, 21, 22, 23, 24], 0] = 1
    part[[4, 5, 6, 7, 16, 17, 18, 19, 25], 1] = 1
    part[[8, 9, 10, 11, 26], 2] = 1
    part[24:27, 3] = 1
    b2 = np.zeros((32, 4, D), np.float32)
    for n, k in enumerate(("L0_ffn_b2", "L1_ffn_b2", "L2_ffn_b2", "L3_ffn_b2")):
        v = i[k].reshape(-1, D)
        b2[:v.shape[0], n] = v
    sd = np.stack([i["src"], i["dst"]])
    idx1 = sd.reshape(2, NT1, P).transpose(2, 0, 1)
    idx2 = i["L1_ffn_edge_index"].reshape(2, 128, NT2).transpose(1, 0, 2)
    idxrow = sd.reshape(2, 40, 500).transpose(1, 0, 2).reshape(40, 1000)
    bounds = np.array([[P * min(usual_node_tiles(t)) for t in range(NT1)],
                       [P * (max(usual_node_tiles(t)) + 1) for t in range(NT1)]], np.float32)
    tiles2 = [usual_node_tiles2(r) for r in range(TOP)]
    bounds2 = np.array([[P * t[0] for t in tiles2], [P * (t[-1] + 1) for t in tiles2]], np.float32)
    arrays = {"x": i["x"], "bounds2": bounds2, "bounds": bounds, "idx1": idx1, "idx2": idx2, "idxrow": idxrow, "wmat": wmat, "w2rows": w2rows, "part": part,
              "rows": rows, "cols": cols, "wout": i["L2_gnn_W_out"].T, "wlin": i["L3_gnn_W_lin"], "b2": b2, "wffn": wffn}

    nc = _bacc.Bacc("TRN2", target_bir_lowering=False, num_devices=1)
    feed, args = {}, {}
    for n, v in arrays.items():
        v = np.ascontiguousarray(v)
        feed[f"in_{n}"] = v
        args[n] = nc.dram_tensor(f"in_{n}", v.shape, _mybir.dt.from_np(v.dtype), kind="ExternalInput").ap()
    out = nc.dram_tensor("out_x", (N, D), _mybir.dt.float32, kind="ExternalOutput").ap()
    gnn_ffn_program(nc, args, out)
    r = _run(nc, [feed], core_ids=[0])
    return r.results[0]["out_x"]
```

```python
import numpy as np

N, P, J, D = 625, 125, 5, 256
E1, E2 = 20000, 32768
NT1, NT2 = E1 // 125, E2 // 128
FFN_TILES = [16, 16, 32, 8]
FFN_BASE = [0, 16, 32, 64]
FFN_EXPERTS = [32, 4, 8, 1]
ROW_SIZES = [("b", 520), ("g", 520), ("be", 520), ("m", 520), ("v", 520),
             ("router_b", 32), ("gcn_b2", 256),
             ("att_src", 16), ("att_dst", 16), ("b_gat", 16), ("ln_gamma", 16), ("ln_beta", 16),
             ("b_heads", 512), ("a_src", 512), ("a_dst", 512), ("g_heads", 512), ("beta_heads", 512),
             ("b_out", 256), ("a_out_src", 256), ("a_out_dst", 256), ("g_out", 256), ("beta_out", 256),
             ("bg", 8), ("bias", 8), ("b_lin", 256), ("br", 1)]
ROW_AT, _at = {}, 0
for _n, _s in ROW_SIZES:
    ROW_AT[_n] = (_at, _s)
    _at += _s
ROWS, ROWS_L0 = _at, 2600
W_SIZES = [("table", 14), ("fn_W1b", 4), ("router", 32), ("W_gat", 16), ("Wg", 8), ("wr", 1), ("W_conv", 128),
           ("W_heads", 512), ("gcn_W", 768)]
W_AT, _at = {}, 0
for _n, _s in W_SIZES:
    W_AT[_n] = (_at, _s)
    _at += _s
WCOLS = _at
COL_FFN = [0, 16, 32, 64]
COL_GCN, COL_CONV, COLS = 72, 76, 77


SEAM = 4
TILES_PER_NODE_TILE = NT1 // J


def usual_node_tiles(t):
    m, at = divmod(t, TILES_PER_NODE_TILE)
    return [k for k, near in ((m - 1, at < SEAM), (m, True), (m + 1, at >= TILES_PER_NODE_TILE - SEAM))
            if near and 0 <= k < J]


ROUNDS = 15
TOP = 8 * ROUNDS


def usual_node_tiles2(r):
    lo = (375, 250, 125, 125)[r // 8] if r < 32 else 0
    hi = 625 if r < 40 else 500 if r < 64 else 375 if r < 80 else 250 if r < 104 else 125
    return list(range(lo // P, hi // P))


def gnn_ffn_program(nc, a, out):
    import concourse.bass as bass
    from concourse import mybir
    from concourse.alu_op_type import AluOpType as ALU
    from contextlib import ExitStack

    F32, BF16, F16, I32 = mybir.dt.float32, mybir.dt.bfloat16, mybir.dt.float16, mybir.dt.int32
    ACT = mybir.ActivationFunctionType
    AX = mybir.AxisListType.X
    EPS = 1e-5
    ABSENT = -1e30
    ds = bass.ds

    ctx = ExitStack()
    with ctx:
        def sb(name, shape, dt=F32):
            return ctx.enter_context(nc.sbuf_tensor(name, shape, dt))

        ident = sb("ident", [128, 128])
        ident16 = sb("ident16", [128, 128], BF16)
        node_iota = sb("node_iota", [128, N], F16)
        node_id = sb("node_id", [128, J])
        before8 = sb("before8", [P, 8, 8])
        before4 = sb("before4", [P, 4, 4])
        rev32 = sb("rev32", [P, 32])
        ones_row = sb("ones_row", [1, N])
        ones_col = sb("ones_col", [128, 1])
        rows = sb("rows", [128, ROWS])
        cols = sb("cols", [128, COLS])
        wmat = sb("wmat", [128, 2, WCOLS])
        wout = sb("wout", [128, 4, D + 2])
        wscore = sb("wscore", [128, 2, 16])
        sbias = sb("sbias", [P, 18])
        wlin = sb("wlin", [128, D])
        w2rows = sb("w2rows", [32, 2, D])
        part = sb("part", [32, 4])
        b2 = sb("b2", [32, 4, D])
        id1 = sb("id1", [P, 2, NT1])
        id2 = sb("id2", [128, 2, TOP])
        is_usual = sb("is_usual", [1, 3], I32)
        usual = sb("usual", [128, 3])
        zero16 = sb("zero16", [128, 128], BF16)
        X = sb("X", [P, J, D])
        XN = sb("XN", [P, J, D])
        XT = sb("XT", [128, 2, N])
        TT = sb("TT", [P, J, D])
        stats = sb("stats", [P, J, 6])
        mv = sb("mv", [P, J, 2])
        veps = sb("veps", [P, J])
        std = sb("std", [P, J])
        rstd = sb("rstd", [P, J])
        C1 = sb("C1", [P, J, N])
        AH = sb("AH", [P, J, N])
        C2 = sb("C2", [P, J, N])
        C2T = sb("C2T", [P, J, N])
        big = sb("big", [128, 4, J * N])
        bounds = big[0:P, 2, 400:720].rearrange("p (a b) -> p a b", a=2)
        inside = big[0:P, 2, 720:880]
        inside2 = big[0:P, 2, 2000:2160]
        bounds2 = big[:, 2, 2200:2200 + 2 * TOP].rearrange("p (a b) -> p a b", a=2)
        key = big[:, 3, 0:NT2]
        top = big[:, 3, 300:300 + TOP]
        rest2 = big[:, 3, 500:500 + 2 * NT2].rearrange("p (a b) -> p a b", a=2)
        scr2 = big[:, 3, 1100:1100 + 2 * NT2].rearrange("p (a b) -> p a b", a=2)
        hid_all = sb("hid_all", [128, 4, 632])
        onehot = hid_all[:, :, :].rearrange("p b n -> p (b n)").bitcast(BF16).rearrange(
            "p (b s n) -> p b s n", b=4, s=2)
        HA = C2[:, :, :].rearrange("p j n -> p (j n)")[:, 0:J * 512].rearrange("p (j n) -> p j n", j=J)
        HB_ = C2T[:, :, :].rearrange("p j n -> p (j n)")[:, 0:J * 512].rearrange("p (j n) -> p j n", j=J)
        TAB = sb("TAB", [P, J, 14])
        tabf = sb("tabf", [P, 2, J, 10])
        tabr = sb("tabr", [P, 2, J, 10])
        tab16 = sb("tab16", [P, 2, J, 10, 3], BF16)
        idxrow = big[0:P, 1, 0:2000].bitcast(I32).rearrange("p (b c) -> p b c", b=2)
        idxrow16 = big[0:P, 1, 2000:3000].bitcast(F16).rearrange("p (b c) -> p b c", b=2)
        onehotT = big[0:P, 2:4, :].rearrange("p a c -> p (a c)")[:, 0:5000].bitcast(BF16).rearrange(
            "p (b s j c) -> p b s j c", b=2, s=2, j=J)
        in_AH = AH[:, :, :].rearrange("p j n -> p (j n)")
        in_C2T = C2T[:, :, :].rearrange("p j n -> p (j n)")
        gT = big[0:30, 2:4, :].rearrange("p a c -> p (a c)")[:, 5000:6000].rearrange("p (b c) -> p b c", b=2)
        GS = in_AH[:, 0:10 * NT1].rearrange("p (t c) -> p t c", c=10)
        h1 = in_AH[:, 1600:2240].rearrange("p (t c) -> p t c", c=4)
        h2 = in_AH[:, 2240:2880].rearrange("p (t c) -> p t c", c=4)
        FR = h1
        hs16 = in_C2T[:, 0:16 * NT1].bitcast(BF16).rearrange("p (t c) -> p t c", c=32)
        EX = in_C2T[:, 2560:2560 + NT1]
        in_TT = TT[:, :, :].rearrange("p j n -> p (j n)")
        foldS, foldT = in_TT[:, 0:520], in_TT[:, 520:1040]
        idx1 = big[0:P, 2, 0:2 * NT1].bitcast(I32).rearrange("p (a b) -> p a b", a=2)
        idx2 = big[:, 2, 1000:1000 + 2 * NT2].bitcast(I32).rearrange("p (a b) -> p a b", a=2)
        w2v = big[0:32, 0, 0:514].rearrange("p (a b) -> p a b", a=2)
        w2r = big[0:32, 0, 514:1028].rearrange("p (a b) -> p a b", a=2)
        w2h = big[0:32, 0, 1028:1285].bitcast(BF16).rearrange("p (a b) -> p a b", a=2)
        w2m = big[0:32, 0, 1285:1542].bitcast(BF16).rearrange("p (a b) -> p a b", a=2)
        w2s = sb("w2s", [32, 2, 257], BF16)
        hT = sb("hT", [32, 2, 500], BF16)
        EF = big[:, 2:4, :].rearrange("p a c -> p (a c)")[:, 0:2000].rearrange("p (b h c) -> p b h c", b=2, h=2)
        FT = big[:, 1, 1100:1600]
        msg = big[0:P, 0, 0:8 * 257].rearrange("p (b c) -> p b c", b=8)
        msgr = big[0:P, 2, 0:8 * 257].rearrange("p (b c) -> p b c", b=8)
        msg16 = big[0:P, 1, 0:3096].bitcast(BF16).rearrange("p (b s c) -> p b s c", b=8, s=3)[:, :, :, 0:257]
        wtile = sb("wtile", [128, 4, 512])
        hid, hidg = hid_all[:, 0:2, 0:N], hid_all[:, 2:4, 0:N]
        gate = sb("gate", [P, J, 32])
        gateT = sb("gateT", [32, N])
        grow16 = big[:, 0:2, :].rearrange("p a c -> p (a c)")[:, 0:5000].bitcast(BF16).rearrange(
            "p (e n) -> p e n", e=16)
        grow = big[:, 0:2, :].rearrange("p a c -> p (a c)")[:, 0:5000].rearrange("p (e n) -> p e n", e=8)
        gateT16 = big[0:32, 2, 0:313].bitcast(BF16)[:, 0:N]
        pair16 = big[0:32, 2, 320:1344].bitcast(BF16).rearrange("p (e c) -> p e c", e=16)
        s32a = sb("s32a", [P, J, 32])
        s32b = sb("s32b", [P, J, 32])
        s5a = sb("s5a", [P, J])
        s5b = sb("s5b", [P, J])
        s40a = sb("s40a", [P, 40])
        s40b = sb("s40b", [P, 40])
        s320a = in_TT[:, 0:320].rearrange("p (j c) -> p j c", j=J)
        s320b = in_TT[:, 320:640].rearrange("p (j c) -> p j c", j=J)
        mx = sb("mx", [P, J, 4])
        bmax = sb("bmax", [P, J, 4])
        asrc = sb("asrc", [P, J, 8])
        adst = sb("adst", [P, J, 8])
        esrc = sb("esrc", [P, J, 8])
        nb02 = sb("nb02", [P, J, 8])
        pa02 = sb("pa02", [P, J, 4])
        hx = sb("hx", [P, J, 4, 5])
        dinv = sb("dinv", [P, J])
        wrow = big[0:P, 3, 0:N]

        PS = ctx.enter_context(nc.psum_tensor("PS", [128, 8, 512], F32))

        def wide(b, p=128):
            return PS[0:p, b:b + 2, :].rearrange("p b c -> p (b c)")[:, 0:640].rearrange(
                "p (j c) -> p j c", c=128)[:, :, 0:125]

        def yv(j):
            return PS[0:P, 4 + j // 2, (j % 2) * 256:(j % 2) * 256 + 256]

        def blocks(ap):
            return ap.rearrange("p (b c) -> p b c", c=125)

        def row(name, p=P):
            o, s = ROW_AT[name]
            return rows[0:p, o:o + s]

        def wm(name, h):
            o, s = W_AT[name]
            return wmat[:, h, o:o + s]

        def mid_b(ap, n):
            return ap.unsqueeze(1).to_broadcast([ap.shape[0], n, ap.shape[1]])

        def last_b(ap, n):
            return ap.unsqueeze(2).to_broadcast([ap.shape[0], ap.shape[1], n])

        names = """consts usual_ready usual_psum usual_known rest_onehot rest_used x_in idx_in l0_in rest_in out_done
            vector_step pool_step
            var_ready std_ready ln_rows xt_psum xt_sb
            table_ready tables_split onehot_ready onehot_used counts_out
            fold_var fold_std
            a1_row edge_max_ready rows_cast ids_onehot gathered gT_sb gT_psum gather_read
            logit_in edge_exp h1_ready
            hT_psum hT_sb fe_psum ef_act ef_dve fn1_psum fn1_copied fn1_turned fn1_read h2_ready
            hT2_psum hT2_sb fn2_psum msg_ready msg_hi msg_rest msg_mid msg_lo msg_used edges_done
            deg_ready deg_std b_ready bt_psum bt_act bt_dve
            t_ready t_act t_dve agg_psum h_act h_dve last_psum
            gat_h gat_a row_psum row_read rows2_psum gat_sum gat_sub gat_exp gat_mul gat_mm
            gat_var gat_std sm_in sm_out gates_ready gr_psum gr_act gr_dve gt_psum gt_sb
            h_psum h_sb h_gated y_used y_ready logits_ready
            hh_psum hh_read s_psum s_ready head_row esrc_ready relu_act relu_dve head_exp head_mul head_psum head_out head_read
            hln_var hln_std elu_in elu_exp x2_ready x2_psum x2_act x2_dve
            ho_psum so_ready o_row o_exp o_mul o_psum oelu_in oelu_exp
            w_col w_row_psum w_row_sb w_bcast x_final tri_ready""".split()
        S = {n: ctx.enter_context(nc.semaphore(n)) for n in names}
        idx_row_in = [ctx.enter_context(nc.semaphore(f"idx_row_in{u}")) for u in range(2)]
        w_in = [ctx.enter_context(nc.semaphore(f"w_in{u}")) for u in range(4)]

        def chunk_loops(eng, body, usual_order):
            if not usual_order:
                body(0, lambda u: range(J))
                body(1, lambda u: range(J))
                with eng.Fori(2, 20) as i:
                    body(i, lambda u: range(J))
                return
            for m in range(J):
                def at(i):
                    return lambda u: usual_node_tiles(4 * (2 * i + u) if u == 0 else 4 * (2 * i + u) + 3)
                if m == 0:
                    for i in range(3):
                        body(i, at(i))
                else:
                    body(4 * m, at(4 * m))
                    with eng.Fori(4 * m + 1, 4 * m + 3) as i:
                        body(i, lambda u: [m])
                body(4 * m + 3, at(4 * m + 3))

        block = ctx.enter_context(nc.Block())
        NCONST = 18

        @block.sync
        def _(sp):
            sp.dma_start(X[:], a["x"].rearrange("(j p) d -> p j d", p=P)).then_inc(S["x_in"], 16)
            sp.dma_start(idx2, a["idx2"]).then_inc(S["idx_in"], 16)
            sp.dma_start(idx1, a["idx1"]).then_inc(S["idx_in"], 16)
            sp.dma_start(bounds, a["bounds"].rearrange("a b -> (a b)").unsqueeze(0).to_broadcast([P, 2 * NT1])
                         .rearrange("p (a b) -> p a b", a=2)).then_inc(S["idx_in"], 16)
            sp.dma_start(bounds2, a["bounds2"].rearrange("a b -> (a b)").unsqueeze(0).to_broadcast([128, 2 * TOP])
                         .rearrange("p (a b) -> p a b", a=2)).then_inc(S["idx_in"], 16)
            sp.dma_start(wmat[:], a["wmat"]).then_inc(S["l0_in"], 16)
            sp.dma_start(w2rows[:], a["w2rows"]).then_inc(S["l0_in"], 16)
            sp.dma_start(part[:], a["part"]).then_inc(S["l0_in"], 16)
            sp.dma_start(rows[:], a["rows"].to_broadcast([128, ROWS])).then_inc(S["l0_in"], 16)
            sp.dma_start(cols[:], a["cols"]).then_inc(S["rest_in"], 16)
            sp.dma_start(wout[:, :, 0:D], a["wout"].rearrange("(k p) n -> p k n", p=128)).then_inc(S["rest_in"], 16)
            sp.dma_start(wlin[:], a["wlin"]).then_inc(S["rest_in"], 16)
            sp.dma_start(b2[:], a["b2"]).then_inc(S["rest_in"], 16)
            for u in range(4):
                sp.dma_start(wtile[:, u, :], a["wffn"][u]).then_inc(w_in[u], 16)

            def id_rows(i, first):
                for u in range(2):
                    if not first:
                        sp.wait_ge(S["rows_cast"], 2 * i + u - 1)
                    sp.dma_start(idxrow[:, u, :], a["idxrow"][ds(2 * i + u, 1), :].to_broadcast([P, 1000])
                                 ).then_inc(idx_row_in[u], 16)
            sp.wait_ge(S["edge_max_ready"], 1)
            id_rows(0, True)
            with sp.Fori(1, 20) as i:
                id_rows(i, False)

            with sp.Fori(1, sum(FFN_TILES) // 4) as i:
                for u in range(4):
                    sp.wait_ge(S["y_used"], 4 * i + u - 3)
                    sp.dma_start(wtile[:, u, :], a["wffn"][ds(4 * i + u, 1), :, :].rearrange("a p c -> p (a c)")
                                 ).then_inc(w_in[u], 16)

            sp.wait_ge(S["x_final"], 1)
            sp.dma_start(out.rearrange("(j p) d -> p j d", p=P), X[:]).then_inc(S["out_done"], 16)
            sp.wait_ge(S["out_done"], 16)

        @block.gpsimd
        def _(pool):
            g = nc.gpsimd
            step = [0]

            def link(ins):
                step[0] += 1
                ins.then_inc(S["pool_step"], 1)
                pool.wait_ge(S["pool_step"], step[0])

            link(g.memset(ident[:], 0.0))
            link(g.memset(before8[:], 1.0))
            link(g.memset(before4[:], 1.0))
            c = S["consts"]
            g.affine_select(out=ident[:], in_=ident[:], compare_op=ALU.not_equal, fill=1.0, base=0,
                            pattern=[[-1, 128]], channel_multiplier=1).then_inc(c, 1)
            pool.wait_ge(c, 1)
            g.tensor_copy(ident16[:], ident[:]).then_inc(c, 1)
            g.iota(node_iota[:], pattern=[[1, N]], base=0, channel_multiplier=0,
                   allow_small_or_imprecise_dtypes=True).then_inc(c, 1)
            g.iota(node_id[:], pattern=[[P, J]], base=0, channel_multiplier=1,
                   allow_small_or_imprecise_dtypes=True).then_inc(c, 1)
            g.affine_select(out=before8[:], in_=before8[:], compare_op=ALU.is_gt, fill=0.0, base=0,
                            pattern=[[1, 8], [-1, 8]], channel_multiplier=0).then_inc(c, 1)
            g.affine_select(out=before4[:], in_=before4[:], compare_op=ALU.is_gt, fill=0.0, base=0,
                            pattern=[[1, 4], [-1, 4]], channel_multiplier=0).then_inc(c, 1)
            g.iota(rev32[:], pattern=[[-1, 32]], base=32, channel_multiplier=0,
                   allow_small_or_imprecise_dtypes=True).then_inc(c, 1)
            g.memset(ones_row[:], 1.0).then_inc(c, 1)
            g.memset(hs16, 0.0).then_inc(c, 1)
            pool.wait_ge(c, 9)
            g.memset(hs16[:, :, 24:27], 1.0).then_inc(c, 1)
            g.memset(hx[:, :, :, 4:5], 1.0).then_inc(c, 1)
            g.memset(tabf[:, 0, :, 9:10], 0.0).then_inc(c, 1)
            g.memset(tabf[:, 1, :, 5:9], 0.0).then_inc(c, 1)
            g.memset(ones_col[:], 1.0).then_inc(c, 1)
            g.memset(zero16[:], 0.0).then_inc(c, 1)
            g.memset(usual[:], 1.0).then_inc(c, 1)
            g.memset(s5b[:], 0.0).then_inc(c, 1)
            g.memset(std[:], 0.0).then_inc(c, 1)

            def rest(t, b):
                pool.wait_ge(S["msg_hi"], t + 1)
                g.tensor_tensor(msgr[:, b, :], msg[:, b, :], msg16[:, b, 0, :], ALU.subtract
                                ).then_inc(S["msg_rest"], 1)

            with pool.Fori(0, NT1 // 8) as i:
                for q in range(8):
                    rest(8 * i + q, q)

            tri = big[0:P, 0, :]
            pool.wait_ge(S["y_ready"], 3)
            g.memset(tri, 1.0).then_inc(S["tri_ready"], 1)
            pool.wait_ge(S["tri_ready"], 1)
            triv = tri.rearrange("p (j n) -> p j n", j=J)
            g.affine_select(out=triv, in_=triv, compare_op=ALU.is_gt, fill=0.0, base=0,
                            pattern=[[P, J], [-1, N]], channel_multiplier=1).then_inc(S["tri_ready"], 1)
            pool.wait_ge(S["w_row_sb"], 1)
            g.partition_broadcast(wrow, gateT[0:1, :], channels=P).then_inc(S["w_bcast"], 1)

        @block.scalar
        def _(act):
            s = nc.scalar

            def layernorm(k):
                act.wait_ge(S["var_ready"], k + 1)
                s.activation(std[:], veps[:], ACT.Sqrt).then_inc(S["std_ready"], 1)
                act.wait_ge(S["xt_psum"], 2 * k + 1)
                s.copy(blocks(XT[:, 0, :]), wide(0)).then_inc(S["xt_sb"], 1)

            def evacuate_counts(C):
                s.copy(C[:, :, 0:500], PS[0:P, 0:5, 0:500])
                s.copy(C[:, 0:4, 500:625], PS[0:P, 5, 0:500].rearrange("p (m c) -> p m c", m=4))
                s.copy(C[:, 4, 500:625], PS[0:P, 6, 0:125]).then_inc(S["counts_out"], 1)

            act.wait_ge(S["consts"], NCONST)
            layernorm(0)
            act.wait_ge(S["fold_var"], 1)
            s.activation(foldS, foldS, ACT.Sqrt).then_inc(S["fold_std"], 1)
            act.wait_ge(S["onehot_used"], TOP)
            evacuate_counts(C2)
            act.wait_ge(S["onehot_used"], TOP + NT1)
            evacuate_counts(C1)

            def cast_ids(t, u, arrivals, first):
                act.wait_ge(idx_row_in[u], 16 * arrivals)
                if not first:
                    act.wait_ge(S["ids_onehot"], t - 1)
                s.copy(idxrow16[:, u, :], idxrow[:, u, :]).then_inc(S["rows_cast"], 1)

            def take_gathered(t, u, first):
                act.wait_ge(S["gathered"], t + 1)
                if not first:
                    act.wait_ge(S["gT_psum"], t - 1)
                s.copy(gT[:, u, :], PS[0:30, u, 0:500]).then_inc(S["gT_sb"], 1)

            def two_chunks(i):
                cast_ids(2 * i + 1, 1, i + 1, isinstance(i, int) and i == 0)
                if not (isinstance(i, int) and i == 0):
                    take_gathered(2 * i - 1, 1, isinstance(i, int) and i == 1)
                if not (isinstance(i, int) and i == 19):
                    cast_ids(2 * i + 2, 0, i + 2, False)
                take_gathered(2 * i, 0, isinstance(i, int) and i == 0)
            cast_ids(0, 0, 1, True)
            two_chunks(0)
            two_chunks(1)
            with act.Fori(2, 19) as i:
                two_chunks(i)
            two_chunks(19)
            take_gathered(39, 1, False)

            act.wait_ge(S["logit_in"], 1)
            s.activation(EX, EX, ACT.Exp).then_inc(S["edge_exp"], 1)

            hTp = [blocks(PS[0:32, b, 0:500]) for b in range(8)]

            def edge_hT(t, u):
                act.wait_ge(S["hT_psum"], t + 1)
                s.copy(blocks(hT[:, u, :]), hTp[u]).then_inc(S["hT_sb"], 1)

            def edge_relu(t, u):
                act.wait_ge(S["fe_psum"], t + 1)
                s.activation(EF[:, u, 0, :], PS[:, 2 + 2 * u, 0:500], ACT.Relu).then_inc(S["ef_act"], 1)

            edge_hT(0, 0)

            def fn1_copy(t, g):
                act.wait_ge(S["fn1_psum"], t + 1)
                s.copy(FT[32 * g:32 * g + 4, :], PS[0:4, 6, 0:500]).then_inc(S["fn1_copied"], 1)

            def loop_a(k, first, last):
                for g in range(4):
                    t = 4 * k + g
                    if not (last and g == 3):
                        edge_hT(t + 1, 1 - g % 2)
                    edge_relu(t, g % 2)
                    if not (first and g == 0):
                        fn1_copy(t - 1, (g + 3) % 4)
            loop_a(0, True, False)
            with act.Fori(1, 9) as k:
                loop_a(k, False, False)
            loop_a(9, False, True)
            fn1_copy(39, 3)

            def msg_high(t, b):
                act.wait_ge(S["msg_ready"], t + 1)
                s.copy(msg16[:, b, 0, :], msg[:, b, :]).then_inc(S["msg_hi"], 1)

            def loop_b(i, last):
                for q in range(8):
                    t = 8 * i + q
                    if not (last and q == 7):
                        msg_high(t + 1, (q + 1) % 8)
                    act.wait_ge(S["msg_rest"], t + 1)
                    s.copy(msg16[:, q, 1, :], msgr[:, q, :]).then_inc(S["msg_mid"], 1)
                    if q % 4 == 3 and not last:
                        act.wait_ge(S["hT2_psum"], 2 * i + q // 4 + 3)
                        s.copy(blocks(hT[:, q // 4, :]), hTp[5]).then_inc(S["hT2_sb"], 1)
            act.wait_ge(S["hT2_psum"], 1)
            s.copy(blocks(hT[:, 0, :]), hTp[5]).then_inc(S["hT2_sb"], 1)
            act.wait_ge(S["hT2_psum"], 2)
            s.copy(blocks(hT[:, 1, :]), hTp[5]).then_inc(S["hT2_sb"], 1)
            msg_high(0, 0)
            loop_b(0, False)
            with act.Fori(1, 19) as i:
                loop_b(i, False)
            loop_b(19, True)

            def gate_rows(n, done):
                tiles = 16 if n == 0 else FFN_EXPERTS[n]
                dst = grow16 if n == 0 else grow
                for e in range(0, tiles, 2):
                    act.wait_ge(S["gr_psum"], done + e + 1)
                    s.copy(blocks(dst[:, e, :]), wide(0)).then_inc(S["gr_act"], 1)

            def hidden(n, func):
                base, T = FFN_BASE[n], FFN_TILES[n]

                def body(i, first):
                    for u in range(4):
                        t = base + 4 * i + u
                        act.wait_ge(S["h_psum"], t + 1)
                        if not (first and u < 2):
                            act.wait_ge(S["h_gated"] if n < 3 else S["y_used"], t - 1)
                        s.activation(blocks(hid[:, u % 2, :]), wide(2 * (u % 2)), func,
                                     bias=cols[:, ds(COL_FFN[n] + 4 * i + u, 1)]).then_inc(S["h_sb"], 1)
                body(0, True)
                with act.Fori(1, T // 4) as i:
                    body(i, False)

            act.wait_ge(S["rest_in"], 64)
            layernorm(1)
            gate_rows(0, 0)
            hidden(0, ACT.Relu)

            act.wait_ge(S["deg_ready"], 1)
            s.activation(dinv[:], dinv[:], ACT.Sqrt).then_inc(S["deg_std"], 1)
            for i in range(0, 10, 2):
                act.wait_ge(S["bt_psum"], i + 1)
                if i < 5:
                    s.activation(blocks(AH[:, i, :]), wide(0, P), ACT.Copy, scale=dinv[:, i:i + 1]).then_inc(S["bt_act"], 1)
                else:
                    s.copy(blocks(C2T[:, i - 5, :]), wide(0, P)).then_inc(S["bt_act"], 1)
            layernorm(2)
            tps = PS[0:P, 4:7, :].rearrange("p b c -> p (b c)")
            for l in range(3):
                act.wait_ge(S["t_ready"], l + 1)
                s.copy(TT[:, 0:2, :], tps[:, 0:512].rearrange("p (j c) -> p j c", c=D)).then_inc(S["t_act"], 1)
                if l < 2:
                    act.wait_ge(S["agg_psum"], 2 * l + 1)
                    s.activation(blocks(XT[:, 0, :]), wide(0), ACT.Relu,
                                 bias=cols[:, COL_GCN + 2 * l:COL_GCN + 2 * l + 1]).then_inc(S["h_act"], 1)

            layernorm(3)

            def z(b):
                return big[0:P, b, :].rearrange("p (j n) -> p j n", j=J)

            def scores(h):
                act.wait_ge(S["rows2_psum"], 2 * h + 1)
                for j in range(J):
                    ins = s.activation(blocks(z(h)[:, j, :]), wide(0, P), ACT.Relu,
                                       bias=asrc[:, j, h:h + 1])
                ins.then_inc(S["gat_sum"], 1)

            def exps(h):
                act.wait_ge(S["gat_sub"], h + 1)
                for j in range(J):
                    ins = s.activation(z(h)[:, j, :], z(h)[:, j, :], ACT.Exp, bias=pa02[:, j, h:h + 1])
                ins.then_inc(S["gat_exp"], 1)
            for h in range(4):
                scores(h)
                exps(h)
            act.wait_ge(S["gat_var"], 1)
            s.activation(s5a[:], s5a[:], ACT.Sqrt).then_inc(S["gat_std"], 1)
            act.wait_ge(S["sm_in"], 1)
            s.activation(s32a[:, :, 0:4], s32a[:, :, 0:4], ACT.Exp).then_inc(S["sm_out"], 1)
            gate_rows(1, 16)
            hidden(1, ACT.Gelu)

            layernorm(4)
            act.wait_ge(S["s_ready"], 1)
            s.activation(esrc[:], asrc[:], ACT.Exp, scale=-0.2).then_inc(S["esrc_ready"], 1)

            def head_relu(h):
                act.wait_ge(S["head_row"], h + 1)
                if h >= 4:
                    act.wait_ge(S["head_psum"], h - 3)
                for j in range(J):
                    ins = s.activation(blocks(z(h % 4)[:, j, :]), wide(2 * (h % 2), P), ACT.Relu,
                                       bias=adst[:, j, h:h + 1])
                ins.then_inc(S["relu_act"], 1)

            def head_exp(h):
                act.wait_ge(S["relu_dve" if h % 2 else "relu_act"], h // 2 + 1)
                for j in range(J):
                    ins = s.activation(z(h % 4)[:, j, :], z(h % 4)[:, j, :], ACT.Exp, scale=-0.8,
                                       bias=nb02[:, j, h:h + 1])
                ins.then_inc(S["head_exp"], 1)
            head_relu(0)
            for h in range(8):
                head_exp(h)
                if h == 0:
                    head_relu(2)
                elif h % 2 and 3 <= h < 7:
                    head_relu(h + 1)
            act.wait_ge(S["hln_var"], 1)
            s.activation(s40a[:], s40a[:], ACT.Sqrt).then_inc(S["hln_std"], 1)
            act.wait_ge(S["elu_in"], 1)
            s.activation(HA, HB_, ACT.Exp).then_inc(S["elu_exp"], 1)
            x2t = big[:, 3, 0:2500].rearrange("p (k n) -> p k n", k=4)
            for k in range(0, 4, 2):
                act.wait_ge(S["x2_psum"], k + 1)
                s.copy(blocks(x2t[:, k, :]), wide(0)).then_inc(S["x2_act"], 1)
            act.wait_ge(S["so_ready"], 1)
            s.activation(esrc[:, :, 0], asrc[:, :, 0], ACT.Exp, scale=-0.2).then_inc(S["esrc_ready"], 1)
            act.wait_ge(S["o_row"], 1)
            for j in range(J):
                ins = s.activation(blocks(z(0)[:, j, :]), wide(0, P), ACT.Relu, bias=adst[:, j, 0:1])
            ins.then_inc(S["relu_act"], 1)
            act.wait_ge(S["relu_act"], 5)
            for j in range(J):
                ins = s.activation(z(0)[:, j, :], z(0)[:, j, :], ACT.Exp, scale=-0.8, bias=nb02[:, j, 0:1])
            ins.then_inc(S["o_exp"], 1)
            act.wait_ge(S["hln_var"], 2)
            s.activation(std[:], veps[:], ACT.Sqrt).then_inc(S["hln_std"], 1)
            act.wait_ge(S["oelu_in"], 1)
            s.activation(XN[:], TT[:], ACT.Exp).then_inc(S["oelu_exp"], 1)

            layernorm(5)
            act.wait_ge(S["sm_in"], 2)
            s.activation(s32a[:, :, 0:8], s32a[:, :, 0:8], ACT.Exp).then_inc(S["sm_out"], 1)
            gate_rows(2, 20)
            hidden(2, ACT.Relu)

            layernorm(6)
            act.wait_ge(S["t_ready"], 4)
            s.copy(TT[:, :, 0:128], PS[0:P, 4:6, :].rearrange("p b c -> p (b c)")[:, 0:640].rearrange(
                "p (j c) -> p j c", c=128)).then_inc(S["t_act"], 1)
            act.wait_ge(S["agg_psum"], 5)
            s.activation(blocks(XT[:, 0, :]), wide(0), ACT.Identity, bias=cols[:, COL_CONV:COL_CONV + 1]
                         ).then_inc(S["h_act"], 1)

            layernorm(7)
            act.wait_ge(S["w_row_psum"], 1)
            s.copy(blocks(gateT[0:1, :]), wide(0, 1)).then_inc(S["w_row_sb"], 1)
            hidden(3, ACT.Gelu_apprx_tanh)

        @block.tensor
        def _(pe):
            mm = nc.tensor.matmul
            idn = ident[0:P, 0:P]

            def layernorm(k):
                pe.wait_ge(S["ln_rows"], J * (k + 1))
                for h in range(2):
                    for j in range(J):
                        ins = nc.tensor.transpose(wide(2 * h)[:, j, :], XN[:, j, h * 128:h * 128 + 128], idn)
                    ins.then_inc(S["xt_psum"], 1)
                pe.wait_ge(S["xt_sb"], 2 * (k + 1))

            def project(name, outs, done):
                for j in range(J):
                    for h in range(2):
                        ins = mm(outs[j], XT[:, h, j * P:j * P + P], wm(name, h), start=(h == 0), stop=(h == 1))
                ins.then_inc(done, 1)

            def spread(b, col, p, done):
                for j in range(J):
                    ins = mm(wide(b, p)[:, j, :], col(j), idn, start=True, stop=True)
                ins.then_inc(done, 1)

            pe.wait_ge(S["consts"], NCONST)
            pe.wait_ge(S["l0_in"], 64)
            layernorm(0)
            project("table", [PS[0:P, 4, 16 * j:16 * j + 14] for j in range(J)], S["table_ready"])

            def clear(banks):
                for b in banks:
                    mm(PS[0:P, b, 0:500], zero16[:, 0:P], zero16[:, 0:1].to_broadcast([128, 500]), start=True,
                       stop=False, skip_group_check=True)

            def count(t, u, rows_, nodes, ready="onehot_ready", used="onehot_used"):
                pe.wait_ge(S[ready], t + 1)
                for m in nodes:
                    w = onehot[0:rows_, u, 1, m * P:m * P + P]
                    mm(PS[0:P, m, 0:500], w, onehot[0:rows_, u, 0, 0:500], start=False, stop=False,
                       skip_group_check=True)
                    b, c = (5, m * P) if m < 4 else (6, 0)
                    ins = mm(PS[0:P, b, c:c + P], w, onehot[0:rows_, u, 0, 500:625], start=False, stop=False,
                             skip_group_check=True)
                ins.then_inc(S[used], 1)

            pe.wait_ge(S["usual_ready"], 1)
            mm(PS[0:1, 7, 0:3], ones_col[:], usual[:], start=True, stop=True).then_inc(S["usual_psum"], 1)
            pe.wait_ge(S["usual_known"], 1)
            flag = pe.value_load(is_usual[:, 0:1], min_val=0, max_val=1)
            none_left = pe.value_load(is_usual[:, 1:2], min_val=0, max_val=1)
            even2 = pe.value_load(is_usual[:, 2:3], min_val=0, max_val=1)
            clear(range(7))
            with pe.If(none_left < 1):
                with pe.Fori(0, NT2 // 4) as i:
                    for u in range(4):
                        count(4 * i + u, u, 128, range(J), "rest_onehot", "rest_used")
            with pe.If(even2 > 0):
                for r in range(0, TOP, 8):
                    with pe.Fori(r // 4, r // 4 + 2) as i:
                        for u in range(4):
                            count(4 * i + u, u, 128, usual_node_tiles2(r))
            with pe.Else():
                with pe.Fori(0, TOP // 4) as i:
                    for u in range(4):
                        count(4 * i + u, u, 128, range(J))
            pe.wait_ge(S["counts_out"], 1)
            clear(range(7))
            with pe.If(flag > 0):
                for m in range(J):
                    t0 = m * TILES_PER_NODE_TILE
                    for u in range(4):
                        count(TOP + t0 + u, u, P, usual_node_tiles(t0 + u))
                    with pe.Fori(t0 // 4 + 1, t0 // 4 + TILES_PER_NODE_TILE // 4 - 1) as i:
                        for u in range(4):
                            count(4 * i + u + TOP, u, P, [m])
                    for u in range(4):
                        t = t0 + TILES_PER_NODE_TILE - 4 + u
                        count(TOP + t, u, P, usual_node_tiles(t))
            with pe.Else():
                with pe.Fori(0, NT1 // 4) as i:
                    for u in range(4):
                        count(4 * i + u + TOP, u, P, range(J))

            pe.wait_ge(S["counts_out"], 2)
            spread(0, lambda j: TAB[:, j, 4:5].to_broadcast([P, P]), P, S["a1_row"])
            pe.wait_ge(S["tables_split"], 1)

            def gather(i, nodes):
                for u in range(2):
                    t = 2 * i + u
                    pe.wait_ge(S["ids_onehot"], t + 1)
                    if not (isinstance(t, int) and t < 2):
                        pe.wait_ge(S["gT_sb"], t - 1)
                    sides = [(0, j) for j in range(J)] + [(1, j) for j in nodes(u)]
                    for n, (sd, j) in enumerate(sides):
                        ins = mm(PS[0:30, u, 0:500], tab16[:, sd, j, :, :].rearrange("p a b -> p (a b)"),
                                 onehotT[:, u, sd, j, :], start=(n == 0), stop=(n == len(sides) - 1))
                    ins.then_inc(S["gathered"], 1)
                    if not (isinstance(t, int) and t < 1):
                        turn(t - 1, 1 - u)

            def turn(t, u):
                pe.wait_ge(S["gT_sb"], t + 1)
                if not (isinstance(t, int) and t < 2):
                    pe.wait_ge(S["gather_read"], t - 1)
                mm(PS[0:P, 2 + u, 0:30], gT[:, u, 0:P], ident[0:30, 0:30], start=True, stop=True)
                for q in range(1, 4):
                    ins = nc.tensor.transpose(PS[0:P, 2 + u, 30 * q:30 * q + 30], gT[:, u, q * P:q * P + P],
                                              ident[0:30, 0:30])
                ins.then_inc(S["gT_psum"], 1)
            with pe.If(flag > 0):
                chunk_loops(pe, gather, True)
            with pe.Else():
                chunk_loops(pe, gather, False)
            turn(39, 1)

            hTp = [blocks(PS[0:32, b, 0:500]) for b in range(8)]

            def edge_transpose(t, u, first):
                if not first:
                    pe.wait_ge(S["hT_sb"], t - 1)
                for q in range(4):
                    ins = mm(hTp[u][:, q, :], hs16[:, ds(4 * t + q, 1), :].rearrange("p a c -> p (a c)"),
                             ident16[0:P, 0:P], start=True, stop=True)
                ins.then_inc(S["hT_psum"], 1)

            def edge_up(t, u, first):
                pe.wait_ge(S["hT_sb"], t + 1)
                if not first:
                    pe.wait_ge(S["ef_act"], t - 1)
                    pe.wait_ge(S["ef_dve"], t - 1)
                for h in range(2):
                    ins = mm(PS[:, 2 + 2 * u + h, 0:500], w2s[:, 0, h * 128:h * 128 + 128], hT[:, u, :],
                             start=True, stop=True)
                ins.then_inc(S["fe_psum"], 1)

            def edge_down(t, u, first):
                pe.wait_ge(S["ef_act"], t + 1)
                pe.wait_ge(S["ef_dve"], t + 1)
                if not first:
                    pe.wait_ge(S["fn1_copied"], t)
                for h in range(2):
                    ins = mm(PS[0:4, 6, 0:500], wm("fn_W1b", h), EF[:, u, h, :], start=(h == 0), stop=(h == 1))
                ins.then_inc(S["fn1_psum"], 1)

            def edge_turn(k, first):
                pe.wait_ge(S["fn1_copied"], 4 * k + 4)
                if not first:
                    pe.wait_ge(S["fn1_read"], k)
                picks = ident[:].rearrange("p (g c) -> p g c", c=32)[:, :, 0:4]
                for q in range(4):
                    ins = mm(PS[0:P, 7, 0:64].rearrange("p (g q c) -> p q g c", q=4, c=4)[:, q],
                             FT[:, q * P:q * P + P], picks, start=True, stop=True)
                ins.then_inc(S["fn1_turned"], 1)

            pe.wait_ge(S["h1_ready"], 1)
            edge_transpose(0, 0, True)

            def loop_a(k, last):
                for g in range(4):
                    t = 4 * k + g
                    first = isinstance(k, int) and t < 2
                    if not (last and g == 3):
                        edge_transpose(t + 1, 1 - g % 2, isinstance(k, int) and t == 0)
                    edge_up(t, g % 2, first)
                    if g == 1 and not (isinstance(k, int) and k == 0):
                        edge_turn(k - 1, isinstance(k, int) and k == 1)
                    if not (isinstance(k, int) and t == 0):
                        edge_down(t - 1, 1 - g % 2, isinstance(k, int) and t == 1)
            loop_a(0, False)
            loop_a(1, False)
            with pe.Fori(2, 9) as k:
                loop_a(k, False)
            loop_a(9, True)
            edge_down(39, 1, False)
            edge_turn(9, False)

            pe.wait_ge(S["h2_ready"], 1)

            def msg_transpose(g, first):
                if not first:
                    pe.wait_ge(S["hT2_sb"], g)
                for q in range(4):
                    ins = mm(hTp[5][:, q, :], hs16[:, ds(4 * g + q, 1), :].rearrange("p a c -> p (a c)"),
                             ident16[0:P, 0:P], start=True, stop=True)
                ins.then_inc(S["hT2_psum"], 1)

            def msg_up(q):
                mm(PS[0:P, 6 + q % 2, 0:257], hT[:, q // 4, (q % 4) * P:(q % 4) * P + P], w2s[:, 1, :],
                   start=True, stop=True).then_inc(S["fn2_psum"], 1)

            def msg_sum(t, q, nodes):
                pe.wait_ge(S["onehot_ready"], TOP + NT1 + 1 + t)
                pe.wait_ge(S["msg_lo"], t + 1)
                for m in nodes:
                    for c in range(3):
                        ins = mm(PS[0:P, m, 0:257], onehot[0:P, q % 4, q // 4, m * P:m * P + P], msg16[:, q, c, :],
                                 start=False, stop=False, skip_group_check=True)
                ins.then_inc(S["msg_used"], 1)

            def eight(i, nodes, last):
                for q in range(8):
                    t = 8 * i + q
                    if not (last and q >= 4):
                        if q % 4 == 0:
                            pe.wait_ge(S["hT2_sb"], 2 * i + (2 if q == 0 else 3))
                        pe.wait_ge(S["msg_ready"], t + 3)
                        msg_up((q + 4) % 8)
                    if q % 4 == 0 and not last:
                        msg_transpose(2 * i + q // 4 + 2, False)
                    msg_sum(t, q, nodes(q))

            msg_transpose(0, True)
            clear(range(J))
            msg_transpose(1, False)
            msg_up(0)
            msg_up(1)
            pe.wait_ge(S["msg_ready"], 1)
            msg_up(2)
            pe.wait_ge(S["msg_ready"], 2)
            msg_up(3)
            with pe.If(flag > 0):
                per = TILES_PER_NODE_TILE // 8
                for m in range(J):
                    eight(per * m, lambda q: usual_node_tiles(8 * per * m + q), False)
                    with pe.Fori(per * m + 1, per * m + per - 1) as i:
                        eight(i, lambda q: [m], False)
                    end = per * m + per - 1
                    eight(end, lambda q: usual_node_tiles(8 * end + q), m == J - 1)
            with pe.Else():
                with pe.Fori(0, 19) as i:
                    eight(i, lambda q: range(J), False)
                eight(19, lambda q: range(J), True)

            def gate_rows(n, done):
                pe.wait_ge(S["gates_ready"], n + 1)
                E = FFN_EXPERTS[n]
                for j in range(J):
                    ins = nc.tensor.transpose(wide(4, E)[:, j, :], gate[:, j, 0:E], idn)
                ins.then_inc(S["gt_psum"], 1)
                if n == 0:
                    pe.wait_ge(S["gt_sb"], 1)
                for e in range(16 if n == 0 else E):
                    if e >= 2:
                        pe.wait_ge(S["gr_dve" if e % 2 else "gr_act"], done // 2 + e // 2)
                    if n == 0:
                        for c0, c1 in ((0, 4), (4, 5)):
                            ins = mm(wide(2 * (e % 2))[:, c0:c1, :], pair16[:, e, :], gateT16[:, c0 * P:c1 * P],
                                     start=True, stop=True)
                        ins.then_inc(S["gr_psum"], 1)
                    else:
                        spread(2 * (e % 2), lambda j: gate[:, j, e:e + 1].to_broadcast([P, 128]), 128, S["gr_psum"])
                k = (16 if n == 0 else E) + done
                pe.wait_ge(S["gr_dve"], k // 2)
                pe.wait_ge(S["gr_act"], k // 2)
                pe.wait_ge(S["gt_sb"], n + 1)

            def ffn(n):
                base, T, E = FFN_BASE[n], FFN_TILES[n], FFN_EXPERTS[n]

                def up(i, u, first):
                    t = base + 4 * i + u
                    pe.wait_ge(w_in[u], 16 * (base // 4 + i) + 16)
                    if not first:
                        pe.wait_ge(S["h_sb"], t - 1)
                    for c0, c1 in ((0, 4), (4, 5)):
                        for h in range(2):
                            ins = mm(wide(2 * (u % 2))[:, c0:c1, :], wtile[:, u, h * 128:h * 128 + 128],
                                     XT[:, h, c0 * P:c1 * P], start=(h == 0), stop=(h == 1))
                    ins.then_inc(S["h_psum"], 1)

                src, ready = (hidg, S["h_gated"]) if n < 3 else (hid, S["h_sb"])

                def down(i, u, first):
                    t = base + 4 * i + u
                    pe.wait_ge(ready, t + 1)
                    for j in range(J):
                        ins = mm(yv(j), src[:, u % 2, j * P:j * P + P], wtile[:, u, 256:512],
                                 start=first and j % 2 == 0, stop=False, skip_group_check=True)
                    ins.then_inc(S["y_used"], 1)

                def body(i, first, last):
                    for u in range(4):
                        if u < 3:
                            up(i, u + 1, first and u == 0)
                        elif not last:
                            up(i + 1, 0, False)
                        down(i, u, first and u == 0)
                up(0, 0, True)
                body(0, True, False)
                if T > 8:
                    with pe.Fori(1, T // 4 - 1) as i:
                        body(i, False, False)
                body(T // 4 - 1, False, True)
                lhs = gateT if n < 3 else ones_row
                for j in range(J):
                    ins = mm(yv(j), lhs[0:E, j * P:j * P + P], b2[0:E, n, :], start=False, stop=True,
                             skip_group_check=True)
                ins.then_inc(S["y_ready"], 1)

            pe.wait_ge(S["rest_in"], 64)
            small = [PS[0:P, 7, 32 * j:32 * j + 32] for j in range(J)]
            layernorm(1)
            project("router", small, S["logits_ready"])
            gate_rows(0, 0)
            ffn(0)

            pe.wait_ge(S["b_ready"], 1)
            b1 = big[0:P, 2, :].rearrange("p (j n) -> p j n", j=J)
            for i in range(10):
                src = b1 if i < 5 else C2
                if i >= 2:
                    pe.wait_ge(S["bt_dve" if i % 2 else "bt_act"], i // 2)
                for j in range(J):
                    ins = nc.tensor.transpose(wide(2 * (i % 2), P)[:, j, :], src[:, j, (i % 5) * P:(i % 5) * P + P], idn)
                ins.then_inc(S["bt_psum"], 1)
            pe.wait_ge(S["bt_dve"], 5)
            pe.wait_ge(S["bt_act"], 5)
            layernorm(2)

            def aggregate(h, width, done):
                for c0, c1 in ((0, 4), (4, 5)):
                    for i in range(J):
                        ins = mm(wide(2 * h)[:, c0:c1, :], TT[:, i, h * 128:h * 128 + 128], AH[:, i, c0 * P:c1 * P],
                                 start=(i == 0), stop=(i == J - 1))
                ins.then_inc(done, 1)

            for l in range(3):
                if l > 0:
                    pe.wait_ge(S["h_act"], l)
                    pe.wait_ge(S["h_dve"], l)
                for j in range(J):
                    for h in range(2):
                        o = W_AT["gcn_W"][0] + l * D
                        ins = mm(yv(j), XT[:, h, j * P:j * P + P], wmat[:, h, o:o + D], start=(h == 0), stop=(h == 1))
                ins.then_inc(S["t_ready"], 1)
                pe.wait_ge(S["t_act"], l + 1)
                pe.wait_ge(S["t_dve"], l + 1)
                if l < 2:
                    for h in range(2):
                        aggregate(h, 256, S["agg_psum"])
                else:
                    for j in range(J):
                        for i in range(J):
                            ins = mm(yv(j), AH[:, i, j * P:j * P + P], TT[:, i, :], start=(i == 0), stop=(i == J - 1))
                    ins.then_inc(S["last_psum"], 1)

            def z(b):
                return big[0:P, b, :].rearrange("p (j n) -> p j n", j=J)

            layernorm(3)
            project("W_gat", [v[:, 0:16] for v in small], S["gat_h"])
            pe.wait_ge(S["gat_a"], 1)
            for h in range(4):
                if h >= 2:
                    pe.wait_ge(S["row_read"], h - 1)
                spread(2 * (h % 2), lambda j: asrc[:, j, h:h + 1].to_broadcast([P, P]), P, S["row_psum"])
            pe.wait_ge(S["gat_a"], 2)

            def two_rows(h):
                if h:
                    pe.wait_ge(S["gat_sum"], h)
                spread(0, lambda j: adst[:, j, h:h + 1].to_broadcast([P, P]), P, S["rows2_psum"])
                if h:
                    pe.wait_ge(S["gat_sub"], h)
                spread(2, lambda j: bmax[:, j, h:h + 1].to_broadcast([P, P]), P, S["rows2_psum"])
            two_rows(0)
            two_rows(1)
            for h in range(4):
                pe.wait_ge(S["gat_mul"], h + 1)
                for i in range(J):
                    for j in range(J):
                        ins = mm(PS[0:P, 7, (i * 4 + h) * 5:(i * 4 + h) * 5 + 5], z(h)[:, j, i * P:i * P + P],
                                 hx[:, j, h, :], start=(j == 0), stop=(j == J - 1))
                ins.then_inc(S["gat_mm"], 1)
                if h < 2:
                    two_rows(h + 2)
            gate_rows(1, 16)
            ffn(1)

            layernorm(4)
            for j in range(J):
                for h in range(2):
                    ins = mm(PS[0:P, 2, 16 * j:16 * j + 16], XT[:, h, j * P:j * P + P], wscore[:, h, :],
                             start=(h == 0), stop=(h == 1))
            ins.then_inc(S["s_psum"], 1)

            def project_heads(j):
                for h in range(2):
                    ins = mm(PS[0:P, 3 + j, :], XT[:, h, j * P:j * P + P], wm("W_heads", h), start=(h == 0), stop=(h == 1))
                ins.then_inc(S["hh_psum"], 1)

            def head_row(h):
                if h >= 2:
                    pe.wait_ge(S["relu_dve" if h % 2 else "relu_act"], h // 2)
                spread(2 * (h % 2), lambda j: asrc[:, j, h:h + 1].to_broadcast([P, P]), P, S["head_row"])
            project_heads(0)
            pe.wait_ge(S["s_ready"], 1)
            head_row(0)
            for j in range(1, J):
                project_heads(j)
            pe.wait_ge(S["hh_read"], 1)
            head_row(1)
            head_row(2)
            for h in range(8):
                pe.wait_ge(S["head_mul"], h + 1)
                if h >= 2:
                    pe.wait_ge(S["head_out"], h - 1)
                for i in range(J):
                    for j in range(J):
                        ins = mm(PS[0:P, 4 + h % 2, i * 64:i * 64 + 64], z(h % 4)[:, j, i * P:i * P + P],
                                 HA[:, j, h * 64:h * 64 + 64], start=(j == 0), stop=(j == J - 1))
                ins.then_inc(S["head_psum"], 1)
                if h < 5:
                    head_row(h + 3)
            pe.wait_ge(S["x2_ready"], 1)
            x2t = big[:, 3, 0:2500].rearrange("p (k n) -> p k n", k=4)
            for k in range(4):
                if k >= 2:
                    pe.wait_ge(S["x2_dve" if k % 2 else "x2_act"], k // 2)
                for j in range(J):
                    ins = nc.tensor.transpose(wide(2 * (k % 2))[:, j, :], HB_[:, j, k * 128:k * 128 + 128], idn)
                ins.then_inc(S["x2_psum"], 1)
            pe.wait_ge(S["x2_act"], 2)
            pe.wait_ge(S["x2_dve"], 2)
            for j in range(J):
                for k in range(4):
                    ins = mm(PS[0:P, 3 + j, 0:D + 2], x2t[:, k, j * P:j * P + P], wout[:, k, :], start=(k == 0),
                             stop=(k == 3))
            ins.then_inc(S["ho_psum"], 1)
            pe.wait_ge(S["so_ready"], 1)
            spread(0, lambda j: asrc[:, j, 0:1].to_broadcast([P, P]), P, S["o_row"])
            pe.wait_ge(S["o_mul"], 1)
            for i in range(J):
                for j in range(J):
                    ins = mm(yv(i), z(0)[:, j, i * P:i * P + P], TT[:, j, :], start=(j == 0), stop=(j == J - 1))
            ins.then_inc(S["o_psum"], 1)

            layernorm(5)
            project("Wg", [v[:, 0:8] for v in small], S["logits_ready"])
            gate_rows(2, 20)
            ffn(2)

            layernorm(6)
            tps = PS[0:P, 4:6, :].rearrange("p b c -> p (b c)")
            project("W_conv", [tps[:, 128 * j:128 * j + 128] for j in range(J)], S["t_ready"])
            pe.wait_ge(S["t_act"], 4)
            aggregate(0, 128, S["agg_psum"])
            pe.wait_ge(S["h_act"], 3)
            for j in range(J):
                ins = mm(yv(j), XT[:, 0, j * P:j * P + P], wlin[:], start=True, stop=True)
            ins.then_inc(S["last_psum"], 1)

            layernorm(7)
            project("wr", [PS[0:P, 7, j:j + 1] for j in range(J)], S["logits_ready"])
            pe.wait_ge(S["w_col"], 1)
            for j in range(J):
                ins = nc.tensor.transpose(wide(0, 1)[:, j, :], s5a[:, j:j + 1], idn)
            ins.then_inc(S["w_row_psum"], 1)
            pe.wait_ge(S["w_row_sb"], 1)
            ffn(3)

        @block.vector
        def _(dve):
            v = nc.vector
            step = [0]

            def link(ins):
                step[0] += 1
                ins.then_inc(S["vector_step"], 1)
                dve.wait_ge(S["vector_step"], step[0])

            def split(parts, x, rest):
                link(v.tensor_copy(parts[0], x))
                link(v.tensor_tensor(rest, x, parts[0], ALU.subtract))
                link(v.tensor_copy(parts[1], rest))
                link(v.tensor_tensor(parts[2], rest, parts[1], ALU.subtract))

            def moments(src):
                for j in range(J):
                    ins = v.bn_stats(stats[:, j, :], src(j))
                link(ins)
                for j in range(J):
                    ins = v.bn_aggr(mv[:, j, :], stats[:, j, :])
                link(ins)

            def layernorm(k):
                moments(lambda j: X[:, j, :])
                v.tensor_scalar_add(veps[:], mv[:, :, 1], EPS).then_inc(S["var_ready"], 1)
                dve.wait_ge(S["std_ready"], k + 1)
                link(v.reciprocal(rstd[:], std[:]))
                for j in range(J):
                    ins = v.tensor_scalar(XN[:, j, :], X[:, j, :], mv[:, j, 0:1], rstd[:, j:j + 1], ALU.subtract,
                                          ALU.mult)
                    ins.then_inc(S["ln_rows"], 1)
                dve.wait_ge(S["xt_psum"], 2 * k + 2)
                v.tensor_copy(blocks(XT[:, 1, :]), wide(2)).then_inc(S["xt_sb"], 1)

            dve.wait_ge(S["consts"], NCONST)
            dve.wait_ge(S["x_in"], 16)
            layernorm(0)

            dve.wait_ge(S["l0_in"], 64)
            v.tensor_scalar_add(foldS, row("v"), EPS).then_inc(S["fold_var"], 1)
            dve.wait_ge(S["fold_std"], 1)
            link(v.reciprocal(foldS, foldS))
            link(v.tensor_tensor(foldS, foldS, row("g"), ALU.mult))
            link(v.tensor_tensor(foldT, row("b"), row("m"), ALU.subtract))
            link(v.tensor_tensor(foldT, foldT, foldS, ALU.mult))
            link(v.tensor_tensor(foldT, foldT, row("be"), ALU.add))
            for n, o in ((0, 4), (1, 264)):
                link(v.tensor_tensor(w2v[:, n, 0:D], w2rows[:, n, :], foldS[0:32, o:o + D], ALU.mult))
                link(v.scalar_tensor_tensor(out=w2v[:, n, 0:D], in0=foldT[0:32, o:o + D], scalar=part[:, 3:4],
                                            in1=w2v[:, n, 0:D], op0=ALU.mult, op1=ALU.add))
                link(v.tensor_copy(w2v[:, n, D:D + 1], part[:, 3:4]))
            link(v.tensor_copy(w2h, w2v))
            link(v.tensor_tensor(w2r, w2v, w2h, ALU.subtract))
            link(v.tensor_copy(w2m, w2r))
            link(v.tensor_tensor(w2r, w2r, w2m, ALU.subtract))
            link(v.tensor_scalar(w2r, w2r, part[:, 2:3], None, ALU.mult))
            link(v.scalar_tensor_tensor(out=w2r, in0=w2m, scalar=part[:, 1:2], in1=w2r, op0=ALU.mult,
                                        op1=ALU.add))
            link(v.scalar_tensor_tensor(out=w2s[:], in0=w2h, scalar=part[:, 0:1], in1=w2r, op0=ALU.mult,
                                        op1=ALU.add))
            dve.wait_ge(S["table_ready"], 1)
            link(v.tensor_copy(TAB[:], PS[0:P, 4, 0:80].rearrange("p (j c) -> p j c", c=16)[:, :, 0:14]))

            dve.wait_ge(S["idx_in"], 64)
            link(v.tensor_copy(id1[:], idx1))
            link(v.tensor_tensor(inside, id1[:, 1, :], bounds[:, 0, :], ALU.is_ge))
            link(v.tensor_tensor(inside2, id1[:, 1, :], bounds[:, 1, :], ALU.is_lt))
            link(v.tensor_tensor(inside, inside, inside2, ALU.mult))
            link(v.tensor_reduce(usual[0:P, 0:1], inside, AX, ALU.min))
            link(v.tensor_copy(rest2, idx2))
            link(v.tensor_scalar(rest2[:, 0, :], rest2[:, 0, :], float(N - 1), 1.0, ALU.min, ALU.add))
            link(v.scalar_tensor_tensor(out=key, in0=rest2[:, 1, :], scalar=float(N), in1=rest2[:, 0, :],
                                        op0=ALU.mult, op1=ALU.add))
            link(v.tensor_scalar(rest2[:, 1, :], rest2[:, 1, :], N - 0.5, None, ALU.is_lt))
            link(v.tensor_tensor(key, key, rest2[:, 1, :], ALU.mult))
            link(v.tensor_scalar(key, key, -1.0, None, ALU.add))
            for r in range(ROUNDS):
                link(v.max(out=top[:, 8 * r:8 * r + 8], in_=key))
                link(v.match_replace(out=key, in_to_replace=top[:, 8 * r:8 * r + 8], in_values=key, imm_value=-1.0))

            def decode(ids, keys):
                ROUND = 1.5 * 2.0 ** 23
                link(v.tensor_scalar(ids[:, 1, :], keys, 1.0 / N, -0.5 + 0.5 / N, ALU.mult, ALU.add))
                link(v.tensor_scalar(ids[:, 1, :], ids[:, 1, :], ROUND, None, ALU.add))
                link(v.tensor_scalar(ids[:, 1, :], ids[:, 1, :], -ROUND, None, ALU.add))
                link(v.scalar_tensor_tensor(out=ids[:, 0, :], in0=ids[:, 1, :], scalar=-float(N), in1=keys,
                                            op0=ALU.mult, op1=ALU.add))
            decode(id2, top)
            decode(rest2, key)
            link(v.tensor_reduce(usual[:, 1:2], key, AX, ALU.max))
            link(v.tensor_scalar(usual[:, 1:2], usual[:, 1:2], 0.0, None, ALU.is_lt))
            s_ge, s_lt = scr2[:, 0, 0:TOP], scr2[:, 1, 0:TOP]
            link(v.tensor_tensor(s_ge, id2[:, 1, :], bounds2[:, 0, :], ALU.is_ge))
            link(v.tensor_scalar(s_lt, id2[:, 1, :], 0.0, None, ALU.is_lt))
            link(v.tensor_tensor(s_ge, s_ge, s_lt, ALU.max))
            link(v.tensor_tensor(s_lt, id2[:, 1, :], bounds2[:, 1, :], ALU.is_lt))
            link(v.tensor_tensor(s_ge, s_ge, s_lt, ALU.mult))
            v.tensor_reduce(usual[:, 2:3], s_ge, AX, ALU.min).then_inc(S["usual_ready"], 1)
            dve.wait_ge(S["usual_psum"], 1)
            v.tensor_scalar(is_usual[:], PS[0:1, 7, 0:3], 128 - 0.5, None, ALU.is_gt).then_inc(S["usual_known"], 1)
            dve.wait_ge(S["usual_known"], 1)
            none_left = dve.value_load(is_usual[:, 1:2], min_val=0, max_val=1)

            def onehots(ids, t, u, rows_, sides, wait, nodes=range(J)):
                if wait is not None:
                    dve.wait_ge(S["onehot_used"], wait)
                for sd in sides:
                    n0, n1 = (nodes[0] * P, nodes[-1] * P + P) if sd else (0, N)
                    ins = v.tensor_scalar(onehot[0:rows_, u, sd, n0:n1], node_iota[0:rows_, n0:n1],
                                          ids[0:rows_, sd, ds(t, 1)], None, ALU.is_equal)
                ins.then_inc(S["onehot_ready"], 1)
            with dve.If(none_left < 1):
                def rest_onehots(i, first):
                    for u in range(4):
                        if not first:
                            dve.wait_ge(S["rest_used"], 4 * i + u - 3)
                        for sd in range(2):
                            ins = v.tensor_scalar(onehot[:, u, sd, 0:N], node_iota[:], rest2[:, sd, ds(4 * i + u, 1)],
                                                  None, ALU.is_equal)
                        ins.then_inc(S["rest_onehot"], 1)
                rest_onehots(0, True)
                with dve.Fori(1, NT2 // 4) as i:
                    rest_onehots(i, False)
                dve.wait_ge(S["rest_used"], NT2)
            for u in range(4):
                onehots(id2, u, u, 128, (0, 1), None)
            with dve.Fori(1, TOP // 4) as i:
                for u in range(4):
                    onehots(id2, 4 * i + u, u, 128, (0, 1), 4 * i + u - 3)
            in_order = dve.value_load(is_usual[:, 0:1], min_val=0, max_val=1)
            with dve.If(in_order > 0):
                for m in range(J):
                    t0 = m * TILES_PER_NODE_TILE
                    for u in range(4):
                        onehots(id1, t0 + u, u, P, (0, 1), t0 + u + TOP - 3, usual_node_tiles(t0 + u))
                    with dve.Fori(t0 // 4 + 1, t0 // 4 + TILES_PER_NODE_TILE // 4 - 1) as i:
                        for u in range(4):
                            onehots(id1, 4 * i + u, u, P, (0, 1), 4 * i + u + TOP - 3, [m])
                    for u in range(4):
                        t = t0 + TILES_PER_NODE_TILE - 4 + u
                        onehots(id1, t, u, P, (0, 1), t + TOP - 3, usual_node_tiles(t))
            with dve.Else():
                with dve.Fori(0, NT1 // 4) as i:
                    for u in range(4):
                        onehots(id1, 4 * i + u, u, P, (0, 1), 4 * i + u + TOP - 3)

            def z(b):
                return big[0:P, b, :].rearrange("p (j n) -> p j n", j=J)

            dve.wait_ge(S["counts_out"], 2)
            link(v.tensor_scalar(z(0), C1[:], 0.0, ABSENT, ALU.is_equal, ALU.mult))
            dve.wait_ge(S["a1_row"], 1)

            def masked_max(dst, mask, scratch, scores):
                for j in range(J):
                    ins = v.tensor_tensor_reduce(out=blocks(scratch[:, j, :]), in0=blocks(mask[:, j, :]), in1=scores,
                                                 scale=1.0, scalar=-3e38, op0=ALU.add, op1=ALU.max, accum_out=dst[j])
                return ins
            link(masked_max([s5a[:, j:j + 1] for j in range(J)], z(0), z(1), wide(0, P)))
            link(v.tensor_tensor(s5a[:], s5a[:], TAB[:, :, 13], ALU.add))
            link(v.scalar_tensor_tensor(out=tabf[:, 1, :, 9], in0=s5a[:], scalar=0.2, in1=s5a[:], op0=ALU.mult,
                                        op1=ALU.max))
            link(v.tensor_copy(tabf[:, 0, :, 0:9], TAB[:, :, 0:9]))
            link(v.tensor_copy(tabf[:, 1, :, 0:5], TAB[:, :, 9:14]))
            split([tab16[:, :, :, :, c] for c in range(3)], tabf[:], tabr[:])
            v.tensor_copy(s5b[:], s5a[:]).then_inc(S["tables_split"], 1)
            dve.wait_ge(S["tables_split"], 1)
            v.tensor_copy(s5b[:], s5a[:]).then_inc(S["edge_max_ready"], 1)

            def add_parts(t, u):
                dve.wait_ge(S["gT_psum"], t + 1)
                v.tensor_reduce(GS[:, ds(4 * t, 4), :], PS[0:P, 2 + u, 0:120].rearrange(
                    "p (q a b) -> p q a b", q=4, b=3), AX, ALU.add).then_inc(S["gather_read"], 1)

            def gathers(i, nodes):
                for u in range(2):
                    t = 2 * i + u
                    dve.wait_ge(S["rows_cast"], t + 1)
                    if not (isinstance(t, int) and t < 2):
                        dve.wait_ge(S["gathered"], t - 1)
                    for sd, j in [(0, j) for j in range(J)] + [(1, j) for j in nodes(u)]:
                        ins = v.tensor_scalar(onehotT[:, u, sd, j, :], idxrow16[:, u, 500 * sd:500 * sd + 500],
                                              node_id[0:P, j:j + 1], None, ALU.is_equal)
                    ins.then_inc(S["ids_onehot"], 1)
                    if not (isinstance(t, int) and t < 2):
                        add_parts(t - 2, u)
            with dve.If(in_order > 0):
                chunk_loops(dve, gathers, True)
            with dve.Else():
                chunk_loops(dve, gathers, False)
            add_parts(38, 0)
            add_parts(39, 1)
            dve.wait_ge(S["gather_read"], 40)

            link(v.memset(FT, 0.0))
            link(v.scalar_tensor_tensor(out=EX, in0=GS[:, :, 4], scalar=0.2, in1=GS[:, :, 4], op0=ALU.mult,
                                        op1=ALU.max))
            link(v.tensor_tensor(EX, EX, GS[:, :, 9], ALU.subtract))
            v.tensor_copy(s5b[:], s5a[:]).then_inc(S["logit_in"], 1)

            def stack(h, pre, o):
                link(v.tensor_tensor(h, pre, mid_b(foldS[0:P, o:o + 4], NT1), ALU.mult))
                link(v.tensor_tensor(h, h, mid_b(foldT[0:P, o:o + 4], NT1), ALU.add))
                link(v.scalar_tensor_tensor(out=h, in0=h, scalar=0.01, in1=h, op0=ALU.mult, op1=ALU.max))
                for c in range(3):
                    ins = v.tensor_copy(hs16[:, :, 4 * c:4 * c + 4], h)
                link(ins)
                link(v.tensor_tensor(h, h, hs16[:, :, 0:4], ALU.subtract))
                for c in range(3, 5):
                    ins = v.tensor_copy(hs16[:, :, 4 * c:4 * c + 4], h)
                link(ins)
                return v.tensor_tensor(hs16[:, :, 20:24], h, hs16[:, :, 12:16], ALU.subtract)
            stack(h1, GS[:, :, 0:4], 0).then_inc(S["h1_ready"], 1)

            def edge_relu(t, u):
                dve.wait_ge(S["fe_psum"], t + 1)
                v.tensor_scalar(EF[:, u, 1, :], PS[:, 3 + 2 * u, 0:500], 0.0, None, ALU.max).then_inc(S["ef_dve"], 1)

            def edge_add(k):
                dve.wait_ge(S["fn1_turned"], k + 1)
                v.tensor_tensor(FR[:, ds(16 * k, 16), :], PS[0:P, 7, 0:64].rearrange("p (t c) -> p t c", c=4),
                                GS[:, ds(16 * k, 16), 5:9], ALU.add).then_inc(S["fn1_read"], 1)

            def loop_a(k, first):
                for g in range(4):
                    edge_relu(4 * k + g, g % 2)
                    if g == 1 and not first:
                        edge_add(k - 1)
            def score_weights(n):
                src = n % 2 == 0
                tmp = big[:, 1, 0:1024].rearrange("p (k c) -> p k c", k=4)
                if n < 4:
                    a_row, w, out = row("a_src" if src else "a_dst", 128), wm("W_heads", n // 2), \
                        wscore[:, n // 2, 8 * (n % 2):8 * (n % 2) + 8]
                    link(v.tensor_tensor(big[:, 1, 0:512], w, a_row, ALU.mult))
                    link(v.tensor_reduce(out, big[:, 1, 0:512].rearrange("p (h e) -> p h e", h=8), AX, ALU.add))
                elif n < 6:
                    a_row = row("a_out_src" if src else "a_out_dst", 128)
                    link(v.tensor_tensor(tmp, wout[:, :, 0:D], mid_b(a_row, 4), ALU.mult))
                    link(v.tensor_reduce(wout[:, :, D + n % 2], tmp, AX, ALU.add))
                elif n < 8:
                    link(v.tensor_tensor(big[0:P, 1, 0:512], row("b_heads"), row("a_src" if src else "a_dst"), ALU.mult))
                    link(v.tensor_reduce(sbias[:, 8 * (n % 2):8 * (n % 2) + 8],
                                         big[0:P, 1, 0:512].rearrange("p (h e) -> p h e", h=8), AX, ALU.add))
                else:
                    link(v.tensor_tensor(big[0:P, 1, 0:D], row("b_out"), row("a_out_src" if src else "a_out_dst"),
                                         ALU.mult))
                    link(v.tensor_reduce(sbias[:, 16 + n % 2:17 + n % 2], big[0:P, 1, 0:D], AX, ALU.add))
            dve.wait_ge(S["rest_in"], 64)
            loop_a(0, True)
            for k in range(1, 6):
                score_weights(2 * k - 2)
                loop_a(k, False)
                score_weights(2 * k - 1)
            with dve.Fori(6, 10) as k:
                loop_a(k, False)
            edge_add(9)
            dve.wait_ge(S["fn1_read"], 10)
            stack(h2, FR, 260).then_inc(S["h2_ready"], 1)
            dve.wait_ge(S["edge_exp"], 1)

            LAG = 3

            def message_low(t, b):
                dve.wait_ge(S["msg_mid"], t + 1)
                v.tensor_tensor(msg16[:, b, 2, :], msgr[:, b, :], msg16[:, b, 1, :], ALU.subtract
                                ).then_inc(S["msg_lo"], 1)

            def messages(i, nodes):
                first = isinstance(i, int) and i == 0
                for q in range(8):
                    t = 8 * i + q
                    if not first:
                        dve.wait_ge(S["msg_used"], t - 7)
                    elif q == 0:
                        dve.wait_ge(S["onehot_used"], TOP + NT1)
                    n0, n1 = nodes(q)[0] * P, nodes(q)[-1] * P + P
                    v.tensor_scalar(onehot[0:P, q % 4, q // 4, n0:n1], node_iota[0:P, n0:n1], id1[0:P, 1, ds(t, 1)],
                                    None, ALU.is_equal).then_inc(S["onehot_ready"], 1)
                    dve.wait_ge(S["fn2_psum"], t + 1)
                    v.tensor_scalar(msg[:, q, :], PS[0:P, 6 + q % 2, 0:257], 0.0, EX[:, ds(t, 1)], ALU.max,
                                    ALU.mult).then_inc(S["msg_ready"], 1)
                    if not (first and q < LAG):
                        message_low(t - LAG, (q - LAG) % 8)
            with dve.If(in_order > 0):
                per = TILES_PER_NODE_TILE // 8
                for m in range(J):
                    messages(per * m, lambda q: usual_node_tiles(8 * per * m + q))
                    with dve.Fori(per * m + 1, per * m + per - 1) as i:
                        messages(i, lambda q: [m])
                    end = per * m + per - 1
                    messages(end, lambda q: usual_node_tiles(8 * end + q))
            with dve.Else():
                messages(0, lambda q: range(J))
                with dve.Fori(1, NT1 // 8) as i:
                    messages(i, lambda q: range(J))
            for q in range(8 - LAG, 8):
                message_low(NT1 - 8 + q, q)
            dve.wait_ge(S["msg_used"], NT1)
            for j in range(J):
                link(v.tensor_scalar(s5a[:, j:j + 1], PS[0:P, j, 256:257], 0.5, None, ALU.max))
            link(v.reciprocal(s5a[:], s5a[:]))
            for j in range(J):
                ins = v.scalar_tensor_tensor(out=XN[:, j, :], in0=PS[0:P, j, 0:D], scalar=s5a[:, j:j + 1],
                                             in1=XN[:, j, :], op0=ALU.mult, op1=ALU.add)
            link(ins)
            link(v.tensor_tensor(X[:], X[:], XN[:], ALU.add))

            def gate_rows(n, done):
                v.tensor_copy(s5b[:], s5a[:]).then_inc(S["gates_ready"], 1)
                E = FFN_EXPERTS[n]
                tiles = 16 if n == 0 else E
                dst = grow16 if n == 0 else grow
                dve.wait_ge(S["gt_psum"], n + 1)
                if n == 0:
                    v.tensor_copy(blocks(gateT16), wide(4, E))
                    v.tensor_copy(pair16.rearrange("p e (a b) -> p (e a) b", a=2), last_b(ident[0:32, 0:32], 64))
                v.tensor_copy(blocks(gateT[0:E, :]), wide(4, E)).then_inc(S["gt_sb"], 1)
                for e in range(1, tiles, 2):
                    dve.wait_ge(S["gr_psum"], done + e + 1)
                    v.tensor_copy(blocks(dst[:, e, :]), wide(2)).then_inc(S["gr_dve"], 1)
                dve.wait_ge(S["gr_dve"], (done + tiles) // 2)
                dve.wait_ge(S["gr_act"], (done + tiles) // 2)

            def gating(n):
                base, T = FFN_BASE[n], FFN_TILES[n]

                def body(i, first):
                    for u in range(4):
                        t = base + 4 * i + u
                        dve.wait_ge(S["h_sb"], t + 1)
                        if not (first and u < 2):
                            dve.wait_ge(S["y_used"], t - 1)
                        g = grow16[:, ds(4 * i + u, 1), :] if n == 0 else grow[:, ds(i, 1), :]
                        v.tensor_tensor(hidg[:, u % 2, :], hid[:, u % 2, :], g.rearrange("p a n -> p (a n)"), ALU.mult
                                        ).then_inc(S["h_gated"], 1)
                body(0, True)
                with dve.Fori(1, T // 4) as i:
                    body(i, False)
                dve.wait_ge(S["y_ready"], n + 1)

            def add_y():
                for j in range(J):
                    ins = v.tensor_tensor(X[:, j, :], X[:, j, :], yv(j), ALU.add)
                link(ins)

            def top_two(E, before, k):
                sc = s32a[:, :, 0:E]
                s3 = s320a[:, :, 0:E * E].rearrange("p j (e f) -> p j e f", e=E)
                s4 = s320b[:, :, 0:E * E].rearrange("p j (e f) -> p j e f", e=E)
                other = sc.unsqueeze(2).to_broadcast([P, J, E, E])
                own = sc.unsqueeze(3).to_broadcast([P, J, E, E])
                link(v.tensor_tensor(s3, other, own, ALU.is_equal))
                link(v.tensor_tensor(s3, s3, before[:].unsqueeze(1).to_broadcast([P, J, E, E]), ALU.mult))
                link(v.tensor_tensor(s4, other, own, ALU.is_gt))
                link(v.tensor_tensor(s3, s3, s4, ALU.add))
                rank = s32b[:, :, 0:E]
                link(v.tensor_reduce(rank, s3, AX, ALU.add))
                link(v.tensor_reduce(s5a[:], sc, AX, ALU.max))
                link(v.tensor_scalar(rank, rank, 1.5, None, ALU.is_lt))
                link(v.tensor_tensor(sc, sc, last_b(s5a[:], E), ALU.subtract))
                v.tensor_copy(s5b[:], s5a[:]).then_inc(S["sm_in"], 1)
                dve.wait_ge(S["sm_out"], k)
                link(v.tensor_tensor(sc, sc, rank, ALU.mult))
                link(v.tensor_reduce(s5a[:], sc, AX, ALU.add))
                link(v.reciprocal(s5a[:], s5a[:]))
                link(v.tensor_tensor(gate[:, :, 0:E], sc, last_b(s5a[:], E), ALU.mult))

            layernorm(1)
            small = PS[0:P, 7, 0:160].rearrange("p (j c) -> p j c", c=32)
            dve.wait_ge(S["logits_ready"], 1)
            link(v.tensor_tensor(s32a[:], small, mid_b(row("router_b"), J), ALU.add))
            link(v.tensor_reduce(s5a[:], s32a[:], AX, ALU.max))
            link(v.tensor_tensor(s32b[:], s32a[:], last_b(s5a[:], 32), ALU.is_equal))
            link(v.tensor_tensor(s32b[:], s32b[:], mid_b(rev32[:], J), ALU.mult))
            link(v.tensor_reduce(s5a[:], s32b[:], AX, ALU.max))
            link(v.tensor_tensor(gate[:], s32b[:], last_b(s5a[:], 32), ALU.is_equal))
            gate_rows(0, 0)
            gating(0)
            for j in range(J):
                ins = v.scalar_tensor_tensor(out=X[:, j, :], in0=yv(j), scalar=0.0, in1=X[:, j, :], op0=ALU.max,
                                             op1=ALU.add)
            link(ins)

            link(v.tensor_reduce(dinv[:], C1[:], AX, ALU.add))
            v.tensor_scalar_add(dinv[:], dinv[:], 1.0).then_inc(S["deg_ready"], 1)
            dve.wait_ge(S["deg_std"], 1)
            link(v.reciprocal(dinv[:], dinv[:]))
            for j in range(J):
                ins = v.tensor_scalar(z(2)[:, j, :], C1[:, j, :], dinv[:, j:j + 1], None, ALU.mult)
            link(ins)
            for j in range(J):
                dg = slice(j * P, j * P + P)
                v.scalar_tensor_tensor(out=z(2)[:, j, dg], in0=ident[0:P, 0:P], scalar=dinv[:, j:j + 1],
                                       in1=z(2)[:, j, dg], op0=ALU.mult, op1=ALU.add)
                ins = v.tensor_tensor(C2[:, j, dg], C2[:, j, dg], ident[0:P, 0:P], ALU.add)
            ins.then_inc(S["b_ready"], 1)
            for i in range(1, 10, 2):
                dve.wait_ge(S["bt_psum"], i + 1)
                if i < 5:
                    v.tensor_scalar(blocks(AH[:, i, :]), wide(2, P), dinv[:, i:i + 1], None, ALU.mult
                                    ).then_inc(S["bt_dve"], 1)
                else:
                    v.tensor_copy(blocks(C2T[:, i - 5, :]), wide(2, P)).then_inc(S["bt_dve"], 1)
            layernorm(2)
            tps = PS[0:P, 4:7, :].rearrange("p b c -> p (b c)")
            for l in range(3):
                dve.wait_ge(S["t_ready"], l + 1)
                v.tensor_copy(TT[:, 2:5, :], tps[:, 512:1280].rearrange("p (j c) -> p j c", c=D)
                              ).then_inc(S["t_dve"], 1)
                if l < 2:
                    dve.wait_ge(S["agg_psum"], 2 * l + 2)
                    v.tensor_scalar(blocks(XT[:, 1, :]), wide(2), cols[:, COL_GCN + 2 * l + 1:COL_GCN + 2 * l + 2],
                                    0.0, ALU.add, ALU.max).then_inc(S["h_dve"], 1)
            dve.wait_ge(S["last_psum"], 1)
            for j in range(J):
                ins = v.tensor_tensor(XN[:, j, :], yv(j), row("gcn_b2"), ALU.add)
            link(ins)
            link(v.scalar_tensor_tensor(out=X[:], in0=XN[:], scalar=0.0, in1=X[:], op0=ALU.max, op1=ALU.add))

            layernorm(3)
            dve.wait_ge(S["gat_h"], 1)
            link(v.tensor_copy(hx[:, :, :, 0:4], small[:, :, 0:16].rearrange("p j (h e) -> p j h e", h=4)))
            for name, dst in (("att_src", asrc), ("att_dst", adst)):
                link(v.tensor_tensor(s32a[:, :, 0:16], small[:, :, 0:16], mid_b(row(name), J), ALU.mult))
                link(v.tensor_reduce(dst[:, :, 0:4], s32a[:, :, 0:16].rearrange("p j (h e) -> p j h e", h=4), AX,
                                     ALU.add))
            v.tensor_copy(s5b[:], s5a[:]).then_inc(S["gat_a"], 1)
            link(v.tensor_scalar(z(2), C2[:], 0.0, ABSENT, ALU.is_equal, ALU.mult))
            for h in range(4):
                dve.wait_ge(S["row_psum"], h + 1)
                masked_max([mx[:, j, h:h + 1] for j in range(J)], z(2), z(3), wide(2 * (h % 2), P)
                           ).then_inc(S["row_read"], 1)
                dve.wait_ge(S["row_read"], h + 1)
            link(v.tensor_tensor(mx[:], mx[:], adst[:, :, 0:4], ALU.add))
            link(v.scalar_tensor_tensor(out=mx[:], in0=mx[:], scalar=0.2, in1=mx[:], op0=ALU.mult, op1=ALU.max))
            link(v.tensor_scalar(pa02[:], asrc[:, :, 0:4], 0.2, None, ALU.mult))
            v.scalar_tensor_tensor(out=bmax[:], in0=adst[:, :, 0:4], scalar=0.2, in1=mx[:], op0=ALU.mult,
                                   op1=ALU.subtract).then_inc(S["gat_a"], 1)

            def sub_max(h):
                dve.wait_ge(S["rows2_psum"], 2 * h + 2)
                dve.wait_ge(S["gat_sum"], h + 1)
                for j in range(J):
                    zj = blocks(z(h)[:, j, :])
                    ins = v.scalar_tensor_tensor(out=zj, in0=zj, scalar=0.8, in1=wide(2, P), op0=ALU.mult,
                                                 op1=ALU.add)
                ins.then_inc(S["gat_sub"], 1)

            for h in range(4):
                sub_max(h)
                dve.wait_ge(S["gat_exp"], h + 1)
                v.tensor_tensor(z(h), z(h), C2T[:], ALU.mult).then_inc(S["gat_mul"], 1)
            dve.wait_ge(S["gat_mm"], 4)
            agg = PS[0:P, 7, 0:100].rearrange("p (i c) -> p i c", c=5)
            den = s40a[:, 0:20]
            g16 = s320a[:, :, 0:16]
            g20 = g16.rearrange("p j (h e) -> p j h e", h=4)
            link(v.tensor_scalar(den, agg[:, :, 4], 1e-16, None, ALU.add))
            link(v.reciprocal(den, den))
            link(v.tensor_tensor(g20, PS[0:P, 7, 0:100].rearrange("p (j h c) -> p j h c", j=J, c=5)[:, :, :, 0:4],
                                 den.rearrange("p (j h) -> p j h", j=J).unsqueeze(3).to_broadcast([P, J, 4, 4]),
                                 ALU.mult))
            link(v.tensor_tensor(g16, g16, mid_b(row("b_gat"), J), ALU.add))
            moments(lambda j: s320a[:, j, 0:16])
            v.tensor_scalar_add(s5a[:], mv[:, :, 1], EPS).then_inc(S["gat_var"], 1)
            dve.wait_ge(S["gat_std"], 1)
            link(v.reciprocal(s5a[:], s5a[:]))
            for j in range(J):
                ins = v.tensor_scalar(s320a[:, j, 0:16], s320a[:, j, 0:16], mv[:, j, 0:1], s5a[:, j:j + 1],
                                      ALU.subtract, ALU.mult)
            link(ins)
            link(v.tensor_tensor(g16, g16, mid_b(row("ln_gamma"), J), ALU.mult))
            link(v.tensor_tensor(g16, g16, mid_b(row("ln_beta"), J), ALU.add))
            link(v.tensor_reduce(s32a[:, :, 0:4], g16.rearrange("p j (h e) -> p j e h", h=4), AX, ALU.add))
            link(v.tensor_scalar(s32a[:, :, 0:4], s32a[:, :, 0:4], 0.25, None, ALU.mult))
            top_two(4, before4, 1)
            gate_rows(1, 16)
            gating(1)
            add_y()

            layernorm(4)
            dve.wait_ge(S["s_psum"], 1)
            scores = PS[0:P, 2, 0:16 * J].rearrange("p (j c) -> p j c", c=16)
            v.tensor_tensor(asrc[:], scores[:, :, 0:8], mid_b(sbias[:, 0:8], J), ALU.add)
            link(v.tensor_tensor(adst[:], scores[:, :, 8:16], mid_b(sbias[:, 8:16], J), ALU.add))
            v.tensor_scalar(nb02[:], adst[:], -0.2, None, ALU.mult).then_inc(S["s_ready"], 1)
            for j in range(J):
                dve.wait_ge(S["hh_psum"], j + 1)
                v.tensor_tensor(HA[:, j, :], PS[0:P, 3 + j, :], row("b_heads"), ALU.add).then_inc(S["hh_read"], 1)

            dve.wait_ge(S["esrc_ready"], 1)

            def head_out(h):
                dve.wait_ge(S["head_psum"], h + 1)
                v.tensor_tensor(HB_[:, :, h * 64:h * 64 + 64], PS[0:P, 4 + h % 2, 0:320].rearrange(
                    "p (i c) -> p i c", c=64), last_b(esrc[:, :, h], 64), ALU.mult).then_inc(S["head_out"], 1)

            def head_relu(h):
                dve.wait_ge(S["head_row"], h + 1)
                if h >= 4:
                    dve.wait_ge(S["head_psum"], h - 3)
                for j in range(J):
                    ins = v.tensor_scalar(blocks(z(h % 4)[:, j, :]), wide(2, P), adst[:, j, h:h + 1], 0.0, ALU.add,
                                          ALU.max)
                ins.then_inc(S["relu_dve"], 1)
            def head_var(h):
                dve.wait_ge(S["head_out"], h + 1)
                x, sq = HB_[:, :, h * 64:h * 64 + 64], s320b
                link(v.tensor_reduce(s5a[:], x, AX, ALU.add))
                link(v.tensor_scalar(s5a[:], s5a[:], 1.0 / 64, None, ALU.mult))
                link(v.tensor_tensor(x, x, last_b(s5a[:], 64), ALU.subtract))
                link(v.tensor_tensor(sq, x, x, ALU.mult))
                link(v.tensor_reduce(s40a[:].rearrange("p (j h) -> p j h", h=8)[:, :, h], sq, AX, ALU.add))
            for h in range(8):
                dve.wait_ge(S["head_exp"], h + 1)
                v.tensor_tensor(z(h % 4), z(h % 4), C1[:], ALU.mult).then_inc(S["head_mul"], 1)
                if h == 0:
                    head_relu(1)
                else:
                    head_out(h - 1)
                    if h % 2 and h < 7:
                        head_relu(h + 2)
                    head_var(h - 1)
            head_out(7)
            head_var(7)
            hp = HB_.rearrange("p j (h e) -> p (j h) e", h=8)
            v.tensor_scalar(s40a[:], s40a[:], 1.0 / 64, EPS, ALU.mult, ALU.add).then_inc(S["hln_var"], 1)
            dve.wait_ge(S["hln_std"], 1)
            link(v.reciprocal(s40a[:], s40a[:]))
            link(v.tensor_tensor(hp, hp, last_b(s40a[:], 64), ALU.mult))
            link(v.tensor_tensor(HB_, HB_, mid_b(row("g_heads"), J), ALU.mult))
            v.tensor_tensor(HB_, HB_, mid_b(row("beta_heads"), J), ALU.add).then_inc(S["elu_in"], 1)
            dve.wait_ge(S["elu_in"], 1)
            elu = z(2).rearrange("p j n -> p (j n)")[:, 0:J * 512].rearrange("p (j n) -> p j n", j=J)
            link(v.tensor_scalar(elu, HB_, 0.0, -1.0, ALU.max, ALU.add))
            dve.wait_ge(S["elu_exp"], 1)
            v.scalar_tensor_tensor(out=HB_, in0=HA, scalar=1.0, in1=elu, op0=ALU.min, op1=ALU.add
                                   ).then_inc(S["x2_ready"], 1)
            x2t = big[:, 3, 0:2500].rearrange("p (k n) -> p k n", k=4)
            for k in range(1, 4, 2):
                dve.wait_ge(S["x2_psum"], k + 1)
                v.tensor_copy(blocks(x2t[:, k, :]), wide(2)).then_inc(S["x2_dve"], 1)
            dve.wait_ge(S["ho_psum"], 1)
            v.tensor_scalar(asrc[:, :, 0], PS[0:P, 3:3 + J, D], sbias[:, 16:17], None, ALU.add)
            link(v.tensor_scalar(adst[:, :, 0], PS[0:P, 3:3 + J, D + 1], sbias[:, 17:18], None, ALU.add))
            v.tensor_scalar(nb02[:, :, 0], adst[:, :, 0], -0.2, None, ALU.mult).then_inc(S["so_ready"], 1)
            for j in range(J):
                v.tensor_tensor(TT[:, j, :], PS[0:P, 3 + j, 0:D], row("b_out"), ALU.add)
            dve.wait_ge(S["o_exp"], 1)
            v.tensor_tensor(z(0), z(0), C1[:], ALU.mult).then_inc(S["o_mul"], 1)
            dve.wait_ge(S["o_psum"], 1)
            dve.wait_ge(S["esrc_ready"], 2)
            for j in range(J):
                ins = v.tensor_scalar(TT[:, j, :], yv(j), esrc[:, j, 0:1], None, ALU.mult)
            link(ins)
            moments(lambda j: TT[:, j, :])
            v.tensor_scalar_add(veps[:], mv[:, :, 1], EPS).then_inc(S["hln_var"], 1)
            dve.wait_ge(S["hln_std"], 2)
            link(v.reciprocal(rstd[:], std[:]))
            for j in range(J):
                ins = v.tensor_scalar(TT[:, j, :], TT[:, j, :], mv[:, j, 0:1], rstd[:, j:j + 1], ALU.subtract, ALU.mult)
            link(ins)
            link(v.tensor_tensor(TT[:], TT[:], mid_b(row("g_out"), J), ALU.mult))
            v.tensor_tensor(TT[:], TT[:], mid_b(row("beta_out"), J), ALU.add).then_inc(S["oelu_in"], 1)
            dve.wait_ge(S["oelu_in"], 1)
            oelu = big[0:P, 2, 0:J * D].rearrange("p (j n) -> p j n", j=J)
            link(v.tensor_scalar(oelu, TT[:], 0.0, -1.0, ALU.max, ALU.add))
            dve.wait_ge(S["oelu_exp"], 1)
            link(v.scalar_tensor_tensor(out=XN[:], in0=XN[:], scalar=1.0, in1=oelu, op0=ALU.min, op1=ALU.add))
            link(v.tensor_tensor(X[:], X[:], XN[:], ALU.add))

            layernorm(5)
            dve.wait_ge(S["logits_ready"], 2)
            link(v.tensor_tensor(s32a[:, :, 0:8], small[:, :, 0:8], mid_b(row("bg"), J), ALU.add))
            link(v.tensor_tensor(s32a[:, :, 0:8], s32a[:, :, 0:8], mid_b(row("bias"), J), ALU.add))
            top_two(8, before8, 2)
            gate_rows(2, 20)
            gating(2)
            add_y()

            layernorm(6)
            dve.wait_ge(S["last_psum"], 2)
            add_y()
            link(v.tensor_tensor(X[:], X[:], mid_b(row("b_lin"), J), ALU.add))

            layernorm(7)
            dve.wait_ge(S["logits_ready"], 3)
            v.tensor_scalar(s5a[:], PS[0:P, 7, 0:5], row("br"), None, ALU.add).then_inc(S["w_col"], 1)
            dve.wait_ge(S["w_col"], 1)
            dve.wait_ge(S["w_bcast"], 1)
            dve.wait_ge(S["tri_ready"], 2)
            for j in range(J):
                link(v.tensor_scalar(z(1)[:, j, :], wrow, s5a[:, j:j + 1], None, ALU.is_gt))
                link(v.scalar_tensor_tensor(out=z(2)[:, j, :], in0=wrow, scalar=s5a[:, j:j + 1], in1=z(0)[:, j, :],
                                            op0=ALU.is_equal, op1=ALU.mult))
            link(v.tensor_tensor(z(1), z(1), z(2), ALU.add))
            link(v.tensor_reduce(s5b[:], z(1), AX, ALU.add))
            link(v.tensor_scalar(s5b[:], s5b[:], int(0.5 * N) - 1 - 0.5, None, ALU.is_lt))
            link(v.tensor_tensor(s5b[:], s5b[:], s5a[:], ALU.mult))
            link(v.tensor_tensor(X[:], X[:], XN[:], ALU.add))
            dve.wait_ge(S["y_ready"], 4)
            for j in range(J):
                ins = v.scalar_tensor_tensor(out=X[:, j, :], in0=yv(j), scalar=s5b[:, j:j + 1], in1=X[:, j, :],
                                             op0=ALU.mult, op1=ALU.add)
            ins.then_inc(S["x_final"], 1)


def kernel(**inputs):
    import concourse.bacc as _bacc
    from concourse import mybir as _mybir
    from concourse.bass_utils import run_bass_kernel_spmd as _run

    i = {k: np.asarray(v) for k, v in inputs.items()}
    w1 = np.concatenate([i["L0_ffn_W1"].transpose(1, 0, 2).reshape(D, -1), i["L1_ffn_W1"].transpose(1, 0, 2).reshape(D, -1),
                         i["L2_ffn_W1"].transpose(1, 0, 2).reshape(D, -1), i["L3_ffn_w1"]], axis=1)
    w2 = np.concatenate([i["L0_ffn_W2"].reshape(-1, D), i["L1_ffn_W2"].reshape(-1, D), i["L2_ffn_W2"].reshape(-1, D),
                         i["L3_ffn_w2"]], axis=0)
    T = sum(FFN_TILES)
    w1 = w1.reshape(2, 128, T, 128).transpose(2, 1, 0, 3).reshape(T, 128, 256)
    wffn = np.concatenate([w1, w2.reshape(T, 128, 256)], axis=2)
    fe1, fn1 = i["L0_gnn_fe_W1"], i["L0_gnn_fn_W1"]
    table = np.concatenate([fe1[:D], i["L0_gnn_attn_l"][:, None], fn1[:D], fe1[D:], i["L0_gnn_attn_r"][:, None]], axis=1)
    wmat = np.concatenate([table, fn1[D:], i["L0_ffn_router_w"].T, i["L1_ffn_W_gat"], i["L2_ffn_Wg"], i["L3_ffn_wr"],
                           i["L3_gnn_W_conv"], i["L2_gnn_W_heads"].reshape(512, D).T,
                           i["L1_gnn_W"].transpose(1, 0, 2).reshape(D, 768)], axis=1)
    wmat = wmat.reshape(2, 128, WCOLS).transpose(1, 0, 2)
    f = {}
    for k, n in (("b", "b"), ("g", "g"), ("be", "be"), ("m", "m"), ("v", "v")):
        f[k] = np.concatenate([i[f"L0_gnn_fe_{n}1"], i[f"L0_gnn_fe_{n}2"], i[f"L0_gnn_fn_{n}1"], i[f"L0_gnn_fn_{n}2"]])
    f["router_b"] = i["L0_ffn_router_b"]
    f["gcn_b2"] = i["L1_gnn_b"][2]
    for n in ("att_src", "att_dst", "b_gat", "ln_gamma", "ln_beta"):
        f[n] = i["L1_ffn_" + n].reshape(-1)
    for n in ("b_heads", "g_heads", "beta_heads", "b_out", "g_out", "beta_out"):
        f[n] = i["L2_gnn_" + n].reshape(-1)
    f["a_src"], f["a_dst"] = i["L2_gnn_a_heads"][:, :64].reshape(-1), i["L2_gnn_a_heads"][:, 64:].reshape(-1)
    f["a_out_src"], f["a_out_dst"] = i["L2_gnn_a_out"][:D], i["L2_gnn_a_out"][D:]
    f["bg"], f["bias"], f["b_lin"], f["br"] = i["L2_ffn_bg"], i["L2_ffn_bias"], i["L3_gnn_b_lin"], i["L3_ffn_br"]
    rows = np.concatenate([f[n] for n, _ in ROW_SIZES])[None]
    cols = np.concatenate([i["L0_ffn_b1"].reshape(-1), i["L1_ffn_b1"].reshape(-1), i["L2_ffn_b1"].reshape(-1),
                           i["L3_ffn_b1"], i["L1_gnn_b"][:2].reshape(-1), i["L3_gnn_b_conv"]]).reshape(COLS, 128).T
    w2rows = np.zeros((32, 2, D), np.float32)
    w2rows[:24, 0] = np.tile(i["L0_gnn_fe_W2"], (6, 1))
    w2rows[:24, 1] = np.tile(i["L0_gnn_fn_W2"], (6, 1))
    part = np.zeros((32, 4), np.float32)
    part[[0, 1, 2, 3, 12, 13, 14, 15, 20, 21, 22, 23, 24], 0] = 1
    part[[4, 5, 6, 7, 16, 17, 18, 19, 25], 1] = 1
    part[[8, 9, 10, 11, 26], 2] = 1
    part[24:27, 3] = 1
    b2 = np.zeros((32, 4, D), np.float32)
    for n, k in enumerate(("L0_ffn_b2", "L1_ffn_b2", "L2_ffn_b2", "L3_ffn_b2")):
        v = i[k].reshape(-1, D)
        b2[:v.shape[0], n] = v
    sd = np.stack([i["src"], i["dst"]])
    idx1 = sd.reshape(2, NT1, P).transpose(2, 0, 1)
    idx2 = i["L1_ffn_edge_index"].reshape(2, 128, NT2).transpose(1, 0, 2)
    idxrow = sd.reshape(2, 40, 500).transpose(1, 0, 2).reshape(40, 1000)
    bounds = np.array([[P * min(usual_node_tiles(t)) for t in range(NT1)],
                       [P * (max(usual_node_tiles(t)) + 1) for t in range(NT1)]], np.float32)
    tiles2 = [usual_node_tiles2(r) for r in range(TOP)]
    bounds2 = np.array([[P * t[0] for t in tiles2], [P * (t[-1] + 1) for t in tiles2]], np.float32)
    arrays = {"x": i["x"], "bounds2": bounds2, "bounds": bounds, "idx1": idx1, "idx2": idx2, "idxrow": idxrow, "wmat": wmat, "w2rows": w2rows, "part": part,
              "rows": rows, "cols": cols, "wout": i["L2_gnn_W_out"].T, "wlin": i["L3_gnn_W_lin"], "b2": b2, "wffn": wffn}

    nc = _bacc.Bacc("TRN2", target_bir_lowering=False, num_devices=1)
    feed, args = {}, {}
    for n, v in arrays.items():
        v = np.ascontiguousarray(v)
        feed[f"in_{n}"] = v
        args[n] = nc.dram_tensor(f"in_{n}", v.shape, _mybir.dt.from_np(v.dtype), kind="ExternalInput").ap()
    out = nc.dram_tensor("out_x", (N, D), _mybir.dt.float32, kind="ExternalOutput").ap()
    gnn_ffn_program(nc, args, out)
    r = _run(nc, [feed], core_ids=[0])
    return r.results[0]["out_x"]
```
